# Optimizing a Trainium2 kernel written in Bass

```python
import numpy as np
import jax
import jax.numpy as jnp

def _softmax(x, axis=-1):
    return jax.nn.softmax(x, axis=axis)

def _gelu(x):
    return jax.nn.gelu(x, approximate=True)

def _silu(x):
    return jax.nn.silu(x)

def _sigmoid(x):
    return jax.nn.sigmoid(x)

def _layernorm(x, axis=-1, eps=1e-05):
    m = jnp.mean(x, axis=axis, keepdims=True)
    v = jnp.var(x, axis=axis, keepdims=True)
    return (x - m) / jnp.sqrt(v + eps)

def _scatter_add(tgt, idx, src, axis=0):
    return tgt.at[idx].add(src)

def _segment_sum(src, seg, n):
    return jax.ops.segment_sum(src, seg, n)
kernel_name = 'mk_gnn_preln_d4_gnn_r8_d888a6'

def setup_inputs(seed: int=0):
    np.random.seed(seed)
    _w = jnp.asarray

    def _rec_inputs():
        import jax
        import jax.numpy as jnp
        _gk = jax.random.key(seed)
        x = -0.0006008 + 1.001 * jax.random.normal(jax.random.fold_in(_gk, 1), (6250, 256), jnp.float32)
        _s = jax.random.randint(jax.random.fold_in(_gk, 2), (50000,), 0, 6250, jnp.int32)
        _d = jax.random.randint(jax.random.fold_in(_gk, 3), (50000,), 0, 6250, jnp.int32)
        _loop = jnp.arange(6250, dtype=jnp.int32)
        src = jnp.concatenate([_s, _d, _loop])
        dst = jnp.concatenate([_d, _s, _loop])
        _o = jnp.argsort(dst, stable=True)
        src = src[_o]
        dst = dst[_o]
        edge_attr_64 = 0.000151818 + 1.00006 * jax.random.normal(jax.random.fold_in(_gk, 11), (106250, 64), jnp.float32)
        edge_weight = jax.random.uniform(jax.random.fold_in(_gk, 13), (106250,), jnp.float32, 0.0, 0.999998)
        return (x, src, dst, edge_attr_64, edge_weight)
    x, src, dst, edge_attr_64, edge_weight = _rec_inputs()

    def _L0_gnn_setup():
        import jax, jax.numpy as jnp
        import numpy as np
        import math
        HIDDEN = 256
        NUM_GAUSSIANS = 64
        NUM_FILTERS = 256
        CUTOFF = 1.0
        COSINE_OFFSET = 0.0
        N_NODES = 1250
        N_EDGES = 40000

        def ssp(x):
            return jax.nn.softplus(x) - jnp.log(2.0).astype(x.dtype)
        key = jax.random.key(seed)
        ks = jax.random.split(key, 12)

        def xavier(k, fan_out, fan_in):
            a = math.sqrt(6.0 / (fan_in + fan_out))
            return jax.random.uniform(k, (fan_out, fan_in), jnp.float32, -a, a)
        x = jax.random.normal(ks[0], (N_NODES, HIDDEN), jnp.float32)
        ji_pairs = jax.random.randint(ks[1], (2, N_EDGES), 0, N_NODES, jnp.int64)
        e_ji = jax.random.uniform(ks[2], (N_EDGES,), jnp.float32)
        e_ji_basis = jax.random.normal(ks[3], (N_EDGES, NUM_GAUSSIANS), jnp.float32)
        return {'x': x, 'ji_pairs': ji_pairs, 'e_ji': e_ji, 'e_ji_basis': e_ji_basis, 'fw1': xavier(ks[4], NUM_FILTERS, NUM_GAUSSIANS), 'fb1': jnp.zeros((NUM_FILTERS,), jnp.float32), 'fw2': xavier(ks[5], NUM_FILTERS, NUM_FILTERS), 'fb2': jnp.zeros((NUM_FILTERS,), jnp.float32), 'w1': xavier(ks[6], NUM_FILTERS, HIDDEN), 'w2': xavier(ks[7], HIDDEN, NUM_FILTERS), 'b2': jnp.zeros((HIDDEN,), jnp.float32), 'w3': xavier(ks[8], HIDDEN, HIDDEN), 'b3': jnp.zeros((HIDDEN,), jnp.float32)}
    _L0_gnn_all = _L0_gnn_setup()
    _L0_gnn_in = {k: v for k, v in _L0_gnn_all.items() if k in ('fw1', 'fb1', 'fw2', 'fb2', 'w1', 'w2', 'b2', 'w3', 'b3')}
    del _L0_gnn_all

    def _L1_gnn_setup():
        import jax, jax.numpy as jnp
        import numpy as np
        N = 6250
        E = 100000
        D_IN = 256
        HID = 32
        HEADS = 8
        D_OUT = 64
        NEG_SLOPE = 0.2

        def _gat_conv(x, src, dst, W, att_src, att_dst, bias, heads, out_dim, concat):
            n = x.shape[0]
            h = (x @ W.T).reshape(n, heads, out_dim)
            a_s = jnp.sum(h * att_src, axis=-1)
            a_d = jnp.sum(h * att_dst, axis=-1)
            logits = jax.nn.leaky_relu(a_s[src] + a_d[dst], NEG_SLOPE)
            m = jax.ops.segment_max(logits, dst, num_segments=n)
            e = jnp.exp(logits - m[dst])
            den = jax.ops.segment_sum(e, dst, num_segments=n)
            alpha = e / (den[dst] + 1e-16)
            out = jax.ops.segment_sum(alpha[:, :, None] * h[src], dst, num_segments=n)
            out = out.reshape(n, heads * out_dim) if concat else out.mean(axis=1)
            return out + bias
        key = jax.random.key(seed)
        ks = jax.random.split(key, 12)
        x = jax.random.normal(ks[0], (N, D_IN), jnp.float32)
        edge_index = jax.random.randint(ks[1], (2, E), 0, N, dtype=jnp.int32)
        g = lambda k, shape, fan_in: jax.random.normal(k, shape, jnp.float32) / np.sqrt(fan_in)
        W0 = g(ks[2], (HEADS * HID, D_IN), D_IN)
        att_src0 = g(ks[3], (1, HEADS, HID), HID)
        att_dst0 = g(ks[4], (1, HEADS, HID), HID)
        b0 = jnp.zeros((HEADS * HID,), jnp.float32)
        W1 = g(ks[5], (1 * D_OUT, HEADS * HID), HEADS * HID)
        att_src1 = g(ks[6], (1, 1, D_OUT), D_OUT)
        att_dst1 = g(ks[7], (1, 1, D_OUT), D_OUT)
        b1 = jnp.zeros((D_OUT,), jnp.float32)
        return {'x': x, 'edge_index': edge_index, 'W0': W0, 'att_src0': att_src0, 'att_dst0': att_dst0, 'b0': b0, 'W1': W1, 'att_src1': att_src1, 'att_dst1': att_dst1, 'b1': b1}
    _L1_gnn_all = _L1_gnn_setup()
    _L1_gnn_in = {k: v for k, v in _L1_gnn_all.items() if k in ('W0', 'att_src0', 'att_dst0', 'b0', 'W1', 'att_src1', 'att_dst1', 'b1')}
    del _L1_gnn_all

    def _L2_gnn_setup():
        import jax, jax.numpy as jnp
        import numpy as np
        N_NODES = 12500
        IN_FEATS = 256
        OUT_FEATS = 256
        N_EDGES = 400000
        key = jax.random.key(seed)
        k1, k2, k3, k4 = jax.random.split(key, 4)
        x = jax.random.normal(k1, (N_NODES, IN_FEATS), dtype=jnp.float32)
        edge_index = jax.random.randint(k2, (2, N_EDGES), 0, N_NODES, dtype=jnp.int64)
        scale = 1.0 / np.sqrt(IN_FEATS)
        W = jax.random.uniform(k3, (IN_FEATS, OUT_FEATS), dtype=jnp.float32, minval=-scale, maxval=scale)
        b = jax.random.uniform(k4, (OUT_FEATS,), dtype=jnp.float32, minval=-scale, maxval=scale)
        return {'x': x, 'edge_index': edge_index, 'W': W, 'b': b}
    _L2_gnn_all = _L2_gnn_setup()
    _L2_gnn_in = {k: v for k, v in _L2_gnn_all.items() if k in ('W', 'b')}
    del _L2_gnn_all

    def _L3_gnn_setup():
        import jax, jax.numpy as jnp
        import numpy as np
        N = 12500
        E = 400000
        IN_C = 256
        HID = 64
        OUT_C = 2
        EPS = 1e-05

        def gcn_conv(x, W, b, src, dst, n):
            xw = x @ W
            loops = jnp.arange(n, dtype=src.dtype)
            s = jnp.concatenate([src, loops])
            d = jnp.concatenate([dst, loops])
            deg = jax.ops.segment_sum(jnp.ones_like(d, dtype=x.dtype), d, num_segments=n)
            dinv = jax.lax.rsqrt(deg)
            norm = dinv[s] * dinv[d]
            out = jax.ops.segment_sum(norm[:, None] * xw[s], d, num_segments=n)
            return out + b

        def batch_norm(x, gamma, beta):
            mu = jnp.mean(x, axis=0)
            var = jnp.mean(jnp.square(x - mu), axis=0)
            return (x - mu) * jax.lax.rsqrt(var + EPS) * gamma + beta
        key = jax.random.key(seed)
        ks = jax.random.split(key, 8)
        x = jax.random.normal(ks[0], (N, IN_C), dtype=jnp.float32)
        edge_index = jax.random.randint(ks[1], (2, E), 0, N, dtype=jnp.int64)
        W1 = jax.random.normal(ks[2], (IN_C, HID), dtype=jnp.float32) / np.sqrt(IN_C)
        b1 = jnp.zeros((HID,), dtype=jnp.float32)
        W2 = jax.random.normal(ks[3], (HID, OUT_C), dtype=jnp.float32) / np.sqrt(HID)
        b2 = jnp.zeros((OUT_C,), dtype=jnp.float32)
        g1 = jnp.ones((HID,), dtype=jnp.float32)
        be1 = jnp.zeros((HID,), dtype=jnp.float32)
        g2 = jnp.ones((OUT_C,), dtype=jnp.float32)
        be2 = jnp.zeros((OUT_C,), dtype=jnp.float32)
        Wd = jax.random.normal(ks[4], (OUT_C, IN_C), dtype=jnp.float32) / np.sqrt(OUT_C)
        bd = jnp.zeros((IN_C,), dtype=jnp.float32)
        return {'x': x, 'edge_index': edge_index, 'W1': W1, 'b1': b1, 'g1': g1, 'be1': be1, 'W2': W2, 'b2': b2, 'g2': g2, 'be2': be2, 'Wd': Wd, 'bd': bd}
    _L3_gnn_all = _L3_gnn_setup()
    _L3_gnn_in = {k: v for k, v in _L3_gnn_all.items() if k in ('W1', 'b1', 'g1', 'be1', 'W2', 'b2', 'g2', 'be2', 'Wd', 'bd')}
    del _L3_gnn_all
    return {'x': x, 'src': src, 'dst': dst, 'edge_attr_64': edge_attr_64, 'edge_weight': edge_weight, 'L0_gnn_fw1': _L0_gnn_in['fw1'], 'L0_gnn_fb1': _L0_gnn_in['fb1'], 'L0_gnn_fw2': _L0_gnn_in['fw2'], 'L0_gnn_fb2': _L0_gnn_in['fb2'], 'L0_gnn_w1': _L0_gnn_in['w1'], 'L0_gnn_w2': _L0_gnn_in['w2'], 'L0_gnn_b2': _L0_gnn_in['b2'], 'L0_gnn_w3': _L0_gnn_in['w3'], 'L0_gnn_b3': _L0_gnn_in['b3'], 'L1_gnn_W0': _L1_gnn_in['W0'], 'L1_gnn_att_src0': _L1_gnn_in['att_src0'], 'L1_gnn_att_dst0': _L1_gnn_in['att_dst0'], 'L1_gnn_b0': _L1_gnn_in['b0'], 'L1_gnn_W1': _L1_gnn_in['W1'], 'L1_gnn_att_src1': _L1_gnn_in['att_src1'], 'L1_gnn_att_dst1': _L1_gnn_in['att_dst1'], 'L1_gnn_b1': _L1_gnn_in['b1'], 'L2_gnn_W': _L2_gnn_in['W'], 'L2_gnn_b': _L2_gnn_in['b'], 'L3_gnn_W1': _L3_gnn_in['W1'], 'L3_gnn_b1': _L3_gnn_in['b1'], 'L3_gnn_g1': _L3_gnn_in['g1'], 'L3_gnn_be1': _L3_gnn_in['be1'], 'L3_gnn_W2': _L3_gnn_in['W2'], 'L3_gnn_b2': _L3_gnn_in['b2'], 'L3_gnn_g2': _L3_gnn_in['g2'], 'L3_gnn_be2': _L3_gnn_in['be2'], 'L3_gnn_Wd': _L3_gnn_in['Wd'], 'L3_gnn_bd': _L3_gnn_in['bd']}

def reference(x, src, dst, edge_attr_64, edge_weight, L0_gnn_fw1, L0_gnn_fb1, L0_gnn_fw2, L0_gnn_fb2, L0_gnn_w1, L0_gnn_w2, L0_gnn_b2, L0_gnn_w3, L0_gnn_b3, L1_gnn_W0, L1_gnn_att_src0, L1_gnn_att_dst0, L1_gnn_b0, L1_gnn_W1, L1_gnn_att_src1, L1_gnn_att_dst1, L1_gnn_b1, L2_gnn_W, L2_gnn_b, L3_gnn_W1, L3_gnn_b1, L3_gnn_g1, L3_gnn_be1, L3_gnn_W2, L3_gnn_b2, L3_gnn_g2, L3_gnn_be2, L3_gnn_Wd, L3_gnn_bd):
    import jax
    import jax.numpy as jnp

    def _L0_gnn_ref(x, ji_pairs, e_ji, e_ji_basis, fw1, fb1, fw2, fb2, w1, w2, b2, w3, b3):
        import jax, jax.numpy as jnp
        import numpy as np
        import math
        HIDDEN = 256
        NUM_GAUSSIANS = 64
        NUM_FILTERS = 256
        CUTOFF = 1.0
        COSINE_OFFSET = 0.0
        N_NODES = 1250
        N_EDGES = 40000

        def ssp(x):
            return jax.nn.softplus(x) - jnp.log(2.0).astype(x.dtype)
        pi = jnp.asarray(math.pi, x.dtype)
        C = 0.25 * (jnp.cos((e_ji - COSINE_OFFSET) * pi / (CUTOFF - COSINE_OFFSET)) + 1.0)
        W = ssp(e_ji_basis @ fw1.T + fb1) @ fw2.T + fb2
        W = W * C[:, None]
        h = x @ w1.T
        src, dst = (ji_pairs[0], ji_pairs[1])
        msg = h[src] * W
        agg = jax.ops.segment_sum(msg, dst, num_segments=x.shape[0])
        out = agg @ w2.T + b2
        out = ssp(out) @ w3.T + b3
        return out

    def _L1_gnn_ref(x, edge_index, W0, att_src0, att_dst0, b0, W1, att_src1, att_dst1, b1):
        import jax, jax.numpy as jnp
        import numpy as np
        N = 6250
        E = 100000
        D_IN = 256
        HID = 32
        HEADS = 8
        D_OUT = 64
        NEG_SLOPE = 0.2

        def _gat_conv(x, src, dst, W, att_src, att_dst, bias, heads, out_dim, concat):
            n = x.shape[0]
            h = (x @ W.T).reshape(n, heads, out_dim)
            a_s = jnp.sum(h * att_src, axis=-1)
            a_d = jnp.sum(h * att_dst, axis=-1)
            logits = jax.nn.leaky_relu(a_s[src] + a_d[dst], NEG_SLOPE)
            m = jax.ops.segment_max(logits, dst, num_segments=n)
            e = jnp.exp(logits - m[dst])
            den = jax.ops.segment_sum(e, dst, num_segments=n)
            alpha = e / (den[dst] + 1e-16)
            out = jax.ops.segment_sum(alpha[:, :, None] * h[src], dst, num_segments=n)
            out = out.reshape(n, heads * out_dim) if concat else out.mean(axis=1)
            return out + bias
        n = x.shape[0]
        loop = jnp.arange(n, dtype=edge_index.dtype)
        ei = jnp.concatenate([edge_index, jnp.stack([loop, loop])], axis=1)
        src, dst = (ei[0], ei[1])
        out1 = jax.nn.elu(_gat_conv(x, src, dst, W0, att_src0, att_dst0, b0, HEADS, HID, True))
        _ = _gat_conv(out1, src, dst, W1, att_src1, att_dst1, b1, 1, D_OUT, False)
        return out1

    def _L2_gnn_ref(x, edge_index, W, b):
        import jax, jax.numpy as jnp
        import numpy as np
        N_NODES = 12500
        IN_FEATS = 256
        OUT_FEATS = 256
        N_EDGES = 400000
        n = x.shape[0]
        row = edge_index[0]
        col = edge_index[1]
        h = x @ W + b
        agg = jax.ops.segment_sum(h[col], row, num_segments=n)
        deg = jax.ops.segment_sum(jnp.ones((edge_index.shape[1],), dtype=h.dtype), row, num_segments=n)
        inv_deg = jnp.where(deg > 0, 1.0 / jnp.where(deg > 0, deg, 1.0), 0.0)
        return agg * inv_deg[:, None]

    def _L3_gnn_ref(x, edge_index, W1, b1, g1, be1, W2, b2, g2, be2, Wd, bd):
        import jax, jax.numpy as jnp
        import numpy as np
        N = 12500
        E = 400000
        IN_C = 256
        HID = 64
        OUT_C = 2
        EPS = 1e-05

        def gcn_conv(x, W, b, src, dst, n):
            xw = x @ W
            loops = jnp.arange(n, dtype=src.dtype)
            s = jnp.concatenate([src, loops])
            d = jnp.concatenate([dst, loops])
            deg = jax.ops.segment_sum(jnp.ones_like(d, dtype=x.dtype), d, num_segments=n)
            dinv = jax.lax.rsqrt(deg)
            norm = dinv[s] * dinv[d]
            out = jax.ops.segment_sum(norm[:, None] * xw[s], d, num_segments=n)
            return out + b

        def batch_norm(x, gamma, beta):
            mu = jnp.mean(x, axis=0)
            var = jnp.mean(jnp.square(x - mu), axis=0)
            return (x - mu) * jax.lax.rsqrt(var + EPS) * gamma + beta
        src, dst = (edge_index[0], edge_index[1])
        n = x.shape[0]
        h = gcn_conv(x, W1, b1, src, dst, n)
        h = jax.nn.relu(batch_norm(h, g1, be1))
        z = batch_norm(gcn_conv(h, W2, b2, src, dst, n), g2, be2)
        return z @ Wd + bd
    edge_index = jnp.stack([src, dst])
    h = jnp.maximum(_layernorm(x, axis=-1), 0.0)
    x = x + _L0_gnn_ref(h, edge_index, edge_weight, edge_attr_64, L0_gnn_fw1, L0_gnn_fb1, L0_gnn_fw2, L0_gnn_fb2, L0_gnn_w1, L0_gnn_w2, L0_gnn_b2, L0_gnn_w3, L0_gnn_b3)
    h = jnp.maximum(_layernorm(x, axis=-1), 0.0)
    x = x + _L1_gnn_ref(h, edge_index, L1_gnn_W0, L1_gnn_att_src0, L1_gnn_att_dst0, L1_gnn_b0, L1_gnn_W1, L1_gnn_att_src1, L1_gnn_att_dst1, L1_gnn_b1)
    h = jnp.maximum(_layernorm(x, axis=-1), 0.0)
    x = x + _L2_gnn_ref(h, edge_index, L2_gnn_W, L2_gnn_b)
    h = jnp.maximum(_layernorm(x, axis=-1), 0.0)
    x = x + _L3_gnn_ref(h, edge_index, L3_gnn_W1, L3_gnn_b1, L3_gnn_g1, L3_gnn_be1, L3_gnn_W2, L3_gnn_b2, L3_gnn_g2, L3_gnn_be2, L3_gnn_Wd, L3_gnn_bd)
    return x

_drawn_inputs = setup_inputs


def setup_inputs(seed=0):
    import zlib

    import numpy as np

    out = dict(_drawn_inputs(seed))
    spreads = {'L0_gnn_fb1': (0.0, 0.1),
     'L0_gnn_fb2': (0.0, 0.1),
     'L0_gnn_b2': (0.0, 0.1),
     'L0_gnn_b3': (0.0, 0.1),
     'L1_gnn_b0': (0.0, 0.1),
     'L1_gnn_b1': (0.0, 0.1),
     'L3_gnn_b1': (0.0, 0.1),
     'L3_gnn_g1': (1.0, 0.2),
     'L3_gnn_be1': (0.0, 0.1),
     'L3_gnn_b2': (0.0, 0.1),
     'L3_gnn_g2': (1.0, 0.2),
     'L3_gnn_be2': (0.0, 0.1),
     'L3_gnn_bd': (0.0, 0.1)}
    factors = {}
    for name, (base, spread) in spreads.items():
        noise = np.random.default_rng([zlib.crc32(name.encode()), seed]).standard_normal(out[name].shape)
        drawn = base * np.exp(spread * noise) if base else spread * noise
        out[name] = jnp.asarray(drawn.astype(out[name].dtype))
    for name, factor in factors.items():
        out[name] = (out[name] * factor).astype(out[name].dtype)
    return out
```

```python
from contextlib import ExitStack, contextmanager

import concourse.bass as bass
from concourse import mybir

F32 = mybir.dt.float32
I32 = mybir.dt.int32
U32 = mybir.dt.uint32
ALU = mybir.AluOpType
ACT = mybir.ActivationFunctionType
AX = mybir.AxisListType

P = 128
N = 6250
E = 106250
D = 256
KH = D // P
TILES = 832
GT = 4
GROUPS = TILES // GT
NB = 4
ITERS = GROUPS // NB
CT = 7
CN = CT * P
CHUNKS = 7
NT = CHUNKS * CT
NP = CHUNKS * CN
PAD_DST = 6300
NW = 6432
HEADS = 8
HID = D // HEADS
NG = 64
H3 = 64
OC = 2
BIG = 1.0e38
EPS = 1e-5
HALF_PI = 1.5707963267948966
PI = 3.141592653589793
LN2 = 0.6931471805599453
EXP_LN = "natural_log_exp_and_others"
EXP_CAP = float(2 ** 60)
SEG = GT * NB
HALVES = ((0, 512), (512, CN))
BANKS = ((0, 512), (512, 1024), (1024, 1536), (1536, 1792))

INPUTS = {
    "x": ([NP, D], F32), "src_cols": ([P, TILES], I32), "dst_cols": ([P, TILES], I32),
    "prev_cols": ([P, TILES], I32), "next_cols": ([P, TILES], I32), "ew_cols": ([P, TILES], F32),
    "edge_t": ([GROUPS // 2, P, GT * P], F32),
    "fw1_t": ([NG, D], F32), "fb1": ([P, KH], F32), "fw2_t": ([D, D], F32), "fb2": ([D], F32),
    "w1_t": ([D, D], F32), "w2_t": ([D, D], F32), "b2": ([P, KH], F32), "w3_t": ([D, D], F32), "b3": ([D], F32),
    "gat_w": ([D, D], F32), "gat_w_t": ([D, D], F32), "att_src": ([D], F32), "att_dst": ([D], F32),
    "gat_b": ([D], F32), "mean_w": ([D, D], F32), "mean_b": ([D], F32),
    "gcn_w1": ([D, H3], F32), "gcn_b1": ([H3], F32), "gcn_g1": ([H3], F32), "gcn_be1": ([H3], F32),
    "gcn_w2": ([H3, OC], F32), "gcn_b2": ([OC], F32), "gcn_g2": ([OC], F32), "gcn_be2": ([OC], F32),
    "gcn_wd": ([OC, D], F32), "gcn_bd": ([D], F32),
}
SCRATCH = {
    "tab0": [NP, D], "x1": [NP, D], "tab1": [NP, D], "tab_as": [NP, HEADS], "att_tab": [NW, 2 * HEADS],
    "x2": [NP, D], "tab2": [NP, D], "x3": [NP, D], "tab3": [NP, H3], "tab4": [NP, OC],
    "deg_row": [1, NP], "last_max": [P, ITERS], "first_max": [P, ITERS],
    "carry": [2, TILES, HEADS],
}


class Chain:

    def __init__(self, eng, sem, base=0):
        self.eng, self.sem, self.base, self.n = eng, sem, base, 0

    def link(self, instruction):
        instruction.then_inc(self.sem, 1)
        self.n += 1
        self.eng.wait_ge(self.sem, self.base + self.n)


def hold(eng, ph, sem, value):
    eng.wait_ge(sem, value)
    eng.sem_inc(ph.seen, 1)


class Phase:

    def __init__(self, nc, tag):
        self.nc, self.tag, self.stack, self.sems, self.free = nc, tag, ExitStack(), [], []
        self.seen = self.sem("seen")

    def __enter__(self):
        return self

    def __exit__(self, *_):
        self.stack.close()
        self.nc.clear_and_free_semaphores(self.sems)
        self.nc.all_engine_barrier()

    def sb(self, name, shape, dtype=F32):
        return self.stack.enter_context(self.nc.sbuf_tensor(f"{self.tag}_{name}", shape, dtype))

    def ps(self, name, cols, rows=P):
        return self.stack.enter_context(self.nc.psum_tensor(f"{self.tag}_{name}", [rows, cols], F32))

    def sem(self, name, free=0):
        s = self.nc.alloc_semaphore(f"{self.tag}_{name}")
        self.sems.append(s)
        if free:
            self.free.append((s, free))
        return s

    def begin(self):
        for s, free in self.free:
            self.nc.gpsimd.sem_inc(s, free)
        if self.free:
            self.nc.all_engine_barrier()


def by_half(ap):
    return ap.rearrange("(k p) n -> p k n", p=P)


def on_all(ap, n, rows=P):
    return ap.rearrange("(a n) -> a n", a=1).broadcast_to([rows, n])


def node_rows(ap, c):
    return ap[bass.ds(c * CN, CN), :].rearrange("(t p) n -> p t n", p=P)


class Norm:

    def __init__(self, ph, shared):
        self.ph, self.nc, self.shared = ph, ph.nc, shared
        self.X = ph.sb("X", [P, CT, D])
        self.norm = ph.sb("norm", [P, CT, D])
        self.hT = ph.sb("hT", [P, KH, CN])
        self.stats = ph.sb("stats", [P, CT, 6])
        self.mv = ph.sb("mv", [P, CT, 2])
        self.std = ph.sb("std", [P, CT])
        self.rstd = ph.sb("rstd", [P, CT])
        self.psT = ph.ps("psT", 2048)
        self.stats_done = ph.sem("stats_done")
        self.mv_done = ph.sem("mv_done")
        self.std_done = ph.sem("std_done")
        self.log_done = ph.sem("log_done")
        self.norm_done = ph.sem("norm_done", 1)
        self.xT_done = ph.sem("xT_done", 1)
        self.hT_done = ph.sem("hT_done", 1)

    def vector(self, dve, c):
        nc = self.nc
        for t in range(CT):
            last = nc.vector.bn_stats(self.stats[:, t, :], self.X[:, t, :])
        last.then_inc(self.stats_done, 1)
        hold(dve, self.ph, self.stats_done, c + 1)
        for t in range(CT):
            last = nc.vector.bn_aggr(self.mv[:, t, :], self.stats[:, t, :])
        last.then_inc(self.mv_done, 1)
        dve.wait_ge(self.std_done, c + 1)
        dve.wait_ge(self.xT_done, c + 1)
        for t in range(CT):
            last = nc.vector.tensor_scalar(self.norm[:, t, :], self.X[:, t, :], self.mv[:, t, 0:1],
                                           self.rstd[:, t:t + 1], ALU.subtract, ALU.mult)
        last.then_inc(self.norm_done, 1)

    def scalar_std(self, act, c):
        act.wait_ge(self.mv_done, c + 1)
        self.nc.scalar.activation(self.std[:, :], self.mv[:, :, 1], ACT.Ln,
                                  bias=self.shared["eps"][:, 0:1]).then_inc(self.log_done, 1)
        act.wait_ge(self.log_done, c + 1)
        self.nc.scalar.activation(self.rstd[:, :], self.std[:, :], ACT.Exp, scale=-0.5).then_inc(self.std_done, 1)

    def scalar_relu(self, act, c, used, count):
        act.wait_ge(self.xT_done, c + 2)
        act.wait_ge(used, count)
        flat = self.hT[:, :, :].rearrange("p k n -> p (k n)")
        for lo, hi in BANKS:
            last = self.nc.scalar.activation(flat[:, lo:hi], self.psT[:, lo:hi], ACT.Relu)
        last.then_inc(self.hT_done, 1)

    def tensor(self, pe, c):
        pe.wait_ge(self.norm_done, c + 2)
        pe.wait_ge(self.hT_done, c + 1)
        for k in range(KH):
            for t in range(CT):
                j = k * CT + t
                last = self.nc.tensor.transpose(self.psT[:, j * P:(j + 1) * P],
                                                self.norm[:, t, k * P:(k + 1) * P], self.shared["ident"][:, :])
        last.then_inc(self.xT_done, 1)


def project(nc, out, hT, w):
    for t in range(CT):
        for k in range(KH):
            last = nc.tensor.matmul(out[:, t * D:(t + 1) * D], hT[:, k, t * P:(t + 1) * P], w[:, k, :],
                                    start=(k == 0), stop=(k == KH - 1))
    return last


def constants(nc, dram, sh):
    with Phase(nc, "const") as ph:
        iota_i = ph.sb("iota_i", [P, P], I32)
        base_b = ph.sb("base_b", [P, TILES], I32)
        zrow = ph.sb("zrow", [P, 2 * HEADS])
        loaded, zeroed, made = ph.sem("loaded"), ph.sem("zeroed"), ph.sem("made")
        zstored, rel_done = ph.sem("zstored"), ph.sem("rel_done")
        ph.begin()
        with nc.Block() as block:

            @block.sync
            def _(sp):
                sp.dma_start(sh["src_sb"][:, :], dram["src_cols"][:, :]).then_inc(loaded, 16)
                sp.dma_start(sh["dst_sb"][:, :], dram["dst_cols"][:, :]).then_inc(loaded, 16)
                sp.dma_start(base_b[:, :], dram["dst_cols"][0:1, :].broadcast_to([P, TILES])).then_inc(loaded, 16)
                sp.wait_ge(loaded, 48)
                sp.wait_ge(rel_done, 1)
                sp.dma_start(dram["att_tab"][NP:NP + P, :], zrow[:, :]).then_inc(zstored, 16)
                sp.dma_start(dram["att_tab"][NP + P:NW, :], zrow[0:NW - NP - P, :]).then_inc(zstored, 16)
                sp.wait_ge(zstored, 32)

            @block.gpsimd
            def _(pool):
                nc.gpsimd.iota(iota_i[:, :], [[1, P]], base=0, channel_multiplier=0).then_inc(made, 1)
                nc.gpsimd.memset(sh["ident"][:, :], 0.0).then_inc(zeroed, 1)
                pool.wait_ge(zeroed, 1)
                nc.gpsimd.affine_select(out=sh["ident"][:, :], in_=sh["ident"][:, :],
                                        compare_op=ALU.not_equal, fill=1.0, base=0,
                                        pattern=[[-1, P]], channel_multiplier=1).then_inc(zeroed, 1)
                pool.wait_ge(zeroed, 2)

            @block.vector
            def _(dve):
                nc.vector.memset(zrow[:, :], 0.0).then_inc(rel_done, 1)
                nc.vector.memset(sh["ones"][:, :], 1.0)
                nc.vector.memset(sh["eps"][:, :], EPS)
                dve.wait_ge(made, 1)
                nc.vector.tensor_copy(sh["iota"][:, :], iota_i[:, :])
                dve.wait_ge(loaded, 48)
                nc.vector.tensor_tensor(sh["rel"][:, :], sh["dst_sb"][:, :], base_b[:, :],
                                        ALU.subtract).then_inc(rel_done, 1)
                dve.wait_ge(rel_done, 2)


def embed0(nc, dram, sh):
    with Phase(nc, "n0") as ph:
        nm = Norm(ph, sh)
        w = ph.sb("w", [P, KH, D])
        O = ph.sb("O", [P, CT, D])
        psO = ph.ps("psO", 2048)
        w_in, x_in, stored = (ph.sem(s) for s in ("w_in", "x_in", "stored"))
        mm_done = ph.sem("mm_done", 1)
        o_done = ph.sem("o_done", 1)
        o_free = ph.sem("o_free", 1)
        ph.begin()
        with nc.Block() as block:

            @block.sync
            def _(sp):
                sp.dma_start(w[:, :, :], by_half(dram["w1_t"])).then_inc(w_in, 16)
                with sp.Fori(0, CHUNKS) as c:
                    hold(sp, ph, nm.norm_done, c + 1)
                    sp.dma_start(nm.X[:, :, :], node_rows(dram["x"], c)).then_inc(x_in, 16)

            @block.gpsimd
            def _(pool):
                with pool.Fori(0, CHUNKS) as c:
                    hold(pool, ph, o_done, c + 2)
                    pool.dma_start(node_rows(dram["tab0"], c), O[:, :, :]).then_inc(stored, 16)
                    hold(pool, ph, stored, 16 * c + 16)
                    pool.sem_inc(o_free, 1)

            @block.vector
            def _(dve):
                with dve.Fori(0, CHUNKS) as c:
                    dve.wait_ge(x_in, 16 * c + 16)
                    nm.vector(dve, c)
                    dve.wait_ge(mm_done, c + 2)
                    dve.wait_ge(o_free, c + 1)
                    flat = O[:, :, :].rearrange("p t n -> p (t n)")
                    for lo, hi in BANKS:
                        last = nc.vector.tensor_copy(flat[:, lo:hi], psO[:, lo:hi])
                    last.then_inc(o_done, 1)

            @block.scalar
            def _(act):
                act.preload_act_table_set(EXP_LN)
                with act.Fori(0, CHUNKS) as c:
                    nm.scalar_std(act, c)
                    nm.scalar_relu(act, c, mm_done, c + 1)

            @block.tensor
            def _(pe):
                pe.wait_ge(w_in, 16)
                with pe.Fori(0, CHUNKS) as c:
                    nm.tensor(pe, c)
                    pe.wait_ge(nm.hT_done, c + 2)
                    pe.wait_ge(o_done, c + 1)
                    project(nc, psO, nm.hT, w).then_inc(mm_done, 1)


def gather_group(nc, pool, ph, sh, table, rows, idx, g, done, gathered):
    nc.gpsimd.tensor_copy(idx[:, :], sh["src_sb"][:, bass.ds(g * GT, GT)]).then_inc(done, 1)
    hold(pool, ph, done, g + 1)
    for t in range(GT):
        nc.gpsimd.indirect_dma_start(
            out=rows[:, t, :], out_offset=None, in_=table[:, :],
            in_offset=bass.IndirectOffsetOnAxis(ap=idx[:, t:t + 1].bitcast(U32), axis=0),
        ).then_inc(gathered, 16)


def select_group(nc, sel, sh, g, coef=None):
    for t in range(GT):
        col = sh["rel"][:, bass.ds(g * GT + t, 1)]
        if coef is None:
            last = nc.vector.tensor_scalar(sel[:, t, :], sh["iota"][:, :], col, None, ALU.is_equal)
        else:
            last = nc.vector.tensor_scalar(sel[:, t, :], sh["iota"][:, :], col,
                                           coef[:, bass.ds(g * GT + t, 1)], ALU.is_equal, ALU.mult)
    return last


def window_bases(eng, regs, sh, g):
    eng.load(regs, sh["dst_sb"][0:1, bass.ds(g * GT, GT)])
    return [eng.snap(r, min_val=0, max_val=PAD_DST) for r in regs]


def back(it, b, n):
    return (it, b - n) if b >= n else (it - 1, b - n + NB)


def skewed(eng, step, tail):
    for b in range(NB):
        step(0, b, True)
    with eng.Fori(1, ITERS) as it:
        for b in range(NB):
            step(it, b, False)
    tail(ITERS - 1)


def edges_schnet(nc, dram, sh, acc):
    with Phase(nc, "l0") as ph:
        edge = [ph.sb(f"edge{i}", [P, GT * P]) for i in range(2)]
        fw1 = ph.sb("fw1", [P, D])
        fw2 = ph.sb("fw2", [P, KH, D])
        fb1 = ph.sb("fb1", [P, KH])
        fb2 = ph.sb("fb2", [P, D])
        cut = ph.sb("cut", [P, TILES])
        cut_i = ph.sb("cut_i", [P, TILES], I32)
        cut_f = ph.sb("cut_f", [P, TILES])
        half_pi = ph.sb("half_pi", [P, 1])
        rows = [ph.sb(f"rows{i}", [P, GT, D]) for i in range(NB)]
        idx = [ph.sb(f"idx{i}", [P, GT], I32) for i in range(NB)]
        sel = [ph.sb(f"sel{i}", [P, GT, P]) for i in range(NB)]
        ex = ph.sb("ex", [P, KH, GT * P])
        ssp = [ph.sb(f"ssp{i}", [P, KH, GT * P]) for i in range(2)]
        msg = [ph.sb(f"msg{i}", [P, GT, D]) for i in range(2)]
        psz = ph.ps("psz", 2 * KH * 512)
        psw = ph.ps("psw", 1024)
        psa = ph.ps("psa", 1024)
        S = ph.sem
        w_in, cut_sem, setup, bias_mm = S("w_in"), S("cut"), S("setup"), S("bias_mm")
        edge_in = [S("edge_in0"), S("edge_in1")]
        gathered = [S(f"gathered{i}") for i in range(NB)]
        idx_done = S("idx_done")
        z_done = S("z_done", 1)
        exp_done, cap_done = S("exp_done"), S("cap_done")
        ln_done = S("ln_done", 1)
        ssp_done = S("ssp_done", 2)
        w_done = S("w_done", 4)
        biased = S("biased")
        msg_done = S("msg_done", 2 * NB)
        sel_done = S("sel_done")
        win_done = S("win_done", 2 * NB)
        added = S("added", GT)

        ph.begin()
        with nc.Block() as block:

            @block.sync
            def _(sp):
                for k in range(2):
                    sp.dma_start(fw1[k * NG:(k + 1) * NG, :], dram["fw1_t"][:, :]).then_inc(w_in, 16)
                sp.dma_start(fw2[:, :, :], by_half(dram["fw2_t"])).then_inc(w_in, 16)
                sp.dma_start(fb1[:, :], dram["fb1"][:, :]).then_inc(w_in, 16)
                sp.dma_start(fb2[:, :], on_all(dram["fb2"], D)).then_inc(w_in, 16)
                sp.dma_start(cut[:, :], dram["ew_cols"][:, :]).then_inc(w_in, 16)
                with sp.Fori(0, ITERS) as it:
                    for q in range(2):
                        hold(sp, ph, z_done, it * NB + 2 * q + 1)
                        sp.dma_start(edge[q][:, :], dram["edge_t"][bass.ds(it * 2 + q, 1), :, :]
                                     .rearrange("a p n -> (a p) n")).then_inc(edge_in[q], 16)

            @block.gpsimd
            def _(pool):
                with pool.Fori(0, ITERS) as it:
                    for b in range(NB):
                        g = it * NB + b
                        pool.wait_ge(msg_done, 2 * g + 2)
                        gather_group(nc, pool, ph, sh, dram["tab0"], rows[b], idx[b], g, idx_done, gathered[b])

            @block.scalar
            def _(act):
                act.wait_ge(setup, 1)
                nc.scalar.activation(cut[:, :], cut_f[:, :], ACT.Sin, scale=-PI,
                                     bias=half_pi[:, 0:1]).then_inc(setup, 1)
                act.preload_act_table_set(EXP_LN)
                with act.Fori(0, ITERS) as it:
                    for b in range(NB):
                        g = it * NB + b
                        z = (b % 2) * KH * 512
                        act.wait_ge(z_done, g + 2)
                        act.wait_ge(ln_done, g + 1)
                        for k in range(KH):
                            last = nc.scalar.activation(ex[:, k, :], psz[:, z + k * 512:z + (k + 1) * 512], ACT.Exp,
                                                        bias=fb1[:, k:k + 1])
                        last.then_inc(exp_done, 1)
                        act.wait_ge(cap_done, g + 1)
                        act.wait_ge(w_done, 2 * g + 2)
                        nc.scalar.activation(ssp[b % 2][:, :, :], ex[:, :, :], ACT.Ln, bias=1.0).then_inc(ln_done, 1)

            @block.vector
            def _(dve):
                regs = [dve.alloc_register(f"l0_base{t}") for t in range(GT)]
                ch = Chain(dve, cut_sem)
                ch.link(nc.vector.memset(acc[:, :, :], 0.0))
                dve.wait_ge(w_in, 96)
                ch.link(nc.vector.tensor_scalar(cut_f[:, :], cut[:, :], 0.5, None, ALU.mult))
                ch.link(nc.vector.tensor_copy(cut_i[:, :], cut_f[:, :]))
                ch.link(nc.vector.tensor_copy(cut_f[:, :], cut_i[:, :]))
                ch.link(nc.vector.scalar_tensor_tensor(out=cut[:, :], in0=cut_f[:, :], scalar=-2.0, in1=cut[:, :],
                                                       op0=ALU.mult, op1=ALU.add))
                ch.link(nc.vector.memset(half_pi[:, :], HALF_PI))
                nc.vector.scalar_tensor_tensor(out=cut_f[:, :], in0=cut[:, :], scalar=-1.0, in1=cut[:, :],
                                               op0=ALU.mult, op1=ALU.max).then_inc(setup, 1)
                dve.wait_ge(setup, 2)
                ch.link(nc.vector.tensor_scalar(cut[:, :], cut[:, :], 0.25, 0.25, ALU.mult, ALU.add))
                dve.wait_ge(bias_mm, 1)
                nc.vector.scalar_tensor_tensor(out=fb2[:, :], in0=psw[:, 0:D], scalar=-LN2, in1=fb2[:, :],
                                               op0=ALU.mult, op1=ALU.add).then_inc(biased, 2)
                dve.wait_ge(biased, 2)

                def select(it, b, t):
                    g = it * NB + b
                    if t == 0:
                        dve.wait_ge(win_done, 2 * g + 2)
                    ins = nc.vector.tensor_scalar(sel[b][:, t, :], sh["iota"][:, :], sh["rel"][:, bass.ds(g * GT + t, 1)],
                                                  cut[:, bass.ds(g * GT + t, 1)], ALU.is_equal, ALU.mult)
                    if t == GT - 1:
                        ins.then_inc(sel_done, 1)

                def bias(it, b, h):
                    g = it * NB + b
                    dve.wait_ge(w_done, 2 * g + h + 5)
                    if h == 0:
                        dve.wait_ge(win_done, 2 * g + 6)
                    nc.vector.tensor_tensor(msg[b % 2][:, 2 * h:2 * h + 2, :],
                                            psw[:, h * 512:(h + 1) * 512].rearrange("p (t n) -> p t n", n=D),
                                            fb2[:, :].unsqueeze(1).to_broadcast([P, 2, D]), ALU.add).then_inc(biased, 1)

                def message(it, b, h):
                    g = it * NB + b
                    if h == 0:
                        dve.wait_ge(gathered[b], it * 64 + 64)
                    m = msg[b % 2][:, 2 * h:2 * h + 2, :]
                    dve.wait_ge(biased, 2 * g + h + 3)
                    nc.vector.tensor_tensor(m, m, rows[b][:, 2 * h:2 * h + 2, :], ALU.mult).then_inc(msg_done, 1)

                def add(it, b, bases, t):
                    g = it * NB + b
                    if t % 2 == 0:
                        dve.wait_ge(win_done, 2 * g + t // 2 + 2 * NB + 1)
                    dve.wait_ge(added, GT * g + t + GT)
                    a = acc[:, :, bass.ds(bases[t], P)]
                    nc.vector.tensor_tensor(a, a, psa[:, t * D:(t + 1) * D].rearrange("p (k r) -> p k r", k=KH),
                                            ALU.add).then_inc(added, 1)

                def cap(it, b):
                    g = it * NB + b
                    dve.wait_ge(exp_done, g + 1)
                    flat = ex[:, :, :].rearrange("p k n -> p (k n)")
                    nc.vector.tensor_scalar_min(flat, flat, EXP_CAP).then_inc(cap_done, 1)

                def softplus(it, b):
                    g = it * NB + b
                    dve.wait_ge(ln_done, g + 2)
                    z = (b % 2) * KH * 512
                    for k in range(KH):
                        last = nc.vector.scalar_tensor_tensor(
                            out=ssp[b % 2][:, k, :], in0=psz[:, z + k * 512:z + (k + 1) * 512], scalar=fb1[:, k:k + 1],
                            in1=ssp[b % 2][:, k, :], op0=ALU.add, op1=ALU.max)
                    last.then_inc(ssp_done, 1)

                def step(it, b, first):
                    f, m, a = (None if first and b < k else back(it, b, k) for k in (1, 2, 3))
                    bases = window_bases(dve, regs, sh, a[0] * NB + a[1]) if a else None
                    if a:
                        add(*a, bases, 0)
                    if m:
                        bias(*m, 1)
                    if a:
                        add(*a, bases, 1)
                    if m:
                        message(*m, 0)
                    if a:
                        add(*a, bases, 2)
                    cap(it, b)
                    if a:
                        add(*a, bases, 3)
                    if m:
                        message(*m, 1)
                    select(it, b, 0)
                    select(it, b, 1)
                    softplus(it, b)
                    if f:
                        bias(*f, 0)
                    select(it, b, 2)
                    select(it, b, 3)

                def tail(it):
                    bias(it, NB - 2, 1)
                    for h in range(2):
                        message(it, NB - 2, h)
                    for h in range(2):
                        bias(it, NB - 1, h)
                    for h in range(2):
                        message(it, NB - 1, h)
                    for b in range(1, NB):
                        bases = window_bases(dve, regs, sh, it * NB + b)
                        for t in range(GT):
                            add(it, b, bases, t)

                skewed(dve, step, tail)

            @block.tensor
            def _(pe):
                pe.wait_ge(w_in, 96)
                for k in range(KH):
                    last = nc.tensor.matmul(psw[:, 0:D], sh["ones"][:, :], fw2[:, k, :], start=(k == 0), stop=(k == KH - 1))
                last.then_inc(bias_mm, 1)

                def hidden(it, b):
                    g = it * NB + b
                    z = (b % 2) * KH * 512
                    half = slice((b % 2) * NG, (b % 2 + 1) * NG)
                    if b % 2 == 0:
                        pe.wait_ge(edge_in[b // 2], it * 16 + 16)
                    pe.wait_ge(ssp_done, g + 1)
                    for k in range(KH):
                        last = nc.tensor.matmul(psz[:, z + k * 512:z + (k + 1) * 512], fw1[half, k * P:(k + 1) * P],
                                                edge[b // 2][half, :], start=True, stop=True)
                    last.then_inc(z_done, 1)

                def filters(it, b):
                    g = it * NB + b
                    pe.wait_ge(ssp_done, g + 3)
                    for h in range(2):
                        pe.wait_ge(biased, 2 * g + h + 1)
                        for t in (2 * h, 2 * h + 1):
                            for k in range(KH):
                                last = nc.tensor.matmul(psw[:, t * D:(t + 1) * D], ssp[b % 2][:, k, t * P:(t + 1) * P],
                                                        fw2[:, k, :], start=(k == 0), stop=(k == KH - 1))
                        last.then_inc(w_done, 1)

                def windows(it, b):
                    g = it * NB + b
                    pe.wait_ge(sel_done, g + 1)
                    for h in range(2):
                        pe.wait_ge(msg_done, 2 * g + h + 2 * NB + 1)
                        pe.wait_ge(added, GT * g + 2 * h + 2)
                        for t in (2 * h, 2 * h + 1):
                            for k in range(KH):
                                last = nc.tensor.matmul(psa[:, t * D + k * P:t * D + (k + 1) * P],
                                                        msg[b % 2][:, t, k * P:(k + 1) * P], sel[b][:, t, :],
                                                        start=True, stop=True)
                        last.then_inc(win_done, 1)

                def step(it, b, first):
                    hidden(it, b)
                    if not first or b >= 1:
                        filters(*back(it, b, 1))
                    if not first or b >= 2:
                        windows(*back(it, b, 2))

                def tail(it):
                    filters(it, NB - 1)
                    windows(it, NB - 2)
                    windows(it, NB - 1)

                skewed(pe, step, tail)


def nodes_schnet(nc, dram, sh, acc):
    with Phase(nc, "n1") as ph:
        nm = Norm(ph, sh)
        w2, w3, wg = (ph.sb(s, [P, KH, D]) for s in ("w2", "w3", "wg"))
        gw = ph.sb("gw", [P, KH, D])
        att = ph.sb("att", [P, KH, 2 * HEADS])
        watt = ph.sb("watt", [P, KH, 2 * HEADS])
        b2 = ph.sb("b2", [P, KH])
        b3 = ph.sb("b3", [P, D])
        ssp = ph.sb("ssp", [P, KH, CN])
        O = ph.sb("O", [P, CT, D])
        A = ph.sb("A", [P, CT, 2 * HEADS])
        psO = ph.ps("psO", 2048)
        S = ph.sem
        w_in, att_zero, bias_mm, bias_done, watt_mm, watt_done = (S(s) for s in (
            "w_in", "att_zero", "bias_mm", "bias_done", "watt_mm", "watt_done"))
        res_in, z_done, exp_done, cap_done, ln_done, ssp_done = (S(s) for s in (
            "res_in", "z_done", "exp_done", "cap_done", "ln_done", "ssp_done"))
        y_biased, x_done, x_stored, o_stored = (S(s) for s in ("y_biased", "x_done", "x_stored", "o_stored"))
        y_done = S("y_done", 1)
        mm_done = S("mm_done", 1)
        o_done = S("o_done", 2)
        o_free = S("o_free", 1)
        zcols = [(k, h, k * 1024 + h * 512) for k in range(KH) for h in range(2)]
        HC = CN // 2

        ph.begin()
        with nc.Block() as block:

            @block.sync
            def _(sp):
                sp.dma_start(w2[:, :, :], by_half(dram["w2_t"])).then_inc(w_in, 16)
                sp.dma_start(w3[:, :, :], by_half(dram["w3_t"])).then_inc(w_in, 16)
                sp.dma_start(wg[:, :, :], by_half(dram["gat_w_t"])).then_inc(w_in, 16)
                sp.dma_start(gw[:, :, :], by_half(dram["gat_w"])).then_inc(w_in, 16)
                sp.dma_start(b2[:, :], dram["b2"][:, :]).then_inc(w_in, 16)
                sp.dma_start(b3[:, :], on_all(dram["b3"], D)).then_inc(w_in, 16)
                sp.wait_ge(att_zero, 1)
                for h in range(HEADS):
                    p = (h * HID) % P
                    for j, name in enumerate(("att_src", "att_dst")):
                        sp.dma_start(att[p:p + HID, h * HID // P, j * HEADS + h:j * HEADS + h + 1],
                                     dram[name][h * HID:(h + 1) * HID].rearrange("(p a) -> p a", a=1)).then_inc(w_in, 16)
                with sp.Fori(0, CHUNKS) as c:
                    sp.dma_start(nm.X[:, :, :], node_rows(dram["x"], c)).then_inc(res_in, 16)
                    hold(sp, ph, x_done, c + 1)
                    sp.dma_start(node_rows(dram["x1"], c), nm.X[:, :, :]).then_inc(x_stored, 16)
                    hold(sp, ph, x_stored, 16 * c + 16)
                    hold(sp, ph, nm.norm_done, c + 2)

            @block.gpsimd
            def _(pool):
                with pool.Fori(0, CHUNKS) as c:
                    hold(pool, ph, o_done, 2 * c + 4)
                    pool.dma_start(node_rows(dram["tab1"], c), O[:, :, :]).then_inc(o_stored, 16)
                    pool.dma_start(node_rows(dram["tab_as"], c), A[:, :, 0:HEADS]).then_inc(o_stored, 16)
                    pool.dma_start(node_rows(dram["att_tab"], c), A[:, :, :]).then_inc(o_stored, 16)
                    hold(pool, ph, o_stored, 48 * c + 48)
                    pool.sem_inc(o_free, 1)

            @block.scalar
            def _(act):
                act.preload_act_table_set(EXP_LN)
                with act.Fori(0, CHUNKS) as c:
                    act.wait_ge(z_done, c + 1)
                    act.wait_ge(y_done, c + 1)
                    for k, h, col in zcols:
                        last = nc.scalar.activation(ssp[:, k, h * HC:(h + 1) * HC], psO[:, col:col + HC], ACT.Exp,
                                                    bias=b2[:, k:k + 1])
                    last.then_inc(exp_done, 1)
                    act.wait_ge(cap_done, c + 1)
                    nc.scalar.activation(ssp[:, :, :], ssp[:, :, :], ACT.Ln, bias=1.0).then_inc(ln_done, 1)
                    nm.scalar_std(act, c)
                    nm.scalar_relu(act, c, mm_done, c + 1)

            @block.vector
            def _(dve):
                nc.vector.memset(att[:, :, :], 0.0).then_inc(att_zero, 1)
                dve.wait_ge(w_in, 16 * 22)
                dve.wait_ge(bias_mm, 1)
                nc.vector.scalar_tensor_tensor(out=b3[:, :], in0=psO[:, 0:D], scalar=-LN2, in1=b3[:, :],
                                               op0=ALU.mult, op1=ALU.add).then_inc(bias_done, 1)
                dve.wait_ge(watt_mm, 1)
                nc.vector.tensor_copy(watt[:, :, :].rearrange("p k n -> p (k n)"),
                                      psO[:, 512:512 + KH * 2 * HEADS]).then_inc(watt_done, 1)
                dve.wait_ge(bias_done, 1)
                with dve.Fori(0, CHUNKS) as c:
                    dve.wait_ge(exp_done, c + 1)
                    flat = ssp[:, :, :].rearrange("p k n -> p (k n)")
                    nc.vector.tensor_scalar_min(flat, flat, EXP_CAP).then_inc(cap_done, 1)
                    dve.wait_ge(ln_done, c + 1)
                    for k, h, col in zcols:
                        part = ssp[:, k, h * HC:(h + 1) * HC]
                        last = nc.vector.scalar_tensor_tensor(out=part, in0=psO[:, col:col + HC], scalar=b2[:, k:k + 1],
                                                              in1=part, op0=ALU.add, op1=ALU.max)
                    last.then_inc(ssp_done, 1)
                    dve.wait_ge(res_in, 16 * c + 16)
                    dve.wait_ge(y_done, c + 2)
                    xf = nm.X[:, :, :].rearrange("p t n -> p (t n)")
                    for lo, hi in BANKS:
                        last = nc.vector.tensor_tensor(xf[:, lo:hi], xf[:, lo:hi], psO[:, lo:hi], ALU.add)
                    last.then_inc(y_biased, 1)
                    dve.wait_ge(y_biased, c + 1)
                    nc.vector.tensor_tensor(nm.X[:, :, :], nm.X[:, :, :],
                                            b3[:, :].unsqueeze(1).to_broadcast([P, CT, D]), ALU.add).then_inc(x_done, 1)
                    dve.wait_ge(x_done, c + 1)
                    nm.vector(dve, c)
                    dve.wait_ge(mm_done, c + 2)
                    dve.wait_ge(o_free, c + 1)
                    flat = O[:, :, :].rearrange("p t n -> p (t n)")
                    for lo, hi in BANKS:
                        last = nc.vector.tensor_copy(flat[:, lo:hi], psO[:, lo:hi])
                    last.then_inc(o_done, 1)
                    nc.vector.tensor_copy(A[:, :, :].rearrange("p t n -> p (t n)"),
                                          nm.psT[:, 0:CT * 2 * HEADS]).then_inc(o_done, 1)

            @block.tensor
            def _(pe):
                pe.wait_ge(w_in, 16 * 22)
                for k in range(KH):
                    last = nc.tensor.matmul(psO[:, 0:D], sh["ones"][:, :], w3[:, k, :], start=(k == 0), stop=(k == KH - 1))
                last.then_inc(bias_mm, 1)
                for k in range(KH):
                    for f in range(KH):
                        last = nc.tensor.matmul(psO[:, 512 + k * 2 * HEADS:512 + (k + 1) * 2 * HEADS],
                                                gw[:, f, k * P:(k + 1) * P], att[:, f, :],
                                                start=(f == 0), stop=(f == KH - 1))
                last.then_inc(watt_mm, 1)
                pe.wait_ge(bias_done, 1)
                pe.wait_ge(watt_done, 1)
                with pe.Fori(0, CHUNKS) as c:
                    pe.wait_ge(o_done, 2 * c + 2)
                    for k, h, col in zcols:
                        for f in range(KH):
                            last = nc.tensor.matmul(psO[:, col:col + HC], w2[:, f, k * P:(k + 1) * P],
                                                    acc[:, f, bass.ds(c * CN + h * HC, HC)],
                                                    start=(f == 0), stop=(f == KH - 1))
                    last.then_inc(z_done, 1)
                    pe.wait_ge(ssp_done, c + 1)
                    project(nc, psO, ssp, w3).then_inc(y_done, 1)
                    nm.tensor(pe, c)
                    pe.wait_ge(nm.hT_done, c + 2)
                    pe.wait_ge(y_biased, c + 1)
                    for t in range(CT):
                        for k in range(KH):
                            nc.tensor.matmul(nm.psT[:, t * 2 * HEADS:(t + 1) * 2 * HEADS],
                                             nm.hT[:, k, t * P:(t + 1) * P], watt[:, k, :],
                                             start=(k == 0), stop=(k == KH - 1))
                    project(nc, psO, nm.hT, wg).then_inc(mm_done, 1)


def edges_max(nc, dram, sh, a_src, seg_max):
    SH = SEG * HEADS
    with Phase(nc, "mx") as ph:
        prev_c, next_c = ph.sb("prev_c", [P, TILES], I32), ph.sb("next_c", [P, TILES], I32)
        last_b = ph.sb("last_b", [P, TILES], I32)
        pen = [ph.sb(f"pen{i}", [P, TILES]) for i in range(2)]
        out_seg = [ph.sb(f"out_seg{i}", [P, TILES]) for i in range(2)]
        slot = [ph.sb(f"slot{i}", [P, SEG, HEADS]) for i in range(2)]
        idx = [ph.sb(f"idx{i}", [P, SEG], I32) for i in range(2)]
        pen_x = ph.sb("pen_x", [P, 2, SEG, HEADS])
        pen_t = ph.sb("pen_t", [P, 2, P])
        scan = ph.sb("scan", [P, 2, P])
        both = ph.sb("both", [P, P])
        ends = ph.sb("ends", [P, 2, ITERS])
        row = {n: ph.sb(f"row_{n}", [HEADS, TILES], I32) for n in ("first", "last", "prev", "next")}
        one = ph.sb("one", [HEADS, TILES])
        cont = ph.sb("cont", [HEADS, 2, TILES])
        pass_on = ph.sb("pass_on", [HEADS, 2, TILES])
        tile_max = ph.sb("tile_max", [HEADS, 2, TILES])
        run = ph.sb("run", [HEADS, 2, TILES])
        carry = ph.sb("carry", [HEADS, 2, TILES])
        carry_b = ph.sb("carry_b", [P, TILES, HEADS])
        ps = ph.ps("ps", 2048)
        S = ph.sem
        loaded, link = S("loaded"), S("link")
        gathered = [S("gathered0"), S("gathered1")]
        idx_done, penx_done, pent_ps, pent_done = (S(s) for s in ("idx_done", "penx_done", "pent_ps", "pent_done"))
        val_done = S("val_done", 2)
        scan_done = S("scan_done", 1)
        both_done = S("both_done", 1)
        max_done = S("max_done", 1)
        kept = S("kept", 1)
        copied = S("copied", 2)
        ends_done, ends_out, ends_in = S("ends_done", 2), S("ends_out"), S("ends_in")
        carry_done, carry_out, carry_in, merged = S("carry_done"), S("carry_out"), S("carry_in"), S("merged")

        ph.begin()
        with nc.Block() as block:

            @block.sync
            def _(sp):
                sp.dma_start(prev_c[:, :], dram["prev_cols"][:, :]).then_inc(loaded, 16)
                sp.dma_start(next_c[:, :], dram["next_cols"][:, :]).then_inc(loaded, 16)
                sp.dma_start(last_b[:, :], dram["dst_cols"][P - 1:P, :].broadcast_to([P, TILES])).then_inc(loaded, 16)
                for name, src in (("first", dram["dst_cols"][0:1, :]), ("last", dram["dst_cols"][P - 1:P, :]),
                                  ("prev", dram["prev_cols"][0:1, :]), ("next", dram["next_cols"][P - 1:P, :])):
                    sp.dma_start(row[name][:, :], src.broadcast_to([HEADS, TILES])).then_inc(loaded, 16)
                sp.wait_ge(ends_done, 2 * ITERS + 2)
                for w, name in enumerate(("last_max", "first_max")):
                    sp.dma_start(dram[name][:, :], ends[:, w, :]).then_inc(ends_out, 16)
                sp.wait_ge(ends_out, 32)
                with nc.allow_non_contiguous_dma(reason="transposes 6656 values, twice in the program"):
                    for w, name in enumerate(("last_max", "first_max")):
                        for t in range(SEG):
                            sp.dma_start(tile_max[:, w, t::SEG],
                                         dram[name][t * HEADS:(t + 1) * HEADS, :]).then_inc(ends_in, 16)
                    sp.wait_ge(carry_done, 1)
                    for w in range(2):
                        sp.dma_start(dram["carry"][w, :, :].rearrange("t h -> h t"), carry[:, w, :]).then_inc(carry_out, 16)
                sp.wait_ge(carry_out, 32)
                for w in range(2):
                    if w == 1:
                        sp.wait_ge(merged, 1)
                    sp.dma_start(carry_b[:, :, :].rearrange("p t h -> p (t h)"),
                                 dram["carry"][w:w + 1, :, :].rearrange("a t h -> a (t h)")
                                 .broadcast_to([P, TILES * HEADS])).then_inc(carry_in, 16)

            @block.gpsimd
            def _(pool):
                with pool.Fori(0, ITERS // 2) as i2:
                    for q in range(2):
                        it = i2 * 2 + q
                        hold(pool, ph, val_done, it + 1)
                        hold(pool, ph, copied, it + 1)
                        nc.gpsimd.tensor_copy(idx[q][:, :], sh["src_sb"][:, bass.ds(it * SEG, SEG)]).then_inc(idx_done, 1)
                        hold(pool, ph, idx_done, it + 1)
                        for t in range(SEG):
                            nc.gpsimd.indirect_dma_start(
                                out=slot[q][:, t, :], out_offset=None, in_=dram["tab_as"][:, :],
                                in_offset=bass.IndirectOffsetOnAxis(ap=idx[q][:, t:t + 1].bitcast(U32), axis=0),
                            ).then_inc(gathered[q], 16)

            @block.scalar
            def _(act):
                act.wait_ge(link, 4)
                with act.Fori(0, ITERS // 2) as i2:
                    for q in range(2):
                        it = i2 * 2 + q
                        act.wait_ge(scan_done, it + 1)
                        for w in range(2):
                            last = nc.scalar.activation(
                                pen_x[:, w, :, :], pen[w][:, bass.ds(it * SEG, SEG)].unsqueeze(2)
                                .to_broadcast([P, SEG, HEADS]), ACT.Copy)
                        last.then_inc(penx_done, 1)
                        act.wait_ge(pent_ps, it + 1)
                        nc.scalar.activation(pen_t[:, :, :].rearrange("p w e -> p (w e)"), ps[:, 512:512 + 2 * P],
                                             ACT.Copy).then_inc(pent_done, 1)
                        act.wait_ge(gathered[q], i2 * 16 * SEG + 16 * SEG)
                        nc.scalar.activation(a_src[:, bass.ds(it * SH, SH)], slot[q][:, :, :].rearrange("p t h -> p (t h)"),
                                             ACT.Copy).then_inc(copied, 1)
                        act.wait_ge(scan_done, it + 2)
                        nc.scalar.activation(ends[:, 0, bass.ds(it, 1)], scan[:, 0, P - 1:P], ACT.Copy).then_inc(ends_done, 1)
                        nc.scalar.activation(ends[:, 1, bass.ds(it, 1)], scan[:, 1, 0:1], ACT.Copy).then_inc(ends_done, 1)

            @block.vector
            def _(dve):
                ch = Chain(dve, link)

                def penalty(out, a, b, op=ALU.not_equal):
                    ch.link(nc.vector.tensor_tensor(out, a, b, op))
                    ch.link(nc.vector.tensor_scalar(out, out, -BIG, None, ALU.mult))

                dve.wait_ge(loaded, 16 * 7)
                penalty(pen[0][:, :], sh["dst_sb"][:, :], prev_c[:, :])
                penalty(pen[1][:, :], sh["dst_sb"][:, :], next_c[:, :])
                ch.link(nc.vector.tensor_scalar(out_seg[0][:, :], sh["rel"][:, :], 0.0, -BIG, ALU.not_equal, ALU.mult))
                penalty(out_seg[1][:, :], sh["dst_sb"][:, :], last_b[:, :])
                with dve.Fori(0, ITERS // 2) as i2:
                    for q in range(2):
                        it = i2 * 2 + q
                        dve.wait_ge(val_done, it + 3)
                        dve.wait_ge(pent_done, it + 1)
                        dve.wait_ge(both_done, it + 1)
                        dve.wait_ge(ends_done, 2 * it + 2)
                        nc.vector.tensor_tensor_scan(scan[:, 0, :], pen_t[:, 0, :], ps[:, 0:P], -BIG, ALU.add, ALU.max)
                        nc.vector.tensor_tensor_scan(scan[:, 1, ::-1], pen_t[:, 1, ::-1], ps[:, 0:P][:, ::-1],
                                                     -BIG, ALU.add, ALU.max).then_inc(scan_done, 1)
                        dve.wait_ge(scan_done, it + 2)
                        dve.wait_ge(max_done, it + 1)
                        nc.vector.tensor_tensor(both[:, :], scan[:, 0, :], scan[:, 1, :], ALU.max).then_inc(both_done, 1)
                        dve.wait_ge(max_done, it + 2)
                        nc.vector.tensor_copy(seg_max[:, bass.ds(it * SH, SH)], ps[:, 1024:1024 + P]).then_inc(kept, 1)
                t_first, t_last, t_prev, t_next = (row[n] for n in ("first", "last", "prev", "next"))
                penalty(one[:, :], t_first[:, :], t_last[:, :])
                penalty(cont[:, 0, :], t_first[:, :], t_prev[:, :])
                penalty(cont[:, 1, :], t_last[:, :], t_next[:, :])
                for w in range(2):
                    ch.link(nc.vector.tensor_tensor(pass_on[:, w, :], cont[:, w, :], one[:, :], ALU.min))
                dve.wait_ge(ends_in, 16 * 2 * SEG)
                ch.link(nc.vector.tensor_tensor_scan(run[:, 0, :], pass_on[:, 0, :], tile_max[:, 0, :], -BIG, ALU.add, ALU.max))
                ch.link(nc.vector.tensor_tensor_scan(run[:, 1, ::-1], pass_on[:, 1, ::-1], tile_max[:, 1, ::-1],
                                                     -BIG, ALU.add, ALU.max))
                nc.vector.memset(carry[:, 0, 0:1], -BIG)
                nc.vector.memset(carry[:, 1, TILES - 1:TILES], -BIG)
                nc.vector.tensor_tensor(carry[:, 0, 1:TILES], run[:, 0, 0:TILES - 1], cont[:, 0, 1:TILES], ALU.add)
                nc.vector.tensor_tensor(carry[:, 1, 0:TILES - 1], run[:, 1, 1:TILES], cont[:, 1, 0:TILES - 1],
                                        ALU.add).then_inc(carry_done, 1)
                dve.wait_ge(kept, ITERS + 1)
                for w in range(2):
                    dve.wait_ge(carry_in, 16 * w + 16)
                    ch.link(nc.vector.tensor_tensor(carry_b[:, :, :], carry_b[:, :, :],
                                                    out_seg[w][:, :].unsqueeze(2).to_broadcast([P, TILES, HEADS]), ALU.add))
                    nc.vector.tensor_tensor(seg_max[:, :], seg_max[:, :], carry_b[:, :, :].rearrange("p t h -> p (t h)"),
                                            ALU.max).then_inc(merged, 1)
                    dve.wait_ge(merged, w + 1)

            @block.tensor
            def _(pe):
                with pe.Fori(0, ITERS // 2) as i2:
                    for q in range(2):
                        it = i2 * 2 + q
                        pe.wait_ge(penx_done, it + 1)
                        for w in range(2):
                            last = nc.tensor.transpose(ps[:, 512 + w * P:512 + (w + 1) * P],
                                                       pen_x[:, w, :, :].rearrange("p t h -> p (t h)"), sh["ident"][:, :])
                        last.then_inc(pent_ps, 1)
                        pe.wait_ge(gathered[q], i2 * 16 * SEG + 16 * SEG)
                        pe.wait_ge(scan_done, it + 1)
                        nc.tensor.transpose(ps[:, 0:P], slot[q][:, :, :].rearrange("p t h -> p (t h)"),
                                            sh["ident"][:, :]).then_inc(val_done, 1)
                        pe.wait_ge(both_done, it + 2)
                        pe.wait_ge(kept, it + 1)
                        nc.tensor.transpose(ps[:, 1024:1024 + P], both[:, :], sh["ident"][:, :]).then_inc(max_done, 1)


def edges_gat(nc, dram, sh, a_src, seg_max, acc, acc_d):
    W2 = 2 * HEADS
    with Phase(nc, "l1") as ph:
        next_c = ph.sb("next_c", [P, TILES], I32)
        is_last = ph.sb("is_last", [P, TILES])
        rows = [ph.sb(f"rows{i}", [P, GT, D]) for i in range(NB)]
        idx = [ph.sb(f"idx{i}", [P, GT], I32) for i in range(NB)]
        sel = [ph.sb(f"sel{i}", [P, GT, P]) for i in range(NB)]
        win = [ph.sb(f"win{i}", [P, GT, W2]) for i in range(NB)]
        sel_t = [ph.sb(f"sel_t{i}", [P, GT, P]) for i in range(2)]
        logit = ph.sb("logit", [P, 2, GT * HEADS])
        lrelu = ph.sb("lrelu", [P, 2, GT * HEADS])
        diff = [ph.sb(f"diff{i}", [P, GT, HEADS]) for i in range(2)]
        wx = [ph.sb(f"wx{i}", [P, GT, W2]) for i in range(NB)]
        pst = ph.ps("pst", 512)
        pse = ph.ps("pse", 512)
        psa = ph.ps("psa", 2048)
        psd = ph.ps("psd", 1024)
        S = ph.sem
        loaded, setup = S("loaded"), S("setup")
        gathered = [S(f"gathered{i}") for i in range(NB)]
        win_in = [S(f"win_in{i}") for i in range(NB)]
        idx_done, sel_done = S("idx_done"), S("sel_done")
        st_ps = S("st_ps", 1)
        st_done = S("st_done", 1)
        exp_in = S("exp_in", 4)
        link = S("link", 1)
        logits = S("logits", 2)
        w_done = S("w_done")
        msg_done = S("msg_done")
        win_done = S("win_done", NB)
        added = S("added", 4 * GT)

        ph.begin()
        with nc.Block() as block:

            @block.sync
            def _(sp):
                sp.dma_start(next_c[:, :], dram["next_cols"][:, :]).then_inc(loaded, 16)
                regs = [sp.alloc_register(f"l1_row{t}") for t in range(GT)]
                with sp.Fori(0, ITERS) as it:
                    for b in range(NB):
                        g = it * NB + b
                        hold(sp, ph, exp_in, g + 1)
                        for t, base in enumerate(window_bases(sp, regs, sh, g)):
                            sp.dma_start(win[b][:, t, :], dram["att_tab"][bass.ds(base, P), :]).then_inc(win_in[b], 16)

            @block.gpsimd
            def _(pool):
                with pool.Fori(0, ITERS) as it:
                    for b in range(NB):
                        g = it * NB + b
                        hold(pool, ph, win_done, g + 1)
                        gather_group(nc, pool, ph, sh, dram["tab1"], rows[b], idx[b], g, idx_done, gathered[b])

            @block.scalar
            def _(act):
                def copy_sel(it, b):
                    g = it * NB + b
                    act.wait_ge(st_ps, g + 2)
                    act.wait_ge(exp_in, g + 3)
                    nc.scalar.activation(sel_t[b % 2][:, :, :].rearrange("p t e -> p (t e)"), pst[:, :],
                                         ACT.Copy).then_inc(st_done, 1)

                def weights(it, b):
                    g = it * NB + b
                    act.wait_ge(logits, g + 3)
                    act.wait_ge(win_done, g + 1)
                    nc.scalar.activation(wx[b][:, :, 0:HEADS], diff[b % 2][:, :, :], ACT.Exp).then_inc(w_done, 1)

                def step(it, b, first):
                    copy_sel(it, b)
                    if not first or b >= 1:
                        weights(*back(it, b, 1))

                skewed(act, step, lambda it: weights(it, NB - 1))

            @block.vector
            def _(dve):
                regs = [dve.alloc_register(f"l1_base{t}") for t in range(GT)]
                dve.wait_ge(loaded, 16)
                nc.vector.memset(acc[:, :, :], 0.0)
                nc.vector.memset(acc_d[:, :], 0.0)
                nc.vector.tensor_tensor(is_last[:, :], sh["dst_sb"][:, :], next_c[:, :], ALU.not_equal).then_inc(setup, 1)
                dve.wait_ge(setup, 1)

                def select(it, b, t):
                    g = it * NB + b
                    if t == 0:
                        dve.wait_ge(win_done, g + 1)
                    ins = nc.vector.tensor_scalar(sel[b][:, t, :], sh["iota"][:, :], sh["rel"][:, bass.ds(g * GT + t, 1)],
                                                  None, ALU.is_equal)
                    if t == GT - 1:
                        ins.then_inc(sel_done, 1)

                def logits_of(it, b, step):
                    g = it * NB + b
                    e = pse[:, (b % 2) * GT * W2:(b % 2 + 1) * GT * W2].rearrange("p (t n) -> p t n", n=W2)
                    l0, l1 = (logit[:, w, :].rearrange("p (t n) -> p t n", n=HEADS) for w in range(2))
                    r0, r1 = (lrelu[:, w, :].rearrange("p (t n) -> p t n", n=HEADS) for w in range(2))
                    span = bass.ds(g * GT * HEADS, GT * HEADS)
                    mx, av = (x[:, span].rearrange("p (t n) -> p t n", n=HEADS) for x in (seg_max, a_src))
                    if step == 0:
                        dve.wait_ge(exp_in, g + 5)
                        nc.vector.tensor_tensor(l0, mx, e[:, :, 0:HEADS], ALU.max).then_inc(link, 1)
                        nc.vector.tensor_tensor(l1, av, e[:, :, HEADS:W2], ALU.add)
                    elif step == 1:
                        dve.wait_ge(link, g * 3 + 2)
                        nc.vector.tensor_tensor(l0, l0, e[:, :, HEADS:W2], ALU.add).then_inc(link, 1)
                    elif step == 2:
                        dve.wait_ge(link, g * 3 + 3)
                        nc.vector.scalar_tensor_tensor(out=lrelu[:, :, :], in0=logit[:, :, :], scalar=0.2,
                                                       in1=logit[:, :, :], op0=ALU.mult, op1=ALU.max).then_inc(link, 1)
                    else:
                        dve.wait_ge(link, g * 3 + 4)
                        dve.wait_ge(win_done, g + 1)
                        nc.vector.tensor_tensor(wx[b][:, :, HEADS:W2], r0,
                                                is_last[:, bass.ds(g * GT, GT)].unsqueeze(2)
                                                .to_broadcast([P, GT, HEADS]), ALU.mult)
                        nc.vector.tensor_tensor(diff[b % 2][:, :, :], r1, r0, ALU.subtract).then_inc(logits, 1)

                def message(it, b, t):
                    if t == 0:
                        dve.wait_ge(gathered[b], it * 64 + 64)
                        dve.wait_ge(w_done, it * NB + b + 1)
                    m = rows[b][:, t, :].rearrange("p (h n) -> p h n", n=HID)
                    ins = nc.vector.tensor_tensor(m, m, wx[b][:, t, 0:HEADS].unsqueeze(2).to_broadcast([P, HEADS, HID]),
                                                  ALU.mult)
                    if t == GT - 1:
                        ins.then_inc(msg_done, 1)

                def add(it, b, bases, t, w):
                    g = it * NB + b
                    if t == 0 and w == 0:
                        dve.wait_ge(win_done, g + NB + 1)
                    dve.wait_ge(added, 2 * (GT * g + t) + w + 4 * GT - 1)
                    if w == 0:
                        a = acc[:, :, bass.ds(bases[t], P)]
                        col = (b % 2) * 1024 + t * D
                        nc.vector.tensor_tensor(a, a, psa[:, col:col + D].rearrange("p (k r) -> p k r", k=KH),
                                                ALU.add).then_inc(added, 1)
                    else:
                        a = acc_d[:, bass.ds(bases[t], P)]
                        col = (b % 2) * 512 + t * P
                        nc.vector.tensor_tensor(a, a, psd[0:W2, col:col + P], ALU.add).then_inc(added, 1)

                def step(it, b, first):
                    n, m, a = (None if first and b < k else back(it, b, k) for k in (1, 2, 3))
                    bases = window_bases(dve, regs, sh, a[0] * NB + a[1]) if a else None
                    for t in range(GT):
                        select(it, b, t)
                    if m:
                        for t in range(GT):
                            message(*m, t)
                    for t in range(GT):
                        if n:
                            logits_of(*n, t)
                        if a:
                            for w in range(2):
                                add(*a, bases, t, w)

                def tail(it):
                    for t in range(GT):
                        logits_of(it, 3, t)
                        message(it, 2, t)
                    for t in range(GT):
                        message(it, 3, t)
                    for b in range(1, NB):
                        bases = window_bases(dve, regs, sh, it * NB + b)
                        for t in range(GT):
                            for w in range(2):
                                add(it, b, bases, t, w)

                skewed(dve, step, tail)

            @block.tensor
            def _(pe):
                def transpose(it, b):
                    g = it * NB + b
                    pe.wait_ge(sel_done, g + 1)
                    pe.wait_ge(st_done, g + 1)
                    for t in range(GT):
                        last = nc.tensor.transpose(pst[:, t * P:(t + 1) * P], sel[b][:, t, :], sh["ident"][:, :])
                    last.then_inc(st_ps, 1)

                def expand(it, b):
                    g = it * NB + b
                    pe.wait_ge(st_done, g + 2)
                    pe.wait_ge(win_in[b], it * 64 + 64)
                    pe.wait_ge(logits, g + 2)
                    for t in range(GT):
                        col = (b % 2) * GT * W2 + t * W2
                        last = nc.tensor.matmul(pse[:, col:col + W2], sel_t[b % 2][:, t, :], win[b][:, t, :],
                                                start=True, stop=True)
                    last.then_inc(exp_in, 1)

                def windows(it, b):
                    g = it * NB + b
                    pe.wait_ge(msg_done, g + 1)
                    pe.wait_ge(added, 2 * GT * g + 2 * GT)
                    for t in range(GT):
                        for k in range(KH):
                            col = (b % 2) * 1024 + t * D + k * P
                            nc.tensor.matmul(psa[:, col:col + P], rows[b][:, t, k * P:(k + 1) * P], sel[b][:, t, :],
                                             start=True, stop=True)
                        col = (b % 2) * 512 + t * P
                        last = nc.tensor.matmul(psd[0:W2, col:col + P], wx[b][:, t, :], sel[b][:, t, :],
                                                start=True, stop=True)
                    last.then_inc(win_done, 1)

                def step(it, b, first):
                    if not first or b >= 1:
                        expand(*back(it, b, 1))
                    transpose(it, b)
                    if not first or b >= 2:
                        windows(*back(it, b, 2))

                def tail(it):
                    expand(it, 3)
                    windows(it, 2)
                    windows(it, 3)

                skewed(pe, step, tail)


def stage_chunk(nc, act, parts, sem, c):
    for dst, src in parts:
        last = nc.scalar.activation(dst, src, ACT.Copy)
    last.then_inc(sem, 1)


def unstage(nc, out, stage, ident):
    for t in range(CT):
        for k in range(KH):
            col = t * D + k * P
            last = nc.tensor.transpose(out[:, col:col + P], stage[:, k, t * P:(t + 1) * P], ident)
    return last


def nodes_gat(nc, dram, sh, acc, acc_d):
    W2 = 2 * HEADS
    with Phase(nc, "n2") as ph:
        nm = Norm(ph, sh)
        w = ph.sb("w", [P, KH, D])
        gat_b, mean_b = ph.sb("gat_b", [P, D]), ph.sb("mean_b", [P, D])
        stage = ph.sb("stage", [P, KH, CN])
        stage_d = ph.sb("stage_d", [W2, CN])
        H = ph.sb("H", [P, CT, D])
        neg = ph.sb("neg", [P, CT, D])
        att = ph.sb("att", [P, CT, W2])
        self_l = ph.sb("self_l", [P, CT, HEADS])
        self_w = ph.sb("self_w", [P, CT, HEADS])
        den = ph.sb("den", [P, CT, HEADS])
        psO = ph.ps("psO", 2048)
        S = ph.sem
        w_in, x_in, h_in, a_in, x_stored, o_stored = (S(s) for s in ("w_in", "x_in", "h_in", "a_in", "x_stored", "o_stored"))
        staged, back_done, link, l_done, w_done, neg_done, neg_exp, x_done = (S(s) for s in (
            "staged", "back_done", "link", "l_done", "w_done", "neg_done", "neg_exp", "x_done"))
        h_free = S("h_free", 1)
        mm_done = S("mm_done", 1)
        o_done = S("o_done", 1)

        ph.begin()
        with nc.Block() as block:

            @block.sync
            def _(sp):
                sp.dma_start(w[:, :, :], by_half(dram["mean_w"])).then_inc(w_in, 16)
                sp.dma_start(gat_b[:, :], on_all(dram["gat_b"], D)).then_inc(w_in, 16)
                sp.dma_start(mean_b[:, :], on_all(dram["mean_b"], D)).then_inc(w_in, 16)
                with sp.Fori(0, CHUNKS) as c:
                    sp.dma_start(att[:, :, :], node_rows(dram["att_tab"], c)).then_inc(a_in, 16)
                    sp.dma_start(nm.X[:, :, :], node_rows(dram["x1"], c)).then_inc(x_in, 16)
                    hold(sp, ph, h_free, c + 1)
                    sp.dma_start(H[:, :, :], node_rows(dram["tab1"], c)).then_inc(h_in, 16)
                    hold(sp, ph, x_done, c + 1)
                    sp.dma_start(node_rows(dram["x2"], c), nm.X[:, :, :]).then_inc(x_stored, 16)
                    hold(sp, ph, x_stored, 16 * c + 16)
                    hold(sp, ph, nm.norm_done, c + 2)

            @block.gpsimd
            def _(pool):
                with pool.Fori(0, CHUNKS) as c:
                    hold(pool, ph, o_done, c + 2)
                    pool.dma_start(node_rows(dram["tab2"], c), H[:, :, :]).then_inc(o_stored, 16)
                    hold(pool, ph, o_stored, 16 * c + 16)
                    pool.sem_inc(h_free, 1)

            @block.scalar
            def _(act):
                act.preload_act_table_set(EXP_LN)
                with act.Fori(0, CHUNKS) as c:
                    act.wait_ge(mm_done, c + 1)
                    stage_chunk(nc, act, [(stage[:, k, :], acc[:, k, bass.ds(c * CN, CN)]) for k in range(KH)]
                                + [(stage_d[:, :], acc_d[:, bass.ds(c * CN, CN)])], staged, c)
                    act.wait_ge(l_done, c + 1)
                    nc.scalar.activation(self_w[:, :, :], self_l[:, :, :], ACT.Exp).then_inc(w_done, 1)
                    act.wait_ge(neg_done, c + 1)
                    nc.scalar.activation(neg[:, :, :], neg[:, :, :], ACT.Exp).then_inc(neg_exp, 1)
                    nm.scalar_std(act, c)
                    nm.scalar_relu(act, c, mm_done, c + 1)

            @block.vector
            def _(dve):
                dve.wait_ge(w_in, 48)
                with dve.Fori(0, CHUNKS) as c:
                    per = 10
                    ch = Chain(dve, link, c * per)
                    flat = H[:, :, :].rearrange("p t n -> p (t n)")
                    heads = H[:, :, :].rearrange("p t (h n) -> p (t h) n", n=HID)
                    dd = nm.psT[:, 0:CT * W2].rearrange("p (t n) -> p t n", n=W2)
                    dve.wait_ge(a_in, 16 * c + 16)
                    ch.link(nc.vector.tensor_tensor(self_l[:, :, :], att[:, :, 0:HEADS], att[:, :, HEADS:W2], ALU.add))
                    ch.link(nc.vector.scalar_tensor_tensor(out=self_l[:, :, :], in0=self_l[:, :, :], scalar=0.2,
                                                           in1=self_l[:, :, :], op0=ALU.mult, op1=ALU.max))
                    dve.wait_ge(back_done, c + 1)
                    nc.vector.tensor_tensor(self_l[:, :, :], self_l[:, :, :], dd[:, :, HEADS:W2],
                                            ALU.subtract).then_inc(l_done, 1)
                    dve.wait_ge(w_done, c + 1)
                    ch.link(nc.vector.scalar_tensor_tensor(out=den[:, :, :], in0=dd[:, :, 0:HEADS], scalar=1e-16,
                                                           in1=self_w[:, :, :], op0=ALU.add, op1=ALU.add))
                    ch.link(nc.vector.reciprocal(den[:, :, :], den[:, :, :]))
                    dve.wait_ge(h_in, 16 * c + 16)
                    ch.link(nc.vector.tensor_tensor(heads, heads, self_w[:, :, :].rearrange("p t h -> p (t h)")
                                                    .unsqueeze(2).to_broadcast([P, CT * HEADS, HID]), ALU.mult))
                    for lo, hi in BANKS:
                        last = nc.vector.tensor_tensor(flat[:, lo:hi], flat[:, lo:hi], psO[:, lo:hi], ALU.add)
                    ch.link(last)
                    ch.link(nc.vector.tensor_tensor(heads, heads, den[:, :, :].rearrange("p t h -> p (t h)")
                                                    .unsqueeze(2).to_broadcast([P, CT * HEADS, HID]), ALU.mult))
                    ch.link(nc.vector.tensor_tensor(H[:, :, :], H[:, :, :],
                                                    gat_b[:, :].unsqueeze(1).to_broadcast([P, CT, D]), ALU.add))
                    nc.vector.tensor_scalar_min(neg[:, :, :], H[:, :, :], 0.0).then_inc(neg_done, 1)
                    dve.wait_ge(neg_exp, c + 1)
                    ch.link(nc.vector.tensor_scalar(neg[:, :, :], neg[:, :, :], -1.0, None, ALU.add))
                    ch.link(nc.vector.scalar_tensor_tensor(out=H[:, :, :], in0=H[:, :, :], scalar=0.0, in1=neg[:, :, :],
                                                           op0=ALU.max, op1=ALU.add))
                    assert ch.n == per
                    dve.wait_ge(x_in, 16 * c + 16)
                    nc.vector.tensor_tensor(nm.X[:, :, :], nm.X[:, :, :], H[:, :, :], ALU.add).then_inc(x_done, 1)
                    dve.wait_ge(x_done, c + 1)
                    nm.vector(dve, c)
                    dve.wait_ge(mm_done, c + 2)
                    for t in range(CT):
                        last = nc.vector.tensor_tensor(H[:, t, :], psO[:, t * D:(t + 1) * D], mean_b[:, :], ALU.add)
                    last.then_inc(o_done, 1)

            @block.tensor
            def _(pe):
                pe.wait_ge(w_in, 48)
                with pe.Fori(0, CHUNKS) as c:
                    pe.wait_ge(staged, c + 1)
                    pe.wait_ge(o_done, c + 1)
                    unstage(nc, psO, stage, sh["ident"][:, :])
                    for t in range(CT):
                        last = nc.tensor.transpose(nm.psT[:, t * W2:(t + 1) * W2], stage_d[:, t * P:(t + 1) * P],
                                                   sh["ident"][0:W2, 0:W2])
                    last.then_inc(back_done, 1)
                    nm.tensor(pe, c)
                    pe.wait_ge(nm.hT_done, c + 2)
                    project(nc, psO, nm.hT, w).then_inc(mm_done, 1)


def edges_rows(nc, dram, sh, tag, table, width, acc, count=None):
    blocks = [(0, P), (P, P)] if width == D else [(0, width)]
    wide = len(blocks) * P
    rows_n = min(width, P)
    with Phase(nc, tag) as ph:
        rows = [ph.sb(f"rows{i}", [P, GT, width]) for i in range(NB)]
        idx = [ph.sb(f"idx{i}", [P, GT], I32) for i in range(NB)]
        sel = [ph.sb(f"sel{i}", [P, GT, P]) for i in range(NB)]
        psa = ph.ps("psa", 2 * GT * wide)
        psc = ph.ps("psc", 2 * GT * P)
        S = ph.sem
        gathered = [S(f"gathered{i}") for i in range(NB)]
        idx_done, sel_done = S("idx_done"), S("sel_done")
        cleared = S("cleared")
        win_done = S("win_done", NB)
        adds = 1 if count is None else 2
        added = S("added", 2 * GT * adds)

        ph.begin()
        with nc.Block() as block:

            @block.gpsimd
            def _(pool):
                with pool.Fori(0, ITERS) as it:
                    for b in range(NB):
                        g = it * NB + b
                        hold(pool, ph, win_done, g + 1)
                        gather_group(nc, pool, ph, sh, table, rows[b], idx[b], g, idx_done, gathered[b])

            @block.vector
            def _(dve):
                regs = [dve.alloc_register(f"{tag}_base{t}") for t in range(GT)]
                if count is not None:
                    nc.vector.memset(count[:, :], 0.0)
                    nc.vector.memset(acc[:, :, :], 0.0).then_inc(cleared, 1)
                    dve.wait_ge(cleared, 1)

                def select(it, b):
                    g = it * NB + b
                    dve.wait_ge(win_done, g + 1)
                    select_group(nc, sel[b], sh, g).then_inc(sel_done, 1)

                def add(it, b):
                    g = it * NB + b
                    bases = window_bases(dve, regs, sh, g)
                    dve.wait_ge(win_done, g + NB + 1)
                    for t in range(GT):
                        dve.wait_ge(added, adds * (GT * g + t + 2 * GT))
                        col = ((b % 2) * GT + t) * wide
                        if width == D:
                            a = acc[:, :, bass.ds(bases[t], P)]
                            p = psa[:, col:col + wide].rearrange("p (k r) -> p k r", k=KH)
                        else:
                            a = acc[:, bass.ds(bases[t], P)]
                            p = psa[0:rows_n, col:col + wide]
                        nc.vector.tensor_tensor(a, a, p, ALU.add).then_inc(added, 1)
                        if count is not None:
                            a = count[:, bass.ds(bases[t], P)]
                            col = ((b % 2) * GT + t) * P
                            nc.vector.tensor_tensor(a, a, psc[:, col:col + P], ALU.add).then_inc(added, 1)

                def step(it, b, first):
                    select(it, b)
                    if not first or b >= 1:
                        add(*back(it, b, 1))

                skewed(dve, step, lambda it: add(it, NB - 1))

            @block.tensor
            def _(pe):
                with pe.Fori(0, ITERS) as it:
                    for b in range(NB):
                        g = it * NB + b
                        pe.wait_ge(sel_done, g + 1)
                        pe.wait_ge(gathered[b], it * 64 + 64)
                        pe.wait_ge(added, adds * GT * (g + 1))
                        for t in range(GT):
                            for k, (f, n) in enumerate(blocks):
                                col = ((b % 2) * GT + t) * wide + k * P
                                last = nc.tensor.matmul(psa[0:n, col:col + P], rows[b][:, t, f:f + n], sel[b][:, t, :],
                                                        start=True, stop=True)
                            if count is not None:
                                col = ((b % 2) * GT + t) * P
                                last = nc.tensor.matmul(psc[:, col:col + P], sh["ones"][:, :], sel[b][:, t, :],
                                                        start=True, stop=True)
                        last.then_inc(win_done, 1)


def nodes_mean(nc, dram, sh, acc, deg, acc3):
    with Phase(nc, "n3") as ph:
        nm = Norm(ph, sh)
        w = ph.sb("w", [P, KH, H3])
        deg_c = ph.sb("deg_c", [P, NT])
        inv, dinv_c, has = ph.sb("inv", [P, NT]), ph.sb("dinv_c", [P, NT]), ph.sb("has", [P, NT])
        stage = ph.sb("stage", [P, KH, CN])
        O = ph.sb("O", [P, CT, H3])
        psO = ph.ps("psO", 2048)
        HC = CN // 2
        S = ph.sem
        w_in, deg_out, deg_in, x_in, x_stored, o_stored = (S(s) for s in (
            "w_in", "deg_out", "deg_in", "x_in", "x_stored", "o_stored"))
        staged, back_done, link, cols_done, roots, scaled, x_done = (S(s) for s in (
            "staged", "back_done", "link", "cols_done", "roots", "scaled", "x_done"))
        mm_done = S("mm_done", 1)
        o_done = S("o_done", 1)
        o_free = S("o_free", 1)

        ph.begin()
        with nc.Block() as block:

            @block.sync
            def _(sp):
                sp.dma_start(w[:, :, :], by_half(dram["gcn_w1"])).then_inc(w_in, 16)
                sp.dma_start(dram["deg_row"][:, :], deg[0:1, 0:NP]).then_inc(deg_out, 16)
                sp.wait_ge(deg_out, 16)
                with nc.allow_non_contiguous_dma(reason="one degree for each partition and node tile"):
                    sp.dma_start(deg_c[:, :], dram["deg_row"].rearrange("a (t p) -> p (a t)", p=P)).then_inc(deg_in, 16)
                with sp.Fori(0, CHUNKS) as c:
                    sp.dma_start(nm.X[:, :, :], node_rows(dram["x2"], c)).then_inc(x_in, 16)
                    hold(sp, ph, x_done, c + 1)
                    sp.dma_start(node_rows(dram["x3"], c), nm.X[:, :, :]).then_inc(x_stored, 16)
                    hold(sp, ph, x_stored, 16 * c + 16)
                    hold(sp, ph, nm.norm_done, c + 2)

            @block.gpsimd
            def _(pool):
                with pool.Fori(0, CHUNKS) as c:
                    hold(pool, ph, o_done, c + 2)
                    pool.dma_start(node_rows(dram["tab3"], c), O[:, :, :]).then_inc(o_stored, 16)
                    hold(pool, ph, o_stored, 16 * c + 16)
                    pool.sem_inc(o_free, 1)

            @block.scalar
            def _(act):
                act.wait_ge(deg_in, 16)
                act.wait_ge(deg_out, 16)
                nc.scalar.activation(dinv_c[:, :], deg_c[:, :], ACT.Sqrt, bias=sh["ones"][:, 0:1])
                nc.scalar.activation(deg[:, :], deg[:, :], ACT.Sqrt, bias=sh["ones"][:, 0:1]).then_inc(roots, 1)
                act.preload_act_table_set(EXP_LN)
                with act.Fori(0, CHUNKS) as c:
                    act.wait_ge(mm_done, c + 1)
                    stage_chunk(nc, act, [(stage[:, k, :], acc[:, k, bass.ds(c * CN, CN)]) for k in range(KH)],
                                staged, c)
                    nm.scalar_std(act, c)
                    nm.scalar_relu(act, c, mm_done, c + 1)

            @block.vector
            def _(dve):
                ch = Chain(dve, cols_done)
                dve.wait_ge(deg_in, 16)
                ch.link(nc.vector.tensor_scalar_max(inv[:, :], deg_c[:, :], 1.0))
                ch.link(nc.vector.reciprocal(inv[:, :], inv[:, :]))
                ch.link(nc.vector.tensor_scalar(has[:, :], deg_c[:, :], 0.0, None, ALU.is_gt))
                ch.link(nc.vector.tensor_tensor(inv[:, :], inv[:, :], has[:, :], ALU.mult))
                dve.wait_ge(roots, 1)
                ch.link(nc.vector.reciprocal(dinv_c[:, :], dinv_c[:, :]))
                ch.link(nc.vector.reciprocal(deg[:, :], deg[:, :]))
                ch.link(nc.vector.memset(acc3[:, NP:NW], 0.0))
                with dve.Fori(0, CHUNKS) as c:
                    dve.wait_ge(back_done, c + 1)
                    dve.wait_ge(x_in, 16 * c + 16)
                    for t in range(CT):
                        last = nc.vector.scalar_tensor_tensor(
                            out=nm.X[:, t, :], in0=psO[:, t * D:(t + 1) * D], scalar=inv[:, bass.ds(c * CT + t, 1)],
                            in1=nm.X[:, t, :], op0=ALU.mult, op1=ALU.add)
                    last.then_inc(x_done, 1)
                    dve.wait_ge(x_done, c + 1)
                    nm.vector(dve, c)
                    dve.wait_ge(mm_done, c + 2)
                    dve.wait_ge(o_free, c + 1)
                    for h in range(2):
                        col = bass.ds(c * CN + h * HC, HC)
                        nc.vector.tensor_tensor(acc3[:, col], psO[0:H3, (1 + h) * 512:(1 + h) * 512 + HC],
                                                deg[0:H3, col], ALU.mult)
                    nc.vector.tensor_tensor(O[:, :, :], psO[:, 0:CT * H3].rearrange("p (t n) -> p t n", n=H3),
                                            dinv_c[:, bass.ds(c * CT, CT)].unsqueeze(2).to_broadcast([P, CT, H3]),
                                            ALU.mult).then_inc(o_done, 1)

            @block.tensor
            def _(pe):
                pe.wait_ge(w_in, 16)
                with pe.Fori(0, CHUNKS) as c:
                    pe.wait_ge(staged, c + 1)
                    pe.wait_ge(o_done, c + 1)
                    unstage(nc, psO, stage, sh["ident"][:, :]).then_inc(back_done, 1)
                    nm.tensor(pe, c)
                    pe.wait_ge(nm.hT_done, c + 2)
                    for t in range(CT):
                        for k in range(KH):
                            nc.tensor.matmul(psO[:, t * H3:(t + 1) * H3], nm.hT[:, k, t * P:(t + 1) * P], w[:, k, :],
                                             start=(k == 0), stop=(k == KH - 1))
                    for h in range(2):
                        for k in range(KH):
                            last = nc.tensor.matmul(psO[0:H3, (1 + h) * 512:(1 + h) * 512 + HC], w[:, k, :],
                                                    nm.hT[:, k, h * HC:(h + 1) * HC], start=(k == 0), stop=(k == KH - 1))
                    last.then_inc(mm_done, 1)


FMAX = 512


def batch_norm(nc, dve, ch, acc, dinv, bias, gamma, beta, stats, mv, shift, std_in, std_out, rows):
    ch.link(nc.vector.tensor_tensor(acc[:, 0:NP], acc[:, 0:NP], dinv[0:rows, 0:NP], ALU.mult))
    ch.link(nc.vector.tensor_scalar(acc[:, 0:NP], acc[:, 0:NP], bias, None, ALU.add))
    for i, lo in enumerate(range(0, N, FMAX)):
        last = nc.vector.bn_stats(stats[:, i, :], acc[:, lo:min(lo + FMAX, N)])
    ch.link(last)
    nc.vector.bn_aggr(mv[:, :], stats[:, :, :].rearrange("p a b -> p (a b)")).then_inc(std_in, 1)
    dve.wait_ge(std_out, 1)
    ch.link(nc.vector.reciprocal(mv[:, 1:2], mv[:, 1:2]))
    ch.link(nc.vector.tensor_tensor(mv[:, 1:2], mv[:, 1:2], gamma, ALU.mult))
    ch.link(nc.vector.tensor_tensor(shift, mv[:, 0:1], mv[:, 1:2], ALU.mult))
    return nc.vector.tensor_tensor(shift, beta, shift, ALU.subtract)


def nodes_gcn(nc, dram, sh, dinv, acc3, acc4):
    with Phase(nc, "n4") as ph:
        w2 = ph.sb("w2", [H3, OC])
        par = ph.sb("par", [H3, 3])
        stats = ph.sb("stats", [H3, -(-N // FMAX), 6])
        mv, shift = ph.sb("mv", [H3, 2]), ph.sb("shift", [H3, 1])
        hid = [ph.sb(f"hid{h}", [H3, CN // 2]) for h in range(2)]
        ps = ph.ps("ps", 1024)
        HC = CN // 2
        S = ph.sem
        w_in, link, mv_done, std_done, shift_done, h_done, stored = (S(s) for s in (
            "w_in", "link", "mv_done", "std_done", "shift_done", "h_done", "stored"))
        mm_done = S("mm_done", 2)
        o_done = S("o_done", 2)

        ph.begin()
        with nc.Block() as block:

            @block.sync
            def _(sp):
                sp.dma_start(w2[:, :], dram["gcn_w2"][:, :]).then_inc(w_in, 16)
                for j, name in enumerate(("gcn_b1", "gcn_g1", "gcn_be1")):
                    sp.dma_start(par[:, j:j + 1], dram[name].rearrange("(p a) -> p a", a=1)).then_inc(w_in, 16)
                sp.wait_ge(o_done, 2 + 2 * CHUNKS)
                with nc.allow_non_contiguous_dma(reason="12544 values of the two-column table"):
                    sp.dma_start(dram["tab4"].rearrange("n c -> c n"), acc4[:, 0:NP]).then_inc(stored, 16)
                sp.wait_ge(stored, 16)

            @block.scalar
            def _(act):
                act.wait_ge(mv_done, 1)
                nc.scalar.activation(mv[:, 1:2], mv[:, 1:2], ACT.Sqrt, bias=sh["eps"][0:H3, 0:1]).then_inc(std_done, 1)
                act.wait_ge(shift_done, 1)
                with act.Fori(0, CHUNKS) as c:
                    for h in range(2):
                        act.wait_ge(mm_done, c * 2 + h + 1)
                        nc.scalar.activation(hid[h][:, :], acc3[:, bass.ds(c * CN + h * HC, HC)], ACT.Relu,
                                             bias=shift[:, 0:1], scale=mv[:, 1:2]).then_inc(h_done, 1)

            @block.vector
            def _(dve):
                ch = Chain(dve, link)
                dve.wait_ge(w_in, 64)
                ch.link(nc.vector.memset(acc4[:, NP:NW], 0.0))
                batch_norm(nc, dve, ch, acc3, dinv, par[:, 0:1], par[:, 1:2], par[:, 2:3], stats, mv, shift[:, :],
                           mv_done, std_done, H3).then_inc(shift_done, 1)
                with dve.Fori(0, CHUNKS) as c:
                    for h in range(2):
                        dve.wait_ge(mm_done, c * 2 + h + 3)
                        col = bass.ds(c * CN + h * HC, HC)
                        nc.vector.tensor_tensor(acc4[:, col], ps[0:OC, h * 512:h * 512 + HC], dinv[0:OC, col],
                                                ALU.mult).then_inc(o_done, 1)

            @block.tensor
            def _(pe):
                pe.wait_ge(w_in, 64)
                with pe.Fori(0, CHUNKS) as c:
                    for h in range(2):
                        hold(pe, ph, h_done, c * 2 + h + 1)
                        hold(pe, ph, o_done, c * 2 + h + 1)
                        nc.tensor.matmul(ps[0:OC, h * 512:h * 512 + HC], w2[:, :], hid[h][:, :],
                                         start=True, stop=True).then_inc(mm_done, 1)


def nodes_out(nc, dram, sh, dinv, acc4):
    with Phase(nc, "n5") as ph:
        wd = ph.sb("wd", [OC, D])
        par = ph.sb("par", [OC, 3])
        bd = ph.sb("bd", [P, D])
        stats = ph.sb("stats", [OC, -(-N // FMAX), 6])
        mv, shift = ph.sb("mv", [OC, 2]), ph.sb("shift", [OC, 1])
        z = ph.sb("z", [OC, CN])
        X = ph.sb("X", [P, CT, D])
        ps = ph.ps("ps", 2048)
        S = ph.sem
        w_in, link, mv_done, std_done, shift_done, z_done, x_in, stored = (S(s) for s in (
            "w_in", "link", "mv_done", "std_done", "shift_done", "z_done", "x_in", "stored"))
        biased, mm_done = S("biased"), S("mm_done", 1)
        x_done = S("x_done", 1)

        ph.begin()
        with nc.Block() as block:

            @block.sync
            def _(sp):
                sp.dma_start(wd[:, :], dram["gcn_wd"][:, :]).then_inc(w_in, 16)
                sp.dma_start(bd[:, :], on_all(dram["gcn_bd"], D)).then_inc(w_in, 16)
                for j, name in enumerate(("gcn_b2", "gcn_g2", "gcn_be2")):
                    sp.dma_start(par[:, j:j + 1], dram[name].rearrange("(p a) -> p a", a=1)).then_inc(w_in, 16)
                with sp.Fori(0, CHUNKS) as c:
                    sp.dma_start(X[:, :, :], node_rows(dram["x3"], c)).then_inc(x_in, 16)
                    hold(sp, ph, x_done, c + 2)
                    sp.dma_start(node_rows(dram["out"], c), X[:, :, :]).then_inc(stored, 16)
                    hold(sp, ph, stored, 16 * c + 16)

            @block.scalar
            def _(act):
                act.wait_ge(mv_done, 1)
                nc.scalar.activation(mv[:, 1:2], mv[:, 1:2], ACT.Sqrt, bias=sh["eps"][0:OC, 0:1]).then_inc(std_done, 1)
                act.wait_ge(shift_done, 1)
                with act.Fori(0, CHUNKS) as c:
                    act.wait_ge(mm_done, c + 1)
                    nc.scalar.activation(z[:, :], acc4[:, bass.ds(c * CN, CN)], ACT.Identity, bias=shift[:, 0:1],
                                         scale=mv[:, 1:2]).then_inc(z_done, 1)

            @block.vector
            def _(dve):
                ch = Chain(dve, link)
                dve.wait_ge(w_in, 80)
                batch_norm(nc, dve, ch, acc4, dinv, par[:, 0:1], par[:, 1:2], par[:, 2:3], stats, mv, shift[:, :],
                           mv_done, std_done, OC).then_inc(shift_done, 1)
                with dve.Fori(0, CHUNKS) as c:
                    dve.wait_ge(x_in, 16 * c + 16)
                    nc.vector.tensor_tensor(X[:, :, :], X[:, :, :], bd[:, :].unsqueeze(1).to_broadcast([P, CT, D]),
                                            ALU.add).then_inc(biased, 1)
                    dve.wait_ge(biased, c + 1)
                    dve.wait_ge(mm_done, c + 2)
                    flat = X[:, :, :].rearrange("p t n -> p (t n)")
                    for lo, hi in BANKS:
                        last = nc.vector.tensor_tensor(flat[:, lo:hi], flat[:, lo:hi], ps[:, lo:hi], ALU.add)
                    last.then_inc(x_done, 1)

            @block.tensor
            def _(pe):
                pe.wait_ge(w_in, 80)
                with pe.Fori(0, CHUNKS) as c:
                    pe.wait_ge(z_done, c + 1)
                    pe.wait_ge(x_done, c + 1)
                    for t in range(CT):
                        last = nc.tensor.matmul(ps[:, t * D:(t + 1) * D], z[:, t * P:(t + 1) * P], wd[:, :],
                                                start=True, stop=True)
                    last.then_inc(mm_done, 1)



def bass_gnn_stack(nc, dram):
    with ExitStack() as ctx:
        def keep(name, shape, dtype=F32):
            return ctx.enter_context(nc.sbuf_tensor(name, shape, dtype))

        sh = {"ident": keep("ident", [P, P]), "iota": keep("iota", [P, P]), "ones": keep("ones", [P, P]),
              "eps": keep("eps", [P, 1]), "src_sb": keep("src_sb", [P, TILES], I32),
              "dst_sb": keep("dst_sb", [P, TILES], I32), "rel": keep("rel", [P, TILES])}
        constants(nc, dram, sh)
        embed0(nc, dram, sh)
        with nc.sbuf_tensor("acc0", [P, KH, NW], F32) as acc:
            edges_schnet(nc, dram, sh, acc)
            nodes_schnet(nc, dram, sh, acc)
        with nc.sbuf_tensor("a_src", [P, TILES * HEADS], F32) as a_src, \
                nc.sbuf_tensor("seg_max", [P, TILES * HEADS], F32) as seg_max:
            edges_max(nc, dram, sh, a_src, seg_max)
            with nc.sbuf_tensor("acc1", [P, KH, NW], F32) as acc, nc.sbuf_tensor("acc_d", [2 * HEADS, NW], F32) as acc_d:
                edges_gat(nc, dram, sh, a_src, seg_max, acc, acc_d)
                nodes_gat(nc, dram, sh, acc, acc_d)
        with nc.sbuf_tensor("deg", [P, NW], F32) as deg, nc.sbuf_tensor("acc3", [H3, NW], F32) as acc3:
            with nc.sbuf_tensor("acc2", [P, KH, NW], F32) as acc:
                edges_rows(nc, dram, sh, "l2", dram["tab2"], D, acc, deg)
                nodes_mean(nc, dram, sh, acc, deg, acc3)
            edges_rows(nc, dram, sh, "l3", dram["tab3"], H3, acc3)
            with nc.sbuf_tensor("acc4", [OC, NW], F32) as acc4:
                nodes_gcn(nc, dram, sh, deg, acc3, acc4)
                edges_rows(nc, dram, sh, "l4", dram["tab4"], OC, acc4)
                nodes_out(nc, dram, sh, deg, acc4)


def layout(i):
    import numpy as np

    def padded(a, rows, value=0):
        out = np.full((rows, *a.shape[1:]), value, a.dtype)
        out[:a.shape[0]] = a
        return out

    def cols(a):
        return np.ascontiguousarray(a.reshape(TILES, P).T)

    a = {k: np.asarray(v) for k, v in i.items()}
    src = padded(a["src"], TILES * P)
    dst = padded(a["dst"], TILES * P, PAD_DST)
    flat = np.concatenate([np.full(1, -1, dst.dtype), dst, np.full(1, -1, dst.dtype)])
    edge = padded(a["edge_attr_64"], TILES * P).reshape(GROUPS // 2, 2, GT * P, NG).transpose(0, 1, 3, 2)
    d = {
        "x": padded(a["x"], NP), "src_cols": cols(src), "dst_cols": cols(dst), "prev_cols": cols(flat[:-2]), "next_cols": cols(flat[2:]),
        "ew_cols": cols(padded(a["edge_weight"], TILES * P)),
        "edge_t": edge.reshape(GROUPS // 2, P, GT * P),
        "fw1_t": a["L0_gnn_fw1"].T, "fb1": a["L0_gnn_fb1"].reshape(KH, P).T, "fw2_t": a["L0_gnn_fw2"].T, "fb2": a["L0_gnn_fb2"],
        "w1_t": a["L0_gnn_w1"].T, "w2_t": a["L0_gnn_w2"].T, "b2": a["L0_gnn_b2"].reshape(KH, P).T,
        "w3_t": a["L0_gnn_w3"].T, "b3": a["L0_gnn_b3"],
        "gat_w": a["L1_gnn_W0"], "gat_w_t": a["L1_gnn_W0"].T, "att_src": a["L1_gnn_att_src0"].reshape(D),
        "att_dst": a["L1_gnn_att_dst0"].reshape(D), "gat_b": a["L1_gnn_b0"],
        "mean_w": a["L2_gnn_W"], "mean_b": a["L2_gnn_b"],
        "gcn_w1": a["L3_gnn_W1"], "gcn_b1": a["L3_gnn_b1"], "gcn_g1": a["L3_gnn_g1"], "gcn_be1": a["L3_gnn_be1"],
        "gcn_w2": a["L3_gnn_W2"], "gcn_b2": a["L3_gnn_b2"], "gcn_g2": a["L3_gnn_g2"], "gcn_be2": a["L3_gnn_be2"],
        "gcn_wd": a["L3_gnn_Wd"], "gcn_bd": a["L3_gnn_bd"],
    }
    return {k: np.ascontiguousarray(v) for k, v in d.items()}


def kernel(**inputs):
    import concourse.bacc as bacc
    from concourse.bass_utils import run_bass_kernel_spmd

    nc = bacc.Bacc("TRN2", target_bir_lowering=False, num_devices=1)
    arrays = layout(inputs)
    dram = {}
    for name, (shape, dtype) in INPUTS.items():
        dram[name] = nc.dram_tensor(f"in_{name}", shape, dtype, kind="ExternalInput").ap()
    for name, shape in SCRATCH.items():
        dram[name] = nc.dram_tensor(f"tmp_{name}", shape, F32).ap()
    dram["out"] = nc.dram_tensor("out", [NP, D], F32, kind="ExternalOutput").ap()
    bass_gnn_stack(nc, dram)
    r = run_bass_kernel_spmd(nc, [{f"in_{k}": v for k, v in arrays.items()}], core_ids=[0])
    return r.results[0]["out"][:N]
```

```python
from contextlib import ExitStack, contextmanager

import concourse.bass as bass
from concourse import mybir

F32 = mybir.dt.float32
I32 = mybir.dt.int32
U32 = mybir.dt.uint32
ALU = mybir.AluOpType
ACT = mybir.ActivationFunctionType
AX = mybir.AxisListType

P = 128
N = 6250
E = 106250
D = 256
KH = D // P
TILES = 832
GT = 4
GROUPS = TILES // GT
NB = 4
ITERS = GROUPS // NB
CT = 4
CN = CT * P
CHUNKS = 13
NT = CHUNKS * CT
NP = CHUNKS * CN
PEEL = 5
PAD_DST = 6300
NW = NP
HEADS = 8
HID = D // HEADS
NG = 64
H3 = 64
OC = 2
BIG = 1.0e38
EPS = 1e-5
HALF_PI = 1.5707963267948966
PI = 3.141592653589793
LN2 = 0.6931471805599453
EXP_LN = "natural_log_exp_and_others"
EXP_CAP = float(2 ** 60)
SEG = GT * NB
BANKS = ((0, 512), (512, 1024))

INPUTS = {
    "x": ([NP, D], F32), "src_cols": ([P, TILES], I32), "dst_cols": ([P, TILES], I32),
    "prev_cols": ([P, TILES], I32), "next_cols": ([P, TILES], I32), "ew_cols": ([P, TILES], F32),
    "edge_t": ([GROUPS // 2, P, GT * P], F32),
    "fw1_t": ([NG, D], F32), "fb1": ([P, KH], F32), "fw2_t": ([D, D], F32), "fb2": ([D], F32),
    "w1_t": ([D, D], F32), "w2_t": ([D, D], F32), "b2": ([P, KH], F32), "w3_t": ([D, D], F32), "b3": ([D], F32),
    "gat_w": ([D, D], F32), "gat_w_t": ([D, D], F32), "att_src": ([D], F32), "att_dst": ([D], F32),
    "gat_b": ([D], F32), "mean_w": ([D, D], F32), "mean_b": ([D], F32),
    "gcn_w1": ([D, H3], F32), "gcn_b1": ([H3], F32), "gcn_g1": ([H3], F32), "gcn_be1": ([H3], F32),
    "gcn_w2": ([H3, OC], F32), "gcn_b2": ([OC], F32), "gcn_g2": ([OC], F32), "gcn_be2": ([OC], F32),
    "gcn_wd": ([OC, D], F32), "gcn_bd": ([D], F32),
}
SCRATCH = {
    "tab0": [NP, D], "x1": [NP, D], "tab1": [NP, D], "tab_as": [NP, HEADS], "att_tab": [NW, 2 * HEADS],
    "x2": [NP, D], "tab2": [NP, D], "x3": [NP, D], "tab3": [NP, H3], 
    "deg_row": [1, NP], "carry": [2, HEADS, TILES],
}


class Chain:

    def __init__(self, eng, sem, base=0):
        self.eng, self.sem, self.base, self.n = eng, sem, base, 0

    def link(self, instruction):
        instruction.then_inc(self.sem, 1)
        self.n += 1
        self.eng.wait_ge(self.sem, self.base + self.n)


def hold(eng, ph, sem, value):
    eng.wait_ge(sem, value)
    eng.sem_inc(ph.seen, 1)


class Phase:

    def __init__(self, nc, tag):
        self.nc, self.tag, self.stack, self.sems, self.free = nc, tag, ExitStack(), [], []
        self.seen = self.sem("seen")

    def __enter__(self):
        return self

    def __exit__(self, *_):
        self.stack.close()
        self.nc.clear_and_free_semaphores(self.sems)
        self.nc.all_engine_barrier()

    def sb(self, name, shape, dtype=F32):
        return self.stack.enter_context(self.nc.sbuf_tensor(f"{self.tag}_{name}", shape, dtype))

    def ps(self, name, cols, rows=P):
        return self.stack.enter_context(self.nc.psum_tensor(f"{self.tag}_{name}", [rows, cols], F32))

    def sem(self, name, free=0):
        s = self.nc.alloc_semaphore(f"{self.tag}_{name}")
        self.sems.append(s)
        if free:
            self.free.append((s, free))
        return s

    def begin(self):
        for s, free in self.free:
            self.nc.gpsimd.sem_inc(s, free)
        if self.free:
            self.nc.all_engine_barrier()


def by_half(ap):
    return ap.rearrange("(k p) n -> p k n", p=P)


def on_all(ap, n, rows=P):
    return ap.rearrange("(a n) -> a n", a=1).broadcast_to([rows, n])


def node_rows(ap, c):
    return ap[bass.ds(c * CN, CN), :].rearrange("(t p) n -> p t n", p=P)


class Chunk:

    def __init__(self, base, pairs=None):
        self.p = base % 2
        self.n = base if pairs is None else pairs * 2 + base
        self.k = base // 2 if pairs is None else pairs + base // 2


def staggered(eng, step, lag, count=CHUNKS, peel=PEEL):
    def outside(s):
        step(lambda j: Chunk(s - j) if 0 <= s - j < count else None)

    for s in range(peel):
        outside(s)
    with eng.Fori(0, (count - peel) // 2) as pairs:
        for q in range(2):
            step(lambda j: Chunk(peel + q - j, pairs))
    for s in range(count, count + lag):
        outside(s)


class Norm:

    def __init__(self, ph, shared):
        self.ph, self.nc, self.shared = ph, ph.nc, shared
        pair = lambda name, shape: [ph.sb(f"{name}{p}", shape) for p in range(2)]
        self.X = pair("X", [P, CT, D])
        self.norm = pair("norm", [P, CT, D])
        self.hT = pair("hT", [P, KH, CN])
        self.stats = pair("stats", [P, CT, 6])
        self.mv = pair("mv", [P, CT, 2])
        self.std = pair("std", [P, CT])
        self.rstd = pair("rstd", [P, CT])
        psT = ph.ps("psT", 2 * CT * D)
        self.psT = [psT[:, p * CT * D:(p + 1) * CT * D] for p in range(2)]
        self.stats_done = ph.sem("stats_done")
        self.mv_done = ph.sem("mv_done")
        self.log_done = ph.sem("log_done")
        self.std_done = ph.sem("std_done")
        self.norm_done = ph.sem("norm_done", 2)
        self.xT_done = ph.sem("xT_done", 2)
        self.hT_done = ph.sem("hT_done", 2)

    def statistics(self, dve, c):
        nc = self.nc
        for t in range(CT):
            last = nc.vector.bn_stats(self.stats[c.p][:, t, :], self.X[c.p][:, t, :])
        last.then_inc(self.stats_done, 1)
        hold(dve, self.ph, self.stats_done, c.n + 1)
        for t in range(CT):
            last = nc.vector.bn_aggr(self.mv[c.p][:, t, :], self.stats[c.p][:, t, :])
        last.then_inc(self.mv_done, 1)

    def normalize(self, dve, c):
        dve.wait_ge(self.std_done, c.n + 1)
        dve.wait_ge(self.xT_done, c.n + 1)
        for t in range(CT):
            last = self.nc.vector.tensor_scalar(self.norm[c.p][:, t, :], self.X[c.p][:, t, :], self.mv[c.p][:, t, 0:1],
                                                self.rstd[c.p][:, t:t + 1], ALU.subtract, ALU.mult)
        last.then_inc(self.norm_done, 1)

    def deviations(self, act, c):
        act.wait_ge(self.mv_done, c.n + 1)
        self.nc.scalar.activation(self.std[c.p][:, :], self.mv[c.p][:, :, 1], ACT.Ln,
                                  bias=self.shared["eps"][:, 0:1]).then_inc(self.log_done, 1)
        act.wait_ge(self.log_done, c.n + 1)
        act.wait_ge(self.norm_done, c.n + 1)
        self.nc.scalar.activation(self.rstd[c.p][:, :], self.std[c.p][:, :], ACT.Exp,
                                  scale=-0.5).then_inc(self.std_done, 1)

    def relu(self, act, c, used):
        act.wait_ge(self.xT_done, c.n + 3)
        act.wait_ge(used, c.n + 1)
        flat = self.hT[c.p][:, :, :].rearrange("p k n -> p (k n)")
        for lo, hi in BANKS:
            last = self.nc.scalar.activation(flat[:, lo:hi], self.psT[c.p][:, lo:hi], ACT.Relu)
        last.then_inc(self.hT_done, 1)

    def transpose(self, pe, c):
        pe.wait_ge(self.norm_done, c.n + 3)
        pe.wait_ge(self.hT_done, c.n + 1)
        for k in range(KH):
            for t in range(CT):
                j = k * CT + t
                last = self.nc.tensor.transpose(self.psT[c.p][:, j * P:(j + 1) * P],
                                                self.norm[c.p][:, t, k * P:(k + 1) * P], self.shared["ident"][:, :])
        last.then_inc(self.xT_done, 1)


def pair_of(ph, name, shape):
    return [ph.sb(f"{name}{p}", shape) for p in range(2)]


def psum_pair(ph, name):
    ps = ph.ps(name, 2 * CT * D)
    return [ps[:, p * CT * D:(p + 1) * CT * D] for p in range(2)]


def wait_stored(eng, ph, stored, c, each=16):
    if not (isinstance(c.k, int) and c.k == 0):
        hold(eng, ph, stored[c.p], c.k * each)


def copy_out(nc, act, ph, O, psO, c, mm_done, stored, o_done):
    act.wait_ge(mm_done, c.n + 3)
    wait_stored(act, ph, stored, c)
    flat = O[c.p][:, :, :].rearrange("p t n -> p (t n)")
    for lo, hi in BANKS:
        last = nc.scalar.activation(flat[:, lo:hi], psO[c.p][:, lo:hi], ACT.Copy)
    last.then_inc(o_done, 1)


def store_out(nc, pool, ph, O, table, c, o_done, stored):
    hold(pool, ph, o_done, c.n + 3)
    pool.dma_start(node_rows(table, c.n), O[c.p][:, :, :]).then_inc(stored[c.p], 16)


def all_stored(pool, stored, each=16):
    for p in range(2):
        pool.wait_ge(stored[p], each * ((CHUNKS + 1 - p) // 2))


def project(nc, out, hT, w):
    for t in range(CT):
        for k in range(KH):
            last = nc.tensor.matmul(out[:, t * D:(t + 1) * D], hT[:, k, t * P:(t + 1) * P], w[:, k, :],
                                    start=(k == 0), stop=(k == KH - 1))
    return last


def constants(nc, dram, sh):
    with Phase(nc, "const") as ph:
        iota_i = ph.sb("iota_i", [P, P], I32)
        base_b = ph.sb("base_b", [P, TILES], I32)
        loaded, zeroed, made = ph.sem("loaded"), ph.sem("zeroed"), ph.sem("made")
        rel_done = ph.sem("rel_done")
        ph.begin()
        with nc.Block() as block:

            @block.sync
            def _(sp):
                sp.dma_start(sh["src_sb"][:, :], dram["src_cols"][:, :]).then_inc(loaded, 16)
                sp.dma_start(sh["dst_sb"][:, :], dram["dst_cols"][:, :]).then_inc(loaded, 16)
                sp.dma_start(base_b[:, :], dram["dst_cols"][0:1, :].broadcast_to([P, TILES])).then_inc(loaded, 16)
                sp.wait_ge(loaded, 48)

            @block.gpsimd
            def _(pool):
                nc.gpsimd.iota(iota_i[:, :], [[1, P]], base=0, channel_multiplier=0).then_inc(made, 1)
                nc.gpsimd.memset(sh["ident"][:, :], 0.0).then_inc(zeroed, 1)
                pool.wait_ge(zeroed, 1)
                nc.gpsimd.affine_select(out=sh["ident"][:, :], in_=sh["ident"][:, :],
                                        compare_op=ALU.not_equal, fill=1.0, base=0,
                                        pattern=[[-1, P]], channel_multiplier=1).then_inc(zeroed, 1)
                pool.wait_ge(zeroed, 2)

            @block.vector
            def _(dve):
                nc.vector.memset(sh["ones"][:, :], 1.0)
                nc.vector.memset(sh["eps"][:, :], EPS)
                dve.wait_ge(made, 1)
                nc.vector.tensor_copy(sh["iota"][:, :], iota_i[:, :])
                dve.wait_ge(loaded, 48)
                nc.vector.tensor_tensor(sh["rel"][:, :], sh["dst_sb"][:, :], base_b[:, :],
                                        ALU.subtract).then_inc(rel_done, 1)
                dve.wait_ge(rel_done, 1)


def embed0(nc, dram, sh):
    with Phase(nc, "n0") as ph:
        nm = Norm(ph, sh)
        w = ph.sb("w", [P, KH, D])
        O = pair_of(ph, "O", [P, CT, D])
        psO = psum_pair(ph, "psO")
        w_in = ph.sem("w_in")
        x_in = [ph.sem(f"x_in{p}") for p in range(2)]
        stored = [ph.sem(f"stored{p}") for p in range(2)]
        mm_done = ph.sem("mm_done", 2)
        o_done = ph.sem("o_done", 2)
        ph.begin()
        with nc.Block() as block:

            @block.sync
            def _(sp):
                sp.dma_start(w[:, :, :], by_half(dram["w1_t"])).then_inc(w_in, 16)

                def step(at):
                    c = at(0)
                    hold(sp, ph, nm.norm_done, c.n + 1)
                    sp.dma_start(nm.X[c.p][:, :, :], node_rows(dram["x"], c.n)).then_inc(x_in[c.p], 16)

                staggered(sp, step, 0)

            @block.gpsimd
            def _(pool):
                staggered(pool, lambda at: store_out(nc, pool, ph, O, dram["tab0"], at(0), o_done, stored), 0)
                all_stored(pool, stored)

            @block.vector
            def _(dve):
                def step(at):
                    if at(0):
                        dve.wait_ge(x_in[at(0).p], at(0).k * 16 + 16)
                        nm.statistics(dve, at(0))
                    if at(1):
                        nm.normalize(dve, at(1))

                staggered(dve, step, 1)

            @block.scalar
            def _(act):
                act.preload_act_table_set(EXP_LN)

                def step(at):
                    if at(0):
                        nm.deviations(act, at(0))
                    if at(2):
                        copy_out(nc, act, ph, O, psO, at(2), mm_done, stored, o_done)
                    if at(1):
                        nm.relu(act, at(1), mm_done)

                staggered(act, step, 2)

            @block.tensor
            def _(pe):
                pe.wait_ge(w_in, 16)

                def step(at):
                    if at(0):
                        nm.transpose(pe, at(0))
                    if at(1):
                        c = at(1)
                        pe.wait_ge(nm.hT_done, c.n + 3)
                        pe.wait_ge(o_done, c.n + 1)
                        project(nc, psO[c.p], nm.hT[c.p], w).then_inc(mm_done, 1)

                staggered(pe, step, 1)


def gather_all(nc, pool, ph, sh, table, rows, idx, used, per, idx_done, gathered):
    with pool.Fori(0, ITERS // 2) as pair:
        for q in range(2):
            it = pair * 2 + q
            nc.gpsimd.tensor_copy(idx[q][:, :], sh["src_sb"][:, bass.ds(it * SEG, SEG)]).then_inc(idx_done, 1)
            hold(pool, ph, idx_done, it + 1)
            for b in range(NB):
                hold(pool, ph, used, (it * NB + b) * per + per)
                for t in range(GT):
                    j = b * GT + t
                    nc.gpsimd.indirect_dma_start(
                        out=rows[b][:, t, :], out_offset=None, in_=table[:, :],
                        in_offset=bass.IndirectOffsetOnAxis(ap=idx[q][:, j:j + 1].bitcast(U32), axis=0),
                    ).then_inc(gathered[b], 16)


def select_group(nc, sel, sh, g, coef=None):
    for t in range(GT):
        col = sh["rel"][:, bass.ds(g * GT + t, 1)]
        if coef is None:
            last = nc.vector.tensor_scalar(sel[:, t, :], sh["iota"][:, :], col, None, ALU.is_equal)
        else:
            last = nc.vector.tensor_scalar(sel[:, t, :], sh["iota"][:, :], col,
                                           coef[:, bass.ds(g * GT + t, 1)], ALU.is_equal, ALU.mult)
    return last


def window_bases(eng, regs, sh, g):
    eng.load(regs, sh["dst_sb"][0:1, bass.ds(g * GT, GT)])
    return [eng.snap(r, min_val=0, max_val=PAD_DST) for r in regs]


class WindowBases:

    def __init__(self, eng, sh, tag, lag):
        self.eng, self.sh, self.lag, self.body = eng, sh, lag, None
        self.regs = [eng.alloc_register(f"{tag}_base{t}") for t in range(NB * GT)]

    def step(self, it, b, first):
        if first:
            return None if b < self.lag else self.group(b - self.lag)
        if b == 0:
            self.body = self.load(it * (NB * GT) - self.lag * GT, NB * GT)
        return self.body[b * GT:(b + 1) * GT]

    def group(self, g):
        return self.load(g * GT, GT)

    def load(self, tile, n):
        self.eng.load(self.regs[:n], self.sh["dst_sb"][0:1, bass.ds(tile, n)])
        return [self.eng.snap(r, min_val=0, max_val=PAD_DST) for r in self.regs[:n]]


def back(it, b, n):
    return (it, b - n) if b >= n else (it - 1, b - n + NB)


def skewed(eng, step, tail):
    for b in range(NB):
        step(0, b, True)
    with eng.Fori(1, ITERS) as it:
        for b in range(NB):
            step(it, b, False)
    tail(ITERS - 1)


def edges_schnet(nc, dram, sh, acc):
    with Phase(nc, "l0") as ph:
        edge = [ph.sb(f"edge{i}", [P, GT * P]) for i in range(2)]
        fw1 = ph.sb("fw1", [P, D])
        fw2 = ph.sb("fw2", [P, KH, D])
        fb1 = ph.sb("fb1", [P, KH])
        fb2 = ph.sb("fb2", [P, D])
        cut = ph.sb("cut", [P, TILES])
        cut_i = ph.sb("cut_i", [P, TILES], I32)
        cut_f = ph.sb("cut_f", [P, TILES])
        half_pi = ph.sb("half_pi", [P, 1])
        rows = [ph.sb(f"rows{i}", [P, GT, D]) for i in range(NB)]
        idx = [ph.sb(f"idx{i}", [P, SEG], I32) for i in range(2)]
        sel = [ph.sb(f"sel{i}", [P, GT, P]) for i in range(NB)]
        ex = ph.sb("ex", [P, KH, GT * P])
        ssp = [ph.sb(f"ssp{i}", [P, KH, GT * P]) for i in range(2)]
        msg = [ph.sb(f"msg{i}", [P, GT, D]) for i in range(2)]
        psz = ph.ps("psz", 2 * KH * 512)
        psw = ph.ps("psw", 1024)
        psa = ph.ps("psa", 1024)
        S = ph.sem
        w_in, cut_sem, setup, bias_mm = S("w_in"), S("cut"), S("setup"), S("bias_mm")
        edge_in = [S("edge_in0"), S("edge_in1")]
        gathered = [S(f"gathered{i}") for i in range(NB)]
        idx_done = S("idx_done")
        z_done = S("z_done", 1)
        exp_done, cap_done = S("exp_done"), S("cap_done")
        ln_done = S("ln_done", 1)
        ssp_done = S("ssp_done", 2)
        w_done = S("w_done", 4)
        biased = S("biased")
        msg_done = S("msg_done", 2 * NB)
        sel_done = S("sel_done")
        win_done = S("win_done", 2 * NB)
        added = S("added", GT)

        ph.begin()
        with nc.Block() as block:

            @block.sync
            def _(sp):
                for k in range(2):
                    sp.dma_start(fw1[k * NG:(k + 1) * NG, :], dram["fw1_t"][:, :]).then_inc(w_in, 16)
                sp.dma_start(fw2[:, :, :], by_half(dram["fw2_t"])).then_inc(w_in, 16)
                sp.dma_start(fb1[:, :], dram["fb1"][:, :]).then_inc(w_in, 16)
                sp.dma_start(fb2[:, :], on_all(dram["fb2"], D)).then_inc(w_in, 16)
                sp.dma_start(cut[:, :], dram["ew_cols"][:, :]).then_inc(w_in, 16)
                with sp.Fori(0, ITERS) as it:
                    for q in range(2):
                        hold(sp, ph, z_done, it * NB + 2 * q + 1)
                        sp.dma_start(edge[q][:, :], dram["edge_t"][bass.ds(it * 2 + q, 1), :, :]
                                     .rearrange("a p n -> (a p) n")).then_inc(edge_in[q], 16)

            @block.gpsimd
            def _(pool):
                gather_all(nc, pool, ph, sh, dram["tab0"], rows, idx, msg_done, 2, idx_done, gathered)

            @block.scalar
            def _(act):
                act.wait_ge(setup, 1)
                nc.scalar.activation(cut[:, :], cut_f[:, :], ACT.Sin, scale=-PI,
                                     bias=half_pi[:, 0:1]).then_inc(setup, 1)
                act.preload_act_table_set(EXP_LN)
                with act.Fori(0, ITERS) as it:
                    for b in range(NB):
                        g = it * NB + b
                        z = (b % 2) * KH * 512
                        act.wait_ge(z_done, g + 2)
                        act.wait_ge(ln_done, g + 1)
                        for k in range(KH):
                            last = nc.scalar.activation(ex[:, k, :], psz[:, z + k * 512:z + (k + 1) * 512], ACT.Exp,
                                                        bias=fb1[:, k:k + 1])
                        last.then_inc(exp_done, 1)
                        act.wait_ge(cap_done, g + 1)
                        act.wait_ge(w_done, 2 * g + 2)
                        nc.scalar.activation(ssp[b % 2][:, :, :], ex[:, :, :], ACT.Ln, bias=1.0).then_inc(ln_done, 1)

            @block.vector
            def _(dve):
                bases_of = WindowBases(dve, sh, "l0", 3)
                ch = Chain(dve, cut_sem)
                ch.link(nc.vector.memset(acc[:, :, :], 0.0))
                dve.wait_ge(w_in, 96)
                ch.link(nc.vector.tensor_scalar(cut_f[:, :], cut[:, :], 0.5, None, ALU.mult))
                ch.link(nc.vector.tensor_copy(cut_i[:, :], cut_f[:, :]))
                ch.link(nc.vector.tensor_copy(cut_f[:, :], cut_i[:, :]))
                ch.link(nc.vector.scalar_tensor_tensor(out=cut[:, :], in0=cut_f[:, :], scalar=-2.0, in1=cut[:, :],
                                                       op0=ALU.mult, op1=ALU.add))
                ch.link(nc.vector.memset(half_pi[:, :], HALF_PI))
                nc.vector.scalar_tensor_tensor(out=cut_f[:, :], in0=cut[:, :], scalar=-1.0, in1=cut[:, :],
                                               op0=ALU.mult, op1=ALU.max).then_inc(setup, 1)
                dve.wait_ge(setup, 2)
                ch.link(nc.vector.tensor_scalar(cut[:, :], cut[:, :], 0.25, 0.25, ALU.mult, ALU.add))
                dve.wait_ge(bias_mm, 1)
                nc.vector.scalar_tensor_tensor(out=fb2[:, :], in0=psw[:, 0:D], scalar=-LN2, in1=fb2[:, :],
                                               op0=ALU.mult, op1=ALU.add).then_inc(biased, 2)
                dve.wait_ge(biased, 2)

                def select(it, b, t):
                    g = it * NB + b
                    if t == 0:
                        dve.wait_ge(win_done, 2 * g + 2)
                    ins = nc.vector.tensor_scalar(sel[b][:, t, :], sh["iota"][:, :], sh["rel"][:, bass.ds(g * GT + t, 1)],
                                                  cut[:, bass.ds(g * GT + t, 1)], ALU.is_equal, ALU.mult)
                    if t == GT - 1:
                        ins.then_inc(sel_done, 1)

                def bias(it, b, h):
                    g = it * NB + b
                    dve.wait_ge(w_done, 2 * g + h + 5)
                    if h == 0:
                        dve.wait_ge(win_done, 2 * g + 6)
                    nc.vector.tensor_tensor(msg[b % 2][:, 2 * h:2 * h + 2, :],
                                            psw[:, h * 512:(h + 1) * 512].rearrange("p (t n) -> p t n", n=D),
                                            fb2[:, :].unsqueeze(1).to_broadcast([P, 2, D]), ALU.add).then_inc(biased, 1)

                def message(it, b, h):
                    g = it * NB + b
                    if h == 0:
                        dve.wait_ge(gathered[b], it * 64 + 64)
                    m = msg[b % 2][:, 2 * h:2 * h + 2, :]
                    dve.wait_ge(biased, 2 * g + h + 3)
                    nc.vector.tensor_tensor(m, m, rows[b][:, 2 * h:2 * h + 2, :], ALU.mult).then_inc(msg_done, 1)

                def add(it, b, bases, t):
                    g = it * NB + b
                    if t % 2 == 0:
                        dve.wait_ge(win_done, 2 * g + t // 2 + 2 * NB + 1)
                    dve.wait_ge(added, GT * g + t + GT)
                    a = acc[:, :, bass.ds(bases[t], P)]
                    nc.vector.tensor_tensor(a, a, psa[:, t * D:(t + 1) * D].rearrange("p (k r) -> p k r", k=KH),
                                            ALU.add).then_inc(added, 1)

                def cap(it, b):
                    g = it * NB + b
                    dve.wait_ge(exp_done, g + 1)
                    flat = ex[:, :, :].rearrange("p k n -> p (k n)")
                    nc.vector.tensor_scalar_min(flat, flat, EXP_CAP).then_inc(cap_done, 1)

                def softplus(it, b):
                    g = it * NB + b
                    dve.wait_ge(ln_done, g + 2)
                    z = (b % 2) * KH * 512
                    for k in range(KH):
                        last = nc.vector.scalar_tensor_tensor(
                            out=ssp[b % 2][:, k, :], in0=psz[:, z + k * 512:z + (k + 1) * 512], scalar=fb1[:, k:k + 1],
                            in1=ssp[b % 2][:, k, :], op0=ALU.add, op1=ALU.max)
                    last.then_inc(ssp_done, 1)

                def step(it, b, first):
                    f, m, a = (None if first and b < k else back(it, b, k) for k in (1, 2, 3))
                    bases = bases_of.step(it, b, first)
                    if a:
                        add(*a, bases, 0)
                    if m:
                        bias(*m, 1)
                    if a:
                        add(*a, bases, 1)
                    if m:
                        message(*m, 0)
                    if a:
                        add(*a, bases, 2)
                    cap(it, b)
                    if a:
                        add(*a, bases, 3)
                    if m:
                        message(*m, 1)
                    select(it, b, 0)
                    select(it, b, 1)
                    softplus(it, b)
                    if f:
                        bias(*f, 0)
                    select(it, b, 2)
                    select(it, b, 3)

                def tail(it):
                    bias(it, NB - 2, 1)
                    for h in range(2):
                        message(it, NB - 2, h)
                    for h in range(2):
                        bias(it, NB - 1, h)
                    for h in range(2):
                        message(it, NB - 1, h)
                    for b in range(1, NB):
                        bases = bases_of.group(it * NB + b)
                        for t in range(GT):
                            add(it, b, bases, t)

                skewed(dve, step, tail)

            @block.tensor
            def _(pe):
                pe.wait_ge(w_in, 96)
                for k in range(KH):
                    last = nc.tensor.matmul(psw[:, 0:D], sh["ones"][:, :], fw2[:, k, :], start=(k == 0), stop=(k == KH - 1))
                last.then_inc(bias_mm, 1)

                def hidden(it, b):
                    g = it * NB + b
                    z = (b % 2) * KH * 512
                    half = slice((b % 2) * NG, (b % 2 + 1) * NG)
                    if b % 2 == 0:
                        pe.wait_ge(edge_in[b // 2], it * 16 + 16)
                    pe.wait_ge(ssp_done, g + 1)
                    for k in range(KH):
                        last = nc.tensor.matmul(psz[:, z + k * 512:z + (k + 1) * 512], fw1[half, k * P:(k + 1) * P],
                                                edge[b // 2][half, :], start=True, stop=True)
                    last.then_inc(z_done, 1)

                def filters(it, b):
                    g = it * NB + b
                    pe.wait_ge(ssp_done, g + 3)
                    for h in range(2):
                        pe.wait_ge(biased, 2 * g + h + 1)
                        for t in (2 * h, 2 * h + 1):
                            for k in range(KH):
                                last = nc.tensor.matmul(psw[:, t * D:(t + 1) * D], ssp[b % 2][:, k, t * P:(t + 1) * P],
                                                        fw2[:, k, :], start=(k == 0), stop=(k == KH - 1))
                        last.then_inc(w_done, 1)

                def windows(it, b):
                    g = it * NB + b
                    pe.wait_ge(sel_done, g + 1)
                    for h in range(2):
                        pe.wait_ge(msg_done, 2 * g + h + 2 * NB + 1)
                        pe.wait_ge(added, GT * g + 2 * h + 2)
                        for t in (2 * h, 2 * h + 1):
                            for k in range(KH):
                                last = nc.tensor.matmul(psa[:, t * D + k * P:t * D + (k + 1) * P],
                                                        msg[b % 2][:, t, k * P:(k + 1) * P], sel[b][:, t, :],
                                                        start=True, stop=True)
                        last.then_inc(win_done, 1)

                def step(it, b, first):
                    hidden(it, b)
                    if not first or b >= 1:
                        filters(*back(it, b, 1))
                    if not first or b >= 2:
                        windows(*back(it, b, 2))

                def tail(it):
                    filters(it, NB - 1)
                    windows(it, NB - 2)
                    windows(it, NB - 1)

                skewed(pe, step, tail)


def nodes_schnet(nc, dram, sh, acc):
    with Phase(nc, "n1") as ph:
        nm = Norm(ph, sh)
        w2, w3, wg = (ph.sb(s, [P, KH, D]) for s in ("w2", "w3", "wg"))
        gw = ph.sb("gw", [P, KH, D])
        att = ph.sb("att", [P, KH, 2 * HEADS])
        watt = ph.sb("watt", [P, KH, 2 * HEADS])
        b2 = ph.sb("b2", [P, KH])
        b3 = ph.sb("b3", [P, D])
        ssp = pair_of(ph, "ssp", [P, KH, CN])
        O = pair_of(ph, "O", [P, CT, D])
        A = pair_of(ph, "A", [P, CT, 2 * HEADS])
        psO = psum_pair(ph, "psO")
        S = ph.sem
        w_in, att_zero, bias_mm, bias_done, watt_mm, watt_done = (S(s) for s in (
            "w_in", "att_zero", "bias_mm", "bias_done", "watt_mm", "watt_done"))
        z_done, exp_done, cap_done, ln_done, ssp_done, x_done = (S(s) for s in (
            "z_done", "exp_done", "cap_done", "ln_done", "ssp_done", "x_done"))
        res_in = [S(f"res_in{p}") for p in range(2)]
        x_stored = [S(f"x_stored{p}") for p in range(2)]
        o_stored = [S(f"o_stored{p}") for p in range(2)]
        a_stored = [S(f"a_stored{p}") for p in range(2)]
        y_added = S("y_added", 2)
        y_done = S("y_done", 2)
        mm_done = S("mm_done", 2)
        o_done = S("o_done", 2)
        a_done = S("a_done", 2)

        ph.begin()
        with nc.Block() as block:

            @block.sync
            def _(sp):
                sp.dma_start(w2[:, :, :], by_half(dram["w2_t"])).then_inc(w_in, 16)
                sp.dma_start(w3[:, :, :], by_half(dram["w3_t"])).then_inc(w_in, 16)
                sp.dma_start(wg[:, :, :], by_half(dram["gat_w_t"])).then_inc(w_in, 16)
                sp.dma_start(gw[:, :, :], by_half(dram["gat_w"])).then_inc(w_in, 16)
                sp.dma_start(b2[:, :], dram["b2"][:, :]).then_inc(w_in, 16)
                sp.dma_start(b3[:, :], on_all(dram["b3"], D)).then_inc(w_in, 16)
                sp.wait_ge(att_zero, 1)
                for h in range(HEADS):
                    p = (h * HID) % P
                    for j, name in enumerate(("att_src", "att_dst")):
                        sp.dma_start(att[p:p + HID, h * HID // P, j * HEADS + h:j * HEADS + h + 1],
                                     dram[name][h * HID:(h + 1) * HID].rearrange("(p a) -> p a", a=1)).then_inc(w_in, 16)

                def step(at):
                    if at(0):
                        c = at(0)
                        hold(sp, ph, nm.norm_done, c.n + 1)
                        wait_stored(sp, ph, x_stored, c)
                        sp.dma_start(nm.X[c.p][:, :, :], node_rows(dram["x"], c.n)).then_inc(res_in[c.p], 16)
                    if at(1):
                        c = at(1)
                        hold(sp, ph, x_done, c.n + 1)
                        sp.dma_start(node_rows(dram["x1"], c.n), nm.X[c.p][:, :, :]).then_inc(x_stored[c.p], 16)

                staggered(sp, step, 1)
                all_stored(sp, x_stored)

            @block.gpsimd
            def _(pool):
                def step(at):
                    c = at(0)
                    store_out(nc, pool, ph, O, dram["tab1"], c, o_done, o_stored)
                    hold(pool, ph, a_done, c.n + 3)
                    pool.dma_start(node_rows(dram["tab_as"], c.n), A[c.p][:, :, 0:HEADS]).then_inc(a_stored[c.p], 16)
                    pool.dma_start(node_rows(dram["att_tab"], c.n), A[c.p][:, :, :]).then_inc(a_stored[c.p], 16)

                staggered(pool, step, 0)
                all_stored(pool, o_stored)
                all_stored(pool, a_stored, 32)

            @block.scalar
            def _(act):
                act.preload_act_table_set(EXP_LN)

                def step(at):
                    if at(3):
                        c = at(3)
                        copy_out(nc, act, ph, O, psO, c, mm_done, o_stored, o_done)
                        wait_stored(act, ph, a_stored, c, 32)
                        nc.scalar.activation(A[c.p][:, :, :].rearrange("p t n -> p (t n)"),
                                             nm.psT[c.p][:, 0:CT * 2 * HEADS], ACT.Copy).then_inc(a_done, 1)
                    if at(2):
                        nm.deviations(act, at(2))
                    if at(0):
                        c = at(0)
                        act.wait_ge(z_done, c.n + 1)
                        act.wait_ge(y_done, c.n + 1)
                        for k in range(KH):
                            last = nc.scalar.activation(ssp[c.p][:, k, :], psO[c.p][:, k * CN:(k + 1) * CN], ACT.Exp,
                                                        bias=b2[:, k:k + 1])
                        last.then_inc(exp_done, 1)
                    if at(2):
                        nm.relu(act, at(2), mm_done)
                    if at(0):
                        c = at(0)
                        act.wait_ge(cap_done, c.n + 1)
                        nc.scalar.activation(ssp[c.p][:, :, :], ssp[c.p][:, :, :], ACT.Ln, bias=1.0).then_inc(ln_done, 1)

                staggered(act, step, 3)

            @block.vector
            def _(dve):
                nc.vector.memset(att[:, :, :], 0.0).then_inc(att_zero, 1)
                dve.wait_ge(w_in, 16 * 22)
                dve.wait_ge(bias_mm, 1)
                nc.vector.scalar_tensor_tensor(out=b3[:, :], in0=psO[0][:, 0:D], scalar=-LN2, in1=b3[:, :],
                                               op0=ALU.mult, op1=ALU.add).then_inc(bias_done, 1)
                dve.wait_ge(watt_mm, 1)
                nc.vector.tensor_copy(watt[:, :, :].rearrange("p k n -> p (k n)"),
                                      psO[0][:, 512:512 + KH * 2 * HEADS]).then_inc(watt_done, 1)
                dve.wait_ge(bias_done, 1)

                def softplus(c):
                    dve.wait_ge(exp_done, c.n + 1)
                    flat = ssp[c.p][:, :, :].rearrange("p k n -> p (k n)")
                    nc.vector.tensor_scalar_min(flat, flat, EXP_CAP).then_inc(cap_done, 1)
                    dve.wait_ge(ln_done, c.n + 1)
                    for k in range(KH):
                        part = ssp[c.p][:, k, :]
                        last = nc.vector.scalar_tensor_tensor(out=part, in0=psO[c.p][:, k * CN:(k + 1) * CN],
                                                              scalar=b2[:, k:k + 1], in1=part, op0=ALU.add, op1=ALU.max)
                    last.then_inc(ssp_done, 1)

                def residual(c):
                    dve.wait_ge(res_in[c.p], c.k * 16 + 16)
                    dve.wait_ge(y_done, c.n + 3)
                    xf = nm.X[c.p][:, :, :].rearrange("p t n -> p (t n)")
                    for lo, hi in BANKS:
                        last = nc.vector.tensor_tensor(xf[:, lo:hi], xf[:, lo:hi], psO[c.p][:, lo:hi], ALU.add)
                    last.then_inc(y_added, 1)
                    dve.wait_ge(y_added, c.n + 3)
                    nc.vector.tensor_tensor(nm.X[c.p][:, :, :], nm.X[c.p][:, :, :],
                                            b3[:, :].unsqueeze(1).to_broadcast([P, CT, D]), ALU.add).then_inc(x_done, 1)
                    dve.wait_ge(x_done, c.n + 1)
                    nm.statistics(dve, c)

                def step(at):
                    if at(2):
                        nm.normalize(dve, at(2))
                    if at(0):
                        softplus(at(0))
                    if at(1):
                        residual(at(1))

                staggered(dve, step, 2)

            @block.tensor
            def _(pe):
                pe.wait_ge(w_in, 16 * 22)
                for k in range(KH):
                    last = nc.tensor.matmul(psO[0][:, 0:D], sh["ones"][:, :], w3[:, k, :], start=(k == 0), stop=(k == KH - 1))
                last.then_inc(bias_mm, 1)
                for k in range(KH):
                    for f in range(KH):
                        last = nc.tensor.matmul(psO[0][:, 512 + k * 2 * HEADS:512 + (k + 1) * 2 * HEADS],
                                                gw[:, f, k * P:(k + 1) * P], att[:, f, :],
                                                start=(f == 0), stop=(f == KH - 1))
                last.then_inc(watt_mm, 1)
                pe.wait_ge(bias_done, 1)
                pe.wait_ge(watt_done, 1)

                def hidden(c):
                    pe.wait_ge(y_added, c.n + 1)
                    for k in range(KH):
                        for f in range(KH):
                            last = nc.tensor.matmul(psO[c.p][:, k * CN:(k + 1) * CN], w2[:, f, k * P:(k + 1) * P],
                                                    acc[:, f, bass.ds(c.n * CN, CN)],
                                                    start=(f == 0), stop=(f == KH - 1))
                    last.then_inc(z_done, 1)

                def output(c):
                    pe.wait_ge(ssp_done, c.n + 1)
                    pe.wait_ge(o_done, c.n + 1)
                    project(nc, psO[c.p], ssp[c.p], w3).then_inc(y_done, 1)

                def tables(c, ahead):
                    pe.wait_ge(nm.hT_done, c.n + 3)
                    if ahead:
                        pe.wait_ge(ssp_done, ahead.n + 1)
                    for t in range(CT):
                        for k in range(KH):
                            nc.tensor.matmul(nm.psT[c.p][:, t * 2 * HEADS:(t + 1) * 2 * HEADS],
                                             nm.hT[c.p][:, k, t * P:(t + 1) * P], watt[:, k, :],
                                             start=(k == 0), stop=(k == KH - 1))
                    project(nc, psO[c.p], nm.hT[c.p], wg).then_inc(mm_done, 1)

                def step(at):
                    if at(0):
                        hidden(at(0))
                    if at(2):
                        pe.wait_ge(a_done, at(2).n + 1)
                        nm.transpose(pe, at(2))
                    if at(1):
                        output(at(1))
                    if at(2):
                        tables(at(2), at(0))

                staggered(pe, step, 2)


def edges_max(nc, dram, sh, a_src, seg_max):
    SH = SEG * HEADS
    with Phase(nc, "mx") as ph:
        prev_c, next_c = ph.sb("prev_c", [P, TILES], I32), ph.sb("next_c", [P, TILES], I32)
        last_b = ph.sb("last_b", [P, TILES], I32)
        pen = [ph.sb(f"pen{i}", [P, TILES]) for i in range(2)]
        out_seg = [ph.sb(f"out_seg{i}", [P, TILES]) for i in range(2)]
        slot = [ph.sb(f"slot{i}", [P, SEG, HEADS]) for i in range(2)]
        idx = [ph.sb(f"idx{i}", [P, SEG // 2], I32) for i in range(2)]
        pen_x = ph.sb("pen_x", [P, 2, SEG, HEADS])
        pen_t = ph.sb("pen_t", [P, 2, P])
        scan = ph.sb("scan", [P, 2, P])
        both = ph.sb("both", [P, P])
        ends = ph.sb("ends", [P, 2, ITERS])
        row = {n: ph.sb(f"row_{n}", [HEADS, TILES], I32) for n in ("first", "last", "prev", "next")}
        one = ph.sb("one", [HEADS, TILES])
        cont = ph.sb("cont", [HEADS, 2, TILES])
        pass_on = ph.sb("pass_on", [HEADS, 2, TILES])
        tile_max = ph.sb("tile_max", [HEADS, 2, TILES])
        run = ph.sb("run", [HEADS, 2, TILES])
        carry = ph.sb("carry", [HEADS, 2, TILES])
        carry_b = ph.sb("carry_b", [P, HEADS, TILES])
        tab, tab_h = ph.sb("tab", [P, NT, HEADS]), ph.sb("tab_h", [P, HEADS, NT])
        part = ph.sb("part", [P, TILES], I32)
        lo, hi = ph.sb("lo", [P, TILES]), ph.sb("hi", [P, TILES])
        hot = [ph.sb(f"hot{u}", [P, GT, P]) for u in range(2)]
        hot_t = [ph.sb(f"hot_t{u}", [P, GT, P]) for u in range(2)]
        own = ph.sb("own", [P, GT, HEADS, NT])
        ps = ph.ps("ps", 2048)
        psg = ph.ps("psg", GT * 512)
        S = ph.sem
        loaded, link = S("loaded"), S("link")
        tab_in, split = S("tab_in"), S("split")
        hot_done = S("hot_done")
        st_ps = S("st_ps", 2)
        st_done = S("st_done", 1)
        looked = S("looked", 2 * GT)
        masked = S("masked", GT)
        filled = S("filled")
        gathered = [S("gathered0"), S("gathered1")]
        idx_done, penx_done, pent_ps, pent_done = (S(s) for s in ("idx_done", "penx_done", "pent_ps", "pent_done"))
        val_done = S("val_done", 2)
        scan_done = S("scan_done", 1)
        both_done = S("both_done", 1)
        max_done = S("max_done", 1)
        kept = S("kept", 1)
        copied = S("copied", 2)
        ends_done, ends_ps, ends_in = S("ends_done", 2), S("ends_ps"), S("ends_in")
        carry_done, carry_out, merged = S("carry_done"), S("carry_out"), S("merged")
        carry_in = [S("carry_in0"), S("carry_in1")]

        ph.begin()
        with nc.Block() as block:

            @block.sync
            def _(sp):
                sp.dma_start(prev_c[:, :], dram["prev_cols"][:, :]).then_inc(loaded, 16)
                sp.dma_start(next_c[:, :], dram["next_cols"][:, :]).then_inc(loaded, 16)
                sp.dma_start(last_b[:, :], dram["dst_cols"][P - 1:P, :].broadcast_to([P, TILES])).then_inc(loaded, 16)
                for name, src in (("first", dram["dst_cols"][0:1, :]), ("last", dram["dst_cols"][P - 1:P, :]),
                                  ("prev", dram["prev_cols"][0:1, :]), ("next", dram["next_cols"][P - 1:P, :])):
                    sp.dma_start(row[name][:, :], src.broadcast_to([HEADS, TILES])).then_inc(loaded, 16)
                sp.dma_start(tab[:, :, :], dram["tab_as"].rearrange("(t p) h -> p t h", p=P)).then_inc(tab_in, 16)
                sp.wait_ge(carry_done, 1)
                for w in range(2):
                    sp.dma_start(dram["carry"][w, :, :], carry[:, w, :]).then_inc(carry_out, 16)
                sp.wait_ge(carry_out, 32)
                for w in range(2):
                    if w == 1:
                        sp.wait_ge(merged, 1)
                    sp.dma_start(carry_b[:, :, :].rearrange("p h t -> p (h t)"),
                                 dram["carry"][w:w + 1, :, :].rearrange("a h t -> a (h t)")
                                 .broadcast_to([P, TILES * HEADS])).then_inc(carry_in[w], 16)

            @block.gpsimd
            def _(pool):
                with pool.Fori(0, ITERS // 2) as i2:
                    for q in range(2):
                        it = i2 * 2 + q
                        hold(pool, ph, val_done, it + 1)
                        hold(pool, ph, copied, it + 1)
                        nc.gpsimd.tensor_copy(idx[q][:, :], sh["src_sb"][:, bass.ds(it * SEG, SEG // 2)]).then_inc(idx_done, 1)
                        hold(pool, ph, idx_done, it + 1)
                        for t in range(SEG // 2):
                            nc.gpsimd.indirect_dma_start(
                                out=slot[q][:, t, :], out_offset=None, in_=dram["tab_as"][:, :],
                                in_offset=bass.IndirectOffsetOnAxis(ap=idx[q][:, t:t + 1].bitcast(U32), axis=0),
                            ).then_inc(gathered[q], 16)

            @block.scalar
            def _(act):
                act.wait_ge(link, 4)

                def penalties(c):
                    act.wait_ge(scan_done, c.n + 1)
                    for w in range(2):
                        last = nc.scalar.activation(
                            pen_x[:, w, :, :], pen[w][:, bass.ds(c.n * SEG, SEG)].unsqueeze(2)
                            .to_broadcast([P, SEG, HEADS]), ACT.Copy)
                    last.then_inc(penx_done, 1)
                    act.wait_ge(pent_ps, c.n + 1)
                    nc.scalar.activation(pen_t[:, :, :].rearrange("p w e -> p (w e)"), ps[:, 512:512 + 2 * P],
                                         ACT.Copy).then_inc(pent_done, 1)

                def copy_hot(c, u):
                    unit = c.n * 2 + u
                    act.wait_ge(st_ps, unit + 3)
                    act.wait_ge(looked, unit * GT + GT)
                    nc.scalar.activation(hot_t[u][:, :, :].rearrange("p t e -> p (t e)"), ps[:, 1536:2048],
                                         ACT.Copy).then_inc(st_done, 1)

                def keep_values(c):
                    act.wait_ge(gathered[c.p], (c.k + 1) * (8 * SEG))
                    act.wait_ge(filled, c.n * 2 + 2)
                    nc.scalar.activation(a_src[:, bass.ds(c.n * SH, SH)], slot[c.p][:, :, :].rearrange("p t h -> p (t h)"),
                                         ACT.Copy).then_inc(copied, 1)
                    act.wait_ge(scan_done, c.n + 2)
                    nc.scalar.activation(ends[:, 0, bass.ds(c.n, 1)], scan[:, 0, P - 1:P], ACT.Copy).then_inc(ends_done, 1)
                    nc.scalar.activation(ends[:, 1, bass.ds(c.n, 1)], scan[:, 1, 0:1], ACT.Copy).then_inc(ends_done, 1)

                def step(at):
                    if at(1):
                        penalties(at(1))
                    if at(0):
                        copy_hot(at(0), 0)
                        copy_hot(at(0), 1)
                    if at(1):
                        keep_values(at(1))

                staggered(act, step, 1, ITERS, 2)

            @block.vector
            def _(dve):
                ch = Chain(dve, link)

                def penalty(out, a, b, op=ALU.not_equal):
                    ch.link(nc.vector.tensor_tensor(out, a, b, op))
                    ch.link(nc.vector.tensor_scalar(out, out, -BIG, None, ALU.mult))

                dve.wait_ge(loaded, 16 * 7)
                penalty(pen[0][:, :], sh["dst_sb"][:, :], prev_c[:, :])
                penalty(pen[1][:, :], sh["dst_sb"][:, :], next_c[:, :])
                ch.link(nc.vector.tensor_scalar(out_seg[0][:, :], sh["rel"][:, :], 0.0, -BIG, ALU.not_equal, ALU.mult))
                penalty(out_seg[1][:, :], sh["dst_sb"][:, :], last_b[:, :])

                nc.vector.tensor_scalar(part[:, :], sh["src_sb"][:, :], P - 1, None, ALU.bitwise_and).then_inc(split, 1)
                dve.wait_ge(split, 1)
                nc.vector.tensor_copy(lo[:, :], part[:, :]).then_inc(split, 1)
                nc.vector.tensor_tensor(hi[:, :], sh["src_sb"][:, :], part[:, :], ALU.subtract).then_inc(split, 1)
                dve.wait_ge(split, 3)
                nc.vector.tensor_scalar(hi[:, :], hi[:, :], 1.0 / P, None, ALU.mult).then_inc(split, 1)
                dve.wait_ge(tab_in, 16)
                nc.vector.tensor_copy(tab_h[:, :, :], tab[:, :, :].rearrange("p i h -> p h i")).then_inc(split, 1)
                dve.wait_ge(split, 5)

                def one_hots(c):
                    for u in range(2):
                        dve.wait_ge(st_ps, c.n * 2 + u + 1)
                        for t in range(GT):
                            tile = c.n * SEG + (SEG // 2 + u * GT + t)
                            last = nc.vector.tensor_scalar(hot[u][:, t, :], sh["iota"][:, :], lo[:, bass.ds(tile, 1)],
                                                           None, ALU.is_equal)
                        last.then_inc(hot_done, 1)

                def fill(c, u):
                    first = c.n * (2 * GT) + u * GT
                    for t in range(GT):
                        dve.wait_ge(looked, first + (t + 1 + 2 * GT))
                        tile = c.n * SEG + (SEG // 2 + u * GT + t)
                        nc.vector.scalar_tensor_tensor(
                            out=own[:, t, :, :], in0=sh["iota"][:, 0:NT].unsqueeze(1).to_broadcast([P, HEADS, NT]),
                            scalar=hi[:, bass.ds(tile, 1)],
                            in1=psg[:, t * 512:t * 512 + HEADS * NT].rearrange("p (h i) -> p h i", i=NT),
                            op0=ALU.is_equal, op1=ALU.mult).then_inc(masked, 1)
                    dve.wait_ge(masked, first + 2 * GT)
                    dve.wait_ge(val_done, c.n + 1)
                    dve.wait_ge(copied, c.n + 1)
                    at_slot = SEG // 2 + u * GT
                    nc.vector.tensor_reduce(slot[c.p][:, at_slot:at_slot + GT, :].rearrange("p t h -> p (t h)"),
                                            own[:, :, :, :].rearrange("p t h i -> p (t h) i"),
                                            mybir.AxisListType.X, ALU.add).then_inc(filled, 1)
                    dve.wait_ge(filled, c.n * 2 + u + 1)

                def scans(c):
                    dve.wait_ge(val_done, c.n + 3)
                    dve.wait_ge(pent_done, c.n + 1)
                    dve.wait_ge(both_done, c.n + 1)
                    dve.wait_ge(ends_done, 2 * c.n + 2)
                    nc.vector.tensor_tensor_scan(scan[:, 0, :], pen_t[:, 0, :], ps[:, 0:P], -BIG, ALU.add, ALU.max)
                    nc.vector.tensor_tensor_scan(scan[:, 1, ::-1], pen_t[:, 1, ::-1], ps[:, 0:P][:, ::-1],
                                                 -BIG, ALU.add, ALU.max).then_inc(scan_done, 1)
                    dve.wait_ge(scan_done, c.n + 2)
                    dve.wait_ge(max_done, c.n + 1)
                    nc.vector.tensor_tensor(both[:, :], scan[:, 0, :], scan[:, 1, :], ALU.max).then_inc(both_done, 1)

                def keep_maxima(c):
                    dve.wait_ge(max_done, c.n + 2)
                    nc.vector.tensor_copy(seg_max[:, bass.ds(c.n * SH, SH)], ps[:, 1024:1024 + P]).then_inc(kept, 1)

                def step(at):
                    if at(1):
                        fill(at(1), 0)
                    if at(2):
                        keep_maxima(at(2))
                    if at(0):
                        one_hots(at(0))
                    if at(1):
                        fill(at(1), 1)
                        scans(at(1))

                staggered(dve, step, 2, ITERS, 2)
                t_first, t_last, t_prev, t_next = (row[n] for n in ("first", "last", "prev", "next"))
                penalty(one[:, :], t_first[:, :], t_last[:, :])
                penalty(cont[:, 0, :], t_first[:, :], t_prev[:, :])
                penalty(cont[:, 1, :], t_last[:, :], t_next[:, :])
                for w in range(2):
                    ch.link(nc.vector.tensor_tensor(pass_on[:, w, :], cont[:, w, :], one[:, :], ALU.min))
                for w in range(2):
                    dve.wait_ge(ends_ps, w + 1)
                    for k in range(2):
                        half = slice(k * SEG // 2, (k + 1) * SEG // 2)
                        last = nc.vector.tensor_copy(
                            tile_max[:, w, :].rearrange("h (b t) -> h t b", t=SEG)[:, half, :],
                            ps[0:HEADS, 512 + k * 512:512 + k * 512 + SEG // 2 * ITERS].rearrange("h (t b) -> h t b", b=ITERS))
                    last.then_inc(ends_in, 1)
                dve.wait_ge(ends_in, 2)
                ch.link(nc.vector.tensor_tensor_scan(run[:, 0, :], pass_on[:, 0, :], tile_max[:, 0, :], -BIG, ALU.add, ALU.max))
                ch.link(nc.vector.tensor_tensor_scan(run[:, 1, ::-1], pass_on[:, 1, ::-1], tile_max[:, 1, ::-1],
                                                     -BIG, ALU.add, ALU.max))
                nc.vector.memset(carry[:, 0, 0:1], -BIG)
                nc.vector.memset(carry[:, 1, TILES - 1:TILES], -BIG)
                nc.vector.tensor_tensor(carry[:, 0, 1:TILES], run[:, 0, 0:TILES - 1], cont[:, 0, 1:TILES], ALU.add)
                nc.vector.tensor_tensor(carry[:, 1, 0:TILES - 1], run[:, 1, 1:TILES], cont[:, 1, 0:TILES - 1],
                                        ALU.add).then_inc(carry_done, 1)
                dve.wait_ge(kept, ITERS + 1)
                for w in range(2):
                    dve.wait_ge(carry_in[w], 16)
                    ch.link(nc.vector.tensor_tensor(carry_b[:, :, :], carry_b[:, :, :],
                                                    out_seg[w][:, :].unsqueeze(1).to_broadcast([P, HEADS, TILES]), ALU.add))
                    by_head = seg_max[:, :].rearrange("p (t h) -> p h t", h=HEADS)
                    nc.vector.tensor_tensor(by_head, by_head, carry_b[:, :, :], ALU.max).then_inc(merged, 1)
                    dve.wait_ge(merged, w + 1)

            @block.tensor
            def _(pe):
                pe.wait_ge(split, 5)

                def penalties(c):
                    pe.wait_ge(penx_done, c.n + 1)
                    for w in range(2):
                        last = nc.tensor.transpose(ps[:, 512 + w * P:512 + (w + 1) * P],
                                                   pen_x[:, w, :, :].rearrange("p t h -> p (t h)"), sh["ident"][:, :])
                    last.then_inc(pent_ps, 1)

                def transpose_hot(c, u):
                    pe.wait_ge(hot_done, c.n * 2 + u + 1)
                    pe.wait_ge(st_done, c.n * 2 + u + 1)
                    for t in range(GT):
                        last = nc.tensor.transpose(ps[:, 1536 + t * P:1536 + (t + 1) * P], hot[u][:, t, :], sh["ident"][:, :])
                    last.then_inc(st_ps, 1)

                def look_up(c, u, tiles):
                    pe.wait_ge(st_done, c.n * 2 + u + 2)
                    for t in tiles:
                        pe.wait_ge(masked, c.n * (2 * GT) + u * GT + t + 1)
                        nc.tensor.matmul(psg[:, t * 512:t * 512 + HEADS * NT], hot_t[u][:, t, :],
                                         tab_h[:, :, :].rearrange("p h i -> p (h i)"), start=True, stop=True).then_inc(looked, 1)

                def values(c):
                    pe.wait_ge(gathered[c.p], (c.k + 1) * (8 * SEG))
                    pe.wait_ge(filled, c.n * 2 + 2)
                    pe.wait_ge(scan_done, c.n + 1)
                    nc.tensor.transpose(ps[:, 0:P], slot[c.p][:, :, :].rearrange("p t h -> p (t h)"),
                                        sh["ident"][:, :]).then_inc(val_done, 1)

                def maxima(c):
                    pe.wait_ge(both_done, c.n + 2)
                    pe.wait_ge(kept, c.n + 1)
                    nc.tensor.transpose(ps[:, 1024:1024 + P], both[:, :], sh["ident"][:, :]).then_inc(max_done, 1)

                def step(at):
                    if at(1):
                        penalties(at(1))
                    if at(0):
                        transpose_hot(at(0), 0)
                        transpose_hot(at(0), 1)
                        look_up(at(0), 0, (0, 1))
                    if at(1):
                        values(at(1))
                    if at(0):
                        look_up(at(0), 0, (2, 3))
                    if at(1):
                        maxima(at(1))
                    if at(0):
                        look_up(at(0), 1, range(GT))

                staggered(pe, step, 1, ITERS, 2)
                pe.wait_ge(ends_done, 2 * ITERS + 2)
                pe.wait_ge(kept, ITERS + 1)
                pe.wait_ge(pent_done, ITERS)
                for w in range(2):
                    if w == 1:
                        pe.wait_ge(ends_in, 1)
                    for t in range(SEG):
                        col = 512 + t // (SEG // 2) * 512 + t % (SEG // 2) * ITERS
                        last = nc.tensor.matmul(ps[0:HEADS, col:col + ITERS], sh["ident"][:, t * HEADS:(t + 1) * HEADS],
                                                ends[:, w, :], start=True, stop=True)
                    last.then_inc(ends_ps, 1)


def edges_gat(nc, dram, sh, a_src, seg_max, acc, acc_d):
    W2 = 2 * HEADS
    with Phase(nc, "l1") as ph:
        next_c = ph.sb("next_c", [P, TILES], I32)
        is_last = ph.sb("is_last", [P, TILES])
        rows = [ph.sb(f"rows{i}", [P, GT, D]) for i in range(NB)]
        idx = [ph.sb(f"idx{i}", [P, SEG], I32) for i in range(2)]
        sel = [ph.sb(f"sel{i}", [P, GT, P]) for i in range(NB)]
        win = [ph.sb(f"win{i}", [P, GT, W2]) for i in range(NB)]
        sel_t = [ph.sb(f"sel_t{i}", [P, GT, P]) for i in range(2)]
        logit = ph.sb("logit", [P, 2, GT * HEADS])
        lrelu = ph.sb("lrelu", [P, 2, GT * HEADS])
        diff = [ph.sb(f"diff{i}", [P, GT, HEADS]) for i in range(2)]
        wx = [ph.sb(f"wx{i}", [P, GT, W2]) for i in range(NB)]
        pst = ph.ps("pst", 512)
        pse = ph.ps("pse", 512)
        psa = ph.ps("psa", 2048)
        psd = ph.ps("psd", 1024)
        S = ph.sem
        loaded, setup = S("loaded"), S("setup")
        gathered = [S(f"gathered{i}") for i in range(NB)]
        win_in = [S(f"win_in{i}") for i in range(NB)]
        idx_done, sel_done = S("idx_done"), S("sel_done")
        st_ps = S("st_ps", 1)
        st_done = S("st_done", 1)
        exp_in = S("exp_in", 4)
        link = S("link", 1)
        logits = S("logits", 2)
        w_done = S("w_done")
        msg_done = S("msg_done")
        win_done = S("win_done", NB)
        added = S("added", 4 * GT)

        ph.begin()
        with nc.Block() as block:

            @block.sync
            def _(sp):
                sp.dma_start(next_c[:, :], dram["next_cols"][:, :]).then_inc(loaded, 16)
                regs = [sp.alloc_register(f"l1_row{t}") for t in range(GT)]
                with sp.Fori(0, ITERS) as it:
                    for b in range(NB):
                        g = it * NB + b
                        hold(sp, ph, exp_in, g + 1)
                        for t, base in enumerate(window_bases(sp, regs, sh, g)):
                            sp.dma_start(win[b][:, t, :], dram["att_tab"][bass.ds(base, P), :]).then_inc(win_in[b], 16)

            @block.gpsimd
            def _(pool):
                gather_all(nc, pool, ph, sh, dram["tab1"], rows, idx, win_done, 1, idx_done, gathered)

            @block.scalar
            def _(act):
                def copy_sel(it, b):
                    g = it * NB + b
                    act.wait_ge(st_ps, g + 2)
                    act.wait_ge(exp_in, g + 3)
                    nc.scalar.activation(sel_t[b % 2][:, :, :].rearrange("p t e -> p (t e)"), pst[:, :],
                                         ACT.Copy).then_inc(st_done, 1)

                def weights(it, b):
                    g = it * NB + b
                    act.wait_ge(logits, g + 3)
                    act.wait_ge(win_done, g + 1)
                    nc.scalar.activation(wx[b][:, :, 0:HEADS], diff[b % 2][:, :, :], ACT.Exp).then_inc(w_done, 1)

                def step(it, b, first):
                    copy_sel(it, b)
                    if not first or b >= 1:
                        weights(*back(it, b, 1))

                skewed(act, step, lambda it: weights(it, NB - 1))

            @block.vector
            def _(dve):
                bases_of = WindowBases(dve, sh, "l1", 3)
                dve.wait_ge(loaded, 16)
                nc.vector.memset(acc[:, :, :], 0.0)
                nc.vector.memset(acc_d[:, :], 0.0)
                nc.vector.tensor_tensor(is_last[:, :], sh["dst_sb"][:, :], next_c[:, :], ALU.not_equal).then_inc(setup, 1)
                dve.wait_ge(setup, 1)

                def select(it, b, t):
                    g = it * NB + b
                    if t == 0:
                        dve.wait_ge(win_done, g + 1)
                    ins = nc.vector.tensor_scalar(sel[b][:, t, :], sh["iota"][:, :], sh["rel"][:, bass.ds(g * GT + t, 1)],
                                                  None, ALU.is_equal)
                    if t == GT - 1:
                        ins.then_inc(sel_done, 1)

                def logits_of(it, b, step):
                    g = it * NB + b
                    e = pse[:, (b % 2) * GT * W2:(b % 2 + 1) * GT * W2].rearrange("p (t n) -> p t n", n=W2)
                    l0, l1 = (logit[:, w, :].rearrange("p (t n) -> p t n", n=HEADS) for w in range(2))
                    r0, r1 = (lrelu[:, w, :].rearrange("p (t n) -> p t n", n=HEADS) for w in range(2))
                    span = bass.ds(g * GT * HEADS, GT * HEADS)
                    mx, av = (x[:, span].rearrange("p (t n) -> p t n", n=HEADS) for x in (seg_max, a_src))
                    if step == 0:
                        dve.wait_ge(exp_in, g + 5)
                        nc.vector.tensor_tensor(l0, mx, e[:, :, 0:HEADS], ALU.max).then_inc(link, 1)
                        nc.vector.tensor_tensor(l1, av, e[:, :, HEADS:W2], ALU.add)
                    elif step == 1:
                        dve.wait_ge(link, g * 3 + 2)
                        nc.vector.tensor_tensor(l0, l0, e[:, :, HEADS:W2], ALU.add).then_inc(link, 1)
                    elif step == 2:
                        dve.wait_ge(link, g * 3 + 3)
                        nc.vector.scalar_tensor_tensor(out=lrelu[:, :, :], in0=logit[:, :, :], scalar=0.2,
                                                       in1=logit[:, :, :], op0=ALU.mult, op1=ALU.max).then_inc(link, 1)
                    else:
                        dve.wait_ge(link, g * 3 + 4)
                        dve.wait_ge(win_done, g + 1)
                        nc.vector.tensor_tensor(wx[b][:, :, HEADS:W2], r0,
                                                is_last[:, bass.ds(g * GT, GT)].unsqueeze(2)
                                                .to_broadcast([P, GT, HEADS]), ALU.mult)
                        nc.vector.tensor_tensor(diff[b % 2][:, :, :], r1, r0, ALU.subtract).then_inc(logits, 1)

                def message(it, b, t):
                    if t == 0:
                        dve.wait_ge(gathered[b], it * 64 + 64)
                        dve.wait_ge(w_done, it * NB + b + 1)
                    m = rows[b][:, t, :].rearrange("p (h n) -> p h n", n=HID)
                    ins = nc.vector.tensor_tensor(m, m, wx[b][:, t, 0:HEADS].unsqueeze(2).to_broadcast([P, HEADS, HID]),
                                                  ALU.mult)
                    if t == GT - 1:
                        ins.then_inc(msg_done, 1)

                def add(it, b, bases, t, w):
                    g = it * NB + b
                    if t == 0 and w == 0:
                        dve.wait_ge(win_done, g + NB + 1)
                    dve.wait_ge(added, 2 * (GT * g + t) + w + 4 * GT - 1)
                    if w == 0:
                        a = acc[:, :, bass.ds(bases[t], P)]
                        col = (b % 2) * 1024 + t * D
                        nc.vector.tensor_tensor(a, a, psa[:, col:col + D].rearrange("p (k r) -> p k r", k=KH),
                                                ALU.add).then_inc(added, 1)
                    else:
                        a = acc_d[:, bass.ds(bases[t], P)]
                        col = (b % 2) * 512 + t * P
                        nc.vector.tensor_tensor(a, a, psd[0:W2, col:col + P], ALU.add).then_inc(added, 1)

                def step(it, b, first):
                    n, m, a = (None if first and b < k else back(it, b, k) for k in (1, 2, 3))
                    for t in range(GT):
                        select(it, b, t)
                    bases = bases_of.step(it, b, first)
                    if m:
                        for t in range(GT):
                            message(*m, t)
                    for t in range(GT):
                        if n:
                            logits_of(*n, t)
                        if a:
                            for w in range(2):
                                add(*a, bases, t, w)

                def tail(it):
                    for t in range(GT):
                        logits_of(it, 3, t)
                        message(it, 2, t)
                    for t in range(GT):
                        message(it, 3, t)
                    for b in range(1, NB):
                        bases = bases_of.group(it * NB + b)
                        for t in range(GT):
                            for w in range(2):
                                add(it, b, bases, t, w)

                skewed(dve, step, tail)

            @block.tensor
            def _(pe):
                def transpose(it, b):
                    g = it * NB + b
                    pe.wait_ge(sel_done, g + 1)
                    pe.wait_ge(st_done, g + 1)
                    for t in range(GT):
                        last = nc.tensor.transpose(pst[:, t * P:(t + 1) * P], sel[b][:, t, :], sh["ident"][:, :])
                    last.then_inc(st_ps, 1)

                def expand(it, b):
                    g = it * NB + b
                    pe.wait_ge(st_done, g + 2)
                    pe.wait_ge(win_in[b], it * 64 + 64)
                    pe.wait_ge(logits, g + 2)
                    for t in range(GT):
                        col = (b % 2) * GT * W2 + t * W2
                        last = nc.tensor.matmul(pse[:, col:col + W2], sel_t[b % 2][:, t, :], win[b][:, t, :],
                                                start=True, stop=True)
                    last.then_inc(exp_in, 1)

                def windows(it, b):
                    g = it * NB + b
                    pe.wait_ge(msg_done, g + 1)
                    pe.wait_ge(added, 2 * GT * g + 2 * GT)
                    for t in range(GT):
                        for k in range(KH):
                            col = (b % 2) * 1024 + t * D + k * P
                            nc.tensor.matmul(psa[:, col:col + P], rows[b][:, t, k * P:(k + 1) * P], sel[b][:, t, :],
                                             start=True, stop=True)
                        col = (b % 2) * 512 + t * P
                        last = nc.tensor.matmul(psd[0:W2, col:col + P], wx[b][:, t, :], sel[b][:, t, :],
                                                start=True, stop=True)
                    last.then_inc(win_done, 1)

                def step(it, b, first):
                    if not first or b >= 1:
                        expand(*back(it, b, 1))
                    transpose(it, b)
                    if not first or b >= 2:
                        windows(*back(it, b, 2))

                def tail(it):
                    expand(it, 3)
                    windows(it, 2)
                    windows(it, 3)

                skewed(pe, step, tail)


def nodes_gat(nc, dram, sh, acc, acc_d):
    W2 = 2 * HEADS
    with Phase(nc, "n2") as ph:
        nm = Norm(ph, sh)
        w = ph.sb("w", [P, KH, D])
        gat_b, mean_b = ph.sb("gat_b", [P, D]), ph.sb("mean_b", [P, D])
        stage = pair_of(ph, "stage", [P, KH, CN])
        stage_d = pair_of(ph, "stage_d", [W2, CN])
        H, neg, O = (pair_of(ph, n, [P, CT, D]) for n in ("H", "neg", "O"))
        att = pair_of(ph, "att", [P, CT, W2])
        self_l, self_w, den = (pair_of(ph, n, [P, CT, HEADS]) for n in ("self_l", "self_w", "den"))
        psO = psum_pair(ph, "psO")
        S = ph.sem
        w_in = S("w_in")
        a_in, h_in, x_in = ([S(f"{n}{p}") for p in range(2)] for n in ("a_in", "h_in", "x_in"))
        x_stored, o_stored = ([S(f"{n}{p}") for p in range(2)] for n in ("x_stored", "o_stored"))
        link_l, link_a, link_h, link_x, l_done, w_done, biased, neg_done, exp_done, x_done, back_done = (S(s) for s in (
            "link_l", "link_a", "link_h", "link_x", "l_done", "w_done", "biased", "neg_done", "exp_done", "x_done", "back_done"))
        staged = S("staged")
        mm_done = S("mm_done", 2)
        o_done = S("o_done", 2)
        rows_done = S("rows_done", 2)

        ph.begin()
        with nc.Block() as block:

            @block.sync
            def _(sp):
                sp.dma_start(w[:, :, :], by_half(dram["mean_w"])).then_inc(w_in, 16)
                sp.dma_start(gat_b[:, :], on_all(dram["gat_b"], D)).then_inc(w_in, 16)
                sp.dma_start(mean_b[:, :], on_all(dram["mean_b"], D)).then_inc(w_in, 16)

                def step(at):
                    if at(0):
                        c = at(0)
                        hold(sp, ph, nm.norm_done, c.n + 1)
                        sp.dma_start(att[c.p][:, :, :], node_rows(dram["att_tab"], c.n)).then_inc(a_in[c.p], 16)
                        wait_stored(sp, ph, x_stored, c)
                        sp.dma_start(H[c.p][:, :, :], node_rows(dram["tab1"], c.n)).then_inc(h_in[c.p], 16)
                        sp.dma_start(nm.X[c.p][:, :, :], node_rows(dram["x1"], c.n)).then_inc(x_in[c.p], 16)
                    if at(1):
                        c = at(1)
                        hold(sp, ph, x_done, c.n + 1)
                        sp.dma_start(node_rows(dram["x2"], c.n), nm.X[c.p][:, :, :]).then_inc(x_stored[c.p], 16)

                staggered(sp, step, 1)
                all_stored(sp, x_stored)

            @block.gpsimd
            def _(pool):
                def step(at):
                    if at(0):
                        c = at(0)
                        hold(pool, ph, link_h, 2 * c.n + 2)
                        nc.gpsimd.tensor_tensor(H[c.p][:, :, :], H[c.p][:, :, :],
                                                gat_b[:, :].unsqueeze(1).to_broadcast([P, CT, D]),
                                                ALU.add).then_inc(biased, 1)
                    if at(2):
                        c = at(2)
                        hold(pool, ph, o_done, c.n + 3)
                        nc.gpsimd.tensor_tensor(O[c.p][:, :, :], O[c.p][:, :, :],
                                                mean_b[:, :].unsqueeze(1).to_broadcast([P, CT, D]),
                                                ALU.add).then_inc(rows_done, 1)
                        store_out(nc, pool, ph, O, dram["tab2"], c, rows_done, o_stored)

                staggered(pool, step, 2)
                all_stored(pool, o_stored)

            @block.scalar
            def _(act):
                act.preload_act_table_set(EXP_LN)

                def stage_in(c):
                    if not (isinstance(c.n, int) and c.n < 2):
                        act.wait_ge(back_done, c.n - 1)
                    for k in range(KH):
                        nc.scalar.activation(stage[c.p][:, k, :], acc[:, k, bass.ds(c.n * CN, CN)], ACT.Copy)
                    nc.scalar.activation(stage_d[c.p][:, :], acc_d[:, bass.ds(c.n * CN, CN)], ACT.Copy).then_inc(staged, 1)

                def step(at):
                    if at(0):
                        stage_in(at(0))
                    if at(2):
                        copy_out(nc, act, ph, O, psO, at(2), mm_done, o_stored, o_done)
                    if at(0):
                        c = at(0)
                        act.wait_ge(l_done, c.n + 1)
                        nc.scalar.activation(self_w[c.p][:, :, :], self_l[c.p][:, :, :], ACT.Exp).then_inc(w_done, 1)
                    if at(1):
                        nm.deviations(act, at(1))
                    if at(0):
                        act.wait_ge(biased, c.n + 1)
                        nc.scalar.activation(neg[c.p][:, :, :], H[c.p][:, :, :], ACT.Relu, scale=-1.0).then_inc(neg_done, 1)
                    if at(1):
                        nm.relu(act, at(1), mm_done)
                    if at(0):
                        act.wait_ge(neg_done, c.n + 1)
                        nc.scalar.activation(neg[c.p][:, :, :], neg[c.p][:, :, :], ACT.Exp, scale=-1.0).then_inc(exp_done, 1)

                staggered(act, step, 2)

            @block.vector
            def _(dve):
                dve.wait_ge(w_in, 48)

                def own_logit(c):
                    ch = Chain(dve, link_l, c.n * 2)
                    l = self_l[c.p]
                    dve.wait_ge(a_in[c.p], c.k * 16 + 16)
                    ch.link(nc.vector.tensor_tensor(l[:, :, :], att[c.p][:, :, 0:HEADS], att[c.p][:, :, HEADS:W2], ALU.add))
                    ch.link(nc.vector.scalar_tensor_tensor(out=l[:, :, :], in0=l[:, :, :], scalar=0.2,
                                                           in1=l[:, :, :], op0=ALU.mult, op1=ALU.max))
                    dve.wait_ge(back_done, c.n + 1)
                    dd = nm.psT[c.p][:, 0:CT * W2].rearrange("p (t n) -> p t n", n=W2)
                    nc.vector.tensor_tensor(l[:, :, :], l[:, :, :], dd[:, :, HEADS:W2], ALU.subtract).then_inc(l_done, 1)

                def attention(c):
                    ch = Chain(dve, link_a, c.n * 3)
                    dd = nm.psT[c.p][:, 0:CT * W2].rearrange("p (t n) -> p t n", n=W2)
                    flat = H[c.p][:, :, :].rearrange("p t n -> p (t n)")
                    heads = H[c.p][:, :, :].rearrange("p t (h n) -> p (t h) n", n=HID)
                    dve.wait_ge(w_done, c.n + 1)
                    ch.link(nc.vector.scalar_tensor_tensor(out=den[c.p][:, :, :], in0=dd[:, :, 0:HEADS], scalar=1e-16,
                                                           in1=self_w[c.p][:, :, :], op0=ALU.add, op1=ALU.add))
                    ch.link(nc.vector.reciprocal(den[c.p][:, :, :], den[c.p][:, :, :]))
                    dve.wait_ge(h_in[c.p], c.k * 16 + 16)
                    ch.link(nc.vector.tensor_tensor(heads, heads, self_w[c.p][:, :, :].rearrange("p t h -> p (t h)")
                                                    .unsqueeze(2).to_broadcast([P, CT * HEADS, HID]), ALU.mult))
                    for lo, hi in BANKS:
                        last = nc.vector.tensor_tensor(flat[:, lo:hi], flat[:, lo:hi], psO[c.p][:, lo:hi], ALU.add)
                    last.then_inc(link_h, 1)
                    dve.wait_ge(link_h, 2 * c.n + 1)
                    nc.vector.tensor_tensor(heads, heads, den[c.p][:, :, :].rearrange("p t h -> p (t h)")
                                            .unsqueeze(2).to_broadcast([P, CT * HEADS, HID]), ALU.mult).then_inc(link_h, 1)

                def residual(c):
                    dve.wait_ge(exp_done, c.n + 1)
                    nc.vector.scalar_tensor_tensor(out=H[c.p][:, :, :], in0=H[c.p][:, :, :], scalar=0.0,
                                                   in1=neg[c.p][:, :, :], op0=ALU.max, op1=ALU.add).then_inc(link_x, 1)
                    dve.wait_ge(link_x, c.n + 1)
                    dve.wait_ge(x_in[c.p], c.k * 16 + 16)
                    nc.vector.scalar_tensor_tensor(out=nm.X[c.p][:, :, :], in0=H[c.p][:, :, :], scalar=-1.0,
                                                   in1=nm.X[c.p][:, :, :], op0=ALU.add, op1=ALU.add).then_inc(x_done, 1)
                    dve.wait_ge(x_done, c.n + 1)
                    nm.statistics(dve, c)

                def step(at):
                    if at(0):
                        own_logit(at(0))
                    if at(1):
                        residual(at(1))
                    if at(0):
                        attention(at(0))
                    if at(1):
                        nm.normalize(dve, at(1))

                staggered(dve, step, 1)

            @block.tensor
            def _(pe):
                pe.wait_ge(w_in, 48)

                def unstage(c):
                    pe.wait_ge(staged, c.n + 1)
                    pe.wait_ge(o_done, c.n + 1)
                    pe.wait_ge(nm.hT_done, c.n + 1)
                    for t in range(CT):
                        for k in range(KH):
                            col = t * D + k * P
                            nc.tensor.transpose(psO[c.p][:, col:col + P], stage[c.p][:, k, t * P:(t + 1) * P],
                                                sh["ident"][:, :])
                    for t in range(CT):
                        last = nc.tensor.transpose(nm.psT[c.p][:, t * W2:(t + 1) * W2],
                                                   stage_d[c.p][:, t * P:(t + 1) * P], sh["ident"][0:W2, 0:W2])
                    last.then_inc(back_done, 1)

                def table(c):
                    pe.wait_ge(nm.hT_done, c.n + 3)
                    project(nc, psO[c.p], nm.hT[c.p], w).then_inc(mm_done, 1)

                def step(at):
                    if at(0):
                        unstage(at(0))
                    if at(1):
                        nm.transpose(pe, at(1))
                        table(at(1))

                staggered(pe, step, 1)


def edges_rows(nc, dram, sh, tag, table, width, acc, count=None):
    blocks = [(0, P), (P, P)] if width == D else [(0, width)]
    wide = len(blocks) * P
    rows_n = min(width, P)
    with Phase(nc, tag) as ph:
        rows = [ph.sb(f"rows{i}", [P, GT, width]) for i in range(NB)]
        idx = [ph.sb(f"idx{i}", [P, SEG], I32) for i in range(2)]
        sel = [ph.sb(f"sel{i}", [P, GT, P]) for i in range(NB)]
        psa = ph.ps("psa", 2 * GT * wide)
        psc = ph.ps("psc", 2 * GT * P)
        S = ph.sem
        gathered = [S(f"gathered{i}") for i in range(NB)]
        idx_done, sel_done = S("idx_done"), S("sel_done")
        cleared = S("cleared")
        win_done = S("win_done", NB)
        adds = 1 if count is None else 2
        added = S("added", 2 * GT * adds)

        ph.begin()
        with nc.Block() as block:

            @block.gpsimd
            def _(pool):
                gather_all(nc, pool, ph, sh, table, rows, idx, win_done, 1, idx_done, gathered)

            @block.vector
            def _(dve):
                regs = [dve.alloc_register(f"{tag}_base{t}") for t in range(GT)]
                if count is not None:
                    nc.vector.memset(count[:, :], 0.0)
                    nc.vector.memset(acc[:, :, :], 0.0).then_inc(cleared, 1)
                    dve.wait_ge(cleared, 1)

                def select(it, b):
                    g = it * NB + b
                    dve.wait_ge(win_done, g + 1)
                    select_group(nc, sel[b], sh, g).then_inc(sel_done, 1)

                def add(it, b):
                    g = it * NB + b
                    bases = window_bases(dve, regs, sh, g)
                    dve.wait_ge(win_done, g + NB + 1)
                    for t in range(GT):
                        dve.wait_ge(added, adds * (GT * g + t + 2 * GT))
                        col = ((b % 2) * GT + t) * wide
                        if width == D:
                            a = acc[:, :, bass.ds(bases[t], P)]
                            p = psa[:, col:col + wide].rearrange("p (k r) -> p k r", k=KH)
                        else:
                            a = acc[:, bass.ds(bases[t], P)]
                            p = psa[0:rows_n, col:col + wide]
                        nc.vector.tensor_tensor(a, a, p, ALU.add).then_inc(added, 1)
                        if count is not None:
                            a = count[:, bass.ds(bases[t], P)]
                            col = ((b % 2) * GT + t) * P
                            nc.vector.tensor_tensor(a, a, psc[:, col:col + P], ALU.add).then_inc(added, 1)

                def step(it, b, first):
                    select(it, b)
                    if not first or b >= 1:
                        add(*back(it, b, 1))

                skewed(dve, step, lambda it: add(it, NB - 1))

            @block.tensor
            def _(pe):
                with pe.Fori(0, ITERS) as it:
                    for b in range(NB):
                        g = it * NB + b
                        pe.wait_ge(sel_done, g + 1)
                        pe.wait_ge(gathered[b], it * 64 + 64)
                        pe.wait_ge(added, adds * GT * (g + 1))
                        for t in range(GT):
                            for k, (f, n) in enumerate(blocks):
                                col = ((b % 2) * GT + t) * wide + k * P
                                last = nc.tensor.matmul(psa[0:n, col:col + P], rows[b][:, t, f:f + n], sel[b][:, t, :],
                                                        start=True, stop=True)
                            if count is not None:
                                col = ((b % 2) * GT + t) * P
                                last = nc.tensor.matmul(psc[:, col:col + P], sh["ones"][:, :], sel[b][:, t, :],
                                                        start=True, stop=True)
                        last.then_inc(win_done, 1)


def nodes_mean(nc, dram, sh, acc, deg, acc3):
    with Phase(nc, "n3") as ph:
        nm = Norm(ph, sh)
        w = ph.sb("w", [P, KH, H3])
        deg_c = ph.sb("deg_c", [P, NT])
        dinv_b = ph.sb("dinv_b", [P, NT, H3])
        inv, dinv_c, has = ph.sb("inv", [P, NT]), ph.sb("dinv_c", [P, NT]), ph.sb("has", [P, NT])
        stage = pair_of(ph, "stage", [P, KH, CN])
        O = pair_of(ph, "O", [P, CT, H3])
        psO = psum_pair(ph, "psO")
        S = ph.sem
        w_in, deg_out, deg_in, staged, back_done, cols_done, rooted, cols_in, spread, roots, x_done = (S(s) for s in (
            "w_in", "deg_out", "deg_in", "staged", "back_done", "cols_done", "rooted", "cols_in", "spread", "roots", "x_done"))
        x_in = [S(f"x_in{p}") for p in range(2)]
        x_stored, o_stored = ([S(f"{n}{p}") for p in range(2)] for n in ("x_stored", "o_stored"))
        mm_done = S("mm_done", 2)
        o_done = S("o_done", 2)

        ph.begin()
        with nc.Block() as block:

            @block.sync
            def _(sp):
                sp.dma_start(w[:, :, :], by_half(dram["gcn_w1"])).then_inc(w_in, 16)
                sp.dma_start(dram["deg_row"][:, :], deg[0:1, 0:NP]).then_inc(deg_out, 16)
                sp.wait_ge(deg_out, 16)
                with nc.allow_non_contiguous_dma(reason="one degree for each partition and node tile"):
                    sp.dma_start(deg_c[:, :], dram["deg_row"].rearrange("a (t p) -> p (a t)", p=P)).then_inc(deg_in, 16)

                def step(at):
                    if at(0):
                        c = at(0)
                        hold(sp, ph, nm.norm_done, c.n + 1)
                        wait_stored(sp, ph, x_stored, c)
                        sp.dma_start(nm.X[c.p][:, :, :], node_rows(dram["x2"], c.n)).then_inc(x_in[c.p], 16)
                    if at(1):
                        c = at(1)
                        hold(sp, ph, x_done, c.n + 1)
                        sp.dma_start(node_rows(dram["x3"], c.n), nm.X[c.p][:, :, :]).then_inc(x_stored[c.p], 16)

                staggered(sp, step, 1)
                all_stored(sp, x_stored)

            @block.gpsimd
            def _(pool):
                staggered(pool, lambda at: store_out(nc, pool, ph, O, dram["tab3"], at(0), o_done, o_stored), 0)
                all_stored(pool, o_stored)

            @block.scalar
            def _(act):
                act.wait_ge(deg_in, 16)
                nc.scalar.activation(dinv_c[:, :], deg_c[:, :], ACT.Sqrt, bias=sh["ones"][:, 0:1]).then_inc(rooted, 1)
                act.wait_ge(rooted, 1)
                act.preload_act_table_set(EXP_LN)
                act.wait_ge(deg_out, 16)
                for c in range(CHUNKS):
                    act.wait_ge(spread, c + 1)
                    nc.scalar.activation(deg[0:H3, c * CN:(c + 1) * CN], psO[c % 2][0:H3, 0:CN], ACT.Copy).then_inc(roots, 1)

                def step(at):
                    if at(0):
                        c = at(0)
                        if not (isinstance(c.n, int) and c.n < 2):
                            act.wait_ge(back_done, c.n - 1)
                        for k in range(KH):
                            last = nc.scalar.activation(stage[c.p][:, k, :], acc[:, k, bass.ds(c.n * CN, CN)], ACT.Copy)
                        last.then_inc(staged, 1)
                    if at(1):
                        nm.relu(act, at(1), mm_done)
                    if at(0):
                        nm.deviations(act, at(0))

                staggered(act, step, 1)

            @block.vector
            def _(dve):
                ch = Chain(dve, cols_done)
                dve.wait_ge(deg_in, 16)
                ch.link(nc.vector.tensor_scalar_max(inv[:, :], deg_c[:, :], 1.0))
                ch.link(nc.vector.reciprocal(inv[:, :], inv[:, :]))
                ch.link(nc.vector.tensor_scalar(has[:, :], deg_c[:, :], 0.0, None, ALU.is_gt))
                ch.link(nc.vector.tensor_tensor(inv[:, :], inv[:, :], has[:, :], ALU.mult))
                dve.wait_ge(rooted, 1)
                ch.link(nc.vector.reciprocal(dinv_c[:, :], dinv_c[:, :]))
                nc.vector.tensor_copy(dinv_b[:, :, :], dinv_c[:, :].unsqueeze(2).to_broadcast([P, NT, H3])).then_inc(cols_in, 1)
                dve.wait_ge(roots, CHUNKS)

                def residual(c):
                    dve.wait_ge(back_done, c.n + 1)
                    dve.wait_ge(x_in[c.p], c.k * 16 + 16)
                    for t in range(CT):
                        last = nc.vector.scalar_tensor_tensor(
                            out=nm.X[c.p][:, t, :], in0=psO[c.p][:, t * D:(t + 1) * D],
                            scalar=inv[:, bass.ds(c.n * CT + t, 1)], in1=nm.X[c.p][:, t, :], op0=ALU.mult, op1=ALU.add)
                    last.then_inc(x_done, 1)
                    dve.wait_ge(x_done, c.n + 1)
                    nm.statistics(dve, c)

                def scaled(c):
                    dve.wait_ge(mm_done, c.n + 3)
                    wait_stored(dve, ph, o_stored, c)
                    col = bass.ds(c.n * CN, CN)
                    nc.vector.tensor_tensor(acc3[:, col], psO[c.p][0:H3, 512:512 + CN], deg[0:H3, col], ALU.mult)
                    nc.vector.tensor_tensor(O[c.p][:, :, :], psO[c.p][:, 0:CT * H3].rearrange("p (t n) -> p t n", n=H3),
                                            dinv_c[:, bass.ds(c.n * CT, CT)].unsqueeze(2).to_broadcast([P, CT, H3]),
                                            ALU.mult).then_inc(o_done, 1)

                def step(at):
                    if at(2):
                        scaled(at(2))
                    if at(0):
                        residual(at(0))
                        nm.normalize(dve, at(0))

                staggered(dve, step, 2)

            @block.tensor
            def _(pe):
                pe.wait_ge(w_in, 16)
                pe.wait_ge(cols_in, 1)
                for c in range(CHUNKS):
                    if c >= 2:
                        pe.wait_ge(roots, c - 1)
                    for t in range(CT):
                        last = nc.tensor.transpose(psO[c % 2][0:H3, t * P:(t + 1) * P], dinv_b[:, c * CT + t, :],
                                                   sh["ident"][:, :])
                    last.then_inc(spread, 1)
                pe.wait_ge(roots, CHUNKS)

                def unstage(c):
                    pe.wait_ge(staged, c.n + 1)
                    pe.wait_ge(o_done, c.n + 1)
                    for t in range(CT):
                        for k in range(KH):
                            col = t * D + k * P
                            last = nc.tensor.transpose(psO[c.p][:, col:col + P], stage[c.p][:, k, t * P:(t + 1) * P],
                                                       sh["ident"][:, :])
                    last.then_inc(back_done, 1)

                def tables(c):
                    pe.wait_ge(nm.hT_done, c.n + 3)
                    for t in range(CT):
                        for k in range(KH):
                            nc.tensor.matmul(psO[c.p][:, t * H3:(t + 1) * H3], nm.hT[c.p][:, k, t * P:(t + 1) * P],
                                             w[:, k, :], start=(k == 0), stop=(k == KH - 1))
                    for k in range(KH):
                        last = nc.tensor.matmul(psO[c.p][0:H3, 512:512 + CN], w[:, k, :], nm.hT[c.p][:, k, :],
                                                start=(k == 0), stop=(k == KH - 1))
                    last.then_inc(mm_done, 1)

                def step(at):
                    if at(0):
                        unstage(at(0))
                    if at(1):
                        nm.transpose(pe, at(1))
                        tables(at(1))

                staggered(pe, step, 1)


FMAX = 512


def batch_norm(nc, dve, ch, acc, dinv, bias, gamma, beta, stats, mv, shift, std_in, std_out, rows):
    ch.link(nc.vector.tensor_tensor(acc[:, 0:NP], acc[:, 0:NP], dinv[0:rows, 0:NP], ALU.mult))
    ch.link(nc.vector.tensor_scalar(acc[:, 0:NP], acc[:, 0:NP], bias, None, ALU.add))
    for i, lo in enumerate(range(0, N, FMAX)):
        last = nc.vector.bn_stats(stats[:, i, :], acc[:, lo:min(lo + FMAX, N)])
    ch.link(last)
    nc.vector.bn_aggr(mv[:, :], stats[:, :, :].rearrange("p a b -> p (a b)")).then_inc(std_in, 1)
    dve.wait_ge(std_out, 1)
    ch.link(nc.vector.reciprocal(mv[:, 1:2], mv[:, 1:2]))
    ch.link(nc.vector.tensor_tensor(mv[:, 1:2], mv[:, 1:2], gamma, ALU.mult))
    ch.link(nc.vector.tensor_tensor(shift, mv[:, 0:1], mv[:, 1:2], ALU.mult))
    return nc.vector.tensor_tensor(shift, beta, shift, ALU.subtract)


def nodes_gcn(nc, dram, sh, dinv, acc3, acc4):
    with Phase(nc, "n4") as ph:
        w2 = ph.sb("w2", [H3, OC])
        par = ph.sb("par", [H3, 3])
        stats = ph.sb("stats", [H3, -(-N // FMAX), 6])
        mv, shift = ph.sb("mv", [H3, 2]), ph.sb("shift", [H3, 1])
        hid = [ph.sb(f"hid{h}", [H3, CN // 2]) for h in range(2)]
        ps = ph.ps("ps", 1024)
        HC = CN // 2
        S = ph.sem
        w_in, link, mv_done, std_done, shift_done, h_done = (S(s) for s in (
            "w_in", "link", "mv_done", "std_done", "shift_done", "h_done"))
        mm_done = S("mm_done", 2)
        o_done = S("o_done", 2)

        ph.begin()
        with nc.Block() as block:

            @block.sync
            def _(sp):
                sp.dma_start(w2[:, :], dram["gcn_w2"][:, :]).then_inc(w_in, 16)
                for j, name in enumerate(("gcn_b1", "gcn_g1", "gcn_be1")):
                    sp.dma_start(par[:, j:j + 1], dram[name].rearrange("(p a) -> p a", a=1)).then_inc(w_in, 16)

            @block.scalar
            def _(act):
                act.wait_ge(mv_done, 1)
                nc.scalar.activation(mv[:, 1:2], mv[:, 1:2], ACT.Sqrt, bias=sh["eps"][0:H3, 0:1]).then_inc(std_done, 1)
                act.wait_ge(shift_done, 1)
                with act.Fori(0, CHUNKS) as c:
                    for h in range(2):
                        act.wait_ge(mm_done, c * 2 + h + 1)
                        nc.scalar.activation(hid[h][:, :], acc3[:, bass.ds(c * CN + h * HC, HC)], ACT.Relu,
                                             bias=shift[:, 0:1], scale=mv[:, 1:2]).then_inc(h_done, 1)

            @block.vector
            def _(dve):
                ch = Chain(dve, link)
                dve.wait_ge(w_in, 64)
                batch_norm(nc, dve, ch, acc3, dinv, par[:, 0:1], par[:, 1:2], par[:, 2:3], stats, mv, shift[:, :],
                           mv_done, std_done, H3).then_inc(shift_done, 1)
                with dve.Fori(0, CHUNKS) as c:
                    for h in range(2):
                        dve.wait_ge(mm_done, c * 2 + h + 3)
                        col = bass.ds(c * CN + h * HC, HC)
                        nc.vector.tensor_tensor(acc4[:, col], ps[0:OC, h * 512:h * 512 + HC], dinv[0:OC, col],
                                                ALU.mult).then_inc(o_done, 1)

            @block.tensor
            def _(pe):
                pe.wait_ge(w_in, 64)
                with pe.Fori(0, CHUNKS) as c:
                    for h in range(2):
                        hold(pe, ph, h_done, c * 2 + h + 1)
                        hold(pe, ph, o_done, c * 2 + h + 1)
                        nc.tensor.matmul(ps[0:OC, h * 512:h * 512 + HC], w2[:, :], hid[h][:, :],
                                         start=True, stop=True).then_inc(mm_done, 1)


def edges_pairs(nc, sh, acc4):
    W = NT * OC
    with Phase(nc, "l4") as ph:
        tab = ph.sb("tab", [P, W])
        pick = ph.sb("pick", [W, OC])
        acc = ph.sb("acc", [W, NW])
        part = ph.sb("part", [P, TILES], I32)
        lo, hi = ph.sb("lo", [P, TILES]), ph.sb("hi", [P, TILES])
        lo_g = [ph.sb(f"lo_g{i}", [P, GT]) for i in range(2)]
        hot = [ph.sb(f"hot{i}", [P, GT, P]) for i in range(2)]
        hot_t = [ph.sb(f"hot_t{i}", [P, GT, P]) for i in range(2)]
        own = [ph.sb(f"own{i}", [P, GT, W]) for i in range(2)]
        sel = [ph.sb(f"sel{i}", [P, GT, P]) for i in range(NB)]
        pst = ph.ps("pst", 2 * GT * P)
        psg = ph.ps("psg", 2 * 512)
        psa = ph.ps("psa", 2 * GT * P)
        pss = ph.ps("pss", 2 * 512)
        S = ph.sem
        link, tab_mm, setup = S("link"), S("tab_mm"), S("setup")
        lo_done, hot_done = S("lo_done"), S("hot_done")
        st_ps = S("st_ps", 2)
        st_done = S("st_done", 2)
        looked = S("looked", 2)
        own_done = S("own_done", 2)
        sel_done = S("sel_done")
        win_done = S("win_done", NB)
        added = S("added", 2 * GT)
        sum_done, sum_read = S("sum_done"), S("sum_read", 2)

        ph.begin()
        with nc.Block() as block:

            @block.gpsimd
            def _(pool):
                hold(pool, ph, setup, 1)
                with pool.Fori(0, ITERS) as it:
                    for b in range(NB):
                        g = it * NB + b
                        hold(pool, ph, st_ps, g + 1)
                        nc.gpsimd.tensor_copy(lo_g[b % 2][:, :], lo[:, bass.ds(g * GT, GT)]).then_inc(lo_done, 1)
                        hold(pool, ph, lo_done, g + 1)
                        for t in range(GT):
                            last = nc.gpsimd.tensor_scalar(hot[b % 2][:, t, :], sh["iota"][:, :], lo_g[b % 2][:, t:t + 1],
                                                           None, ALU.is_equal)
                        last.then_inc(hot_done, 1)

            @block.scalar
            def _(act):
                with act.Fori(0, ITERS) as it:
                    for b in range(NB):
                        g = it * NB + b
                        act.wait_ge(st_ps, g + 3)
                        act.wait_ge(looked, g + 1)
                        nc.scalar.activation(hot_t[b % 2][:, :, :].rearrange("p t e -> p (t e)"),
                                             pst[:, (b % 2) * GT * P:(b % 2 + 1) * GT * P], ACT.Copy).then_inc(st_done, 1)

            @block.vector
            def _(dve):
                bases_of = WindowBases(dve, sh, "l4", 3)
                ch = Chain(dve, link)
                ch.link(nc.vector.tensor_scalar(part[:, :], sh["src_sb"][:, :], P - 1, None, ALU.bitwise_and))
                ch.link(nc.vector.tensor_copy(lo[:, :], part[:, :]))
                ch.link(nc.vector.tensor_tensor(hi[:, :], sh["src_sb"][:, :], part[:, :], ALU.subtract))
                nc.vector.tensor_scalar(hi[:, :], hi[:, :], 1.0 / P, None, ALU.mult).then_inc(setup, 1)
                nc.vector.memset(acc[:, :], 0.0)
                nc.vector.tensor_reduce(pick[:, :], sh["ident"][0:W, 0:W].rearrange("p (h c) -> p c h", c=OC),
                                        mybir.AxisListType.X, ALU.add)
                dve.wait_ge(tab_mm, 1)
                nc.vector.tensor_copy(tab[:, :], pss[:, 0:W]).then_inc(setup, 1)
                dve.wait_ge(setup, 2)

                def select(it, b):
                    g = it * NB + b
                    dve.wait_ge(win_done, g + 1)
                    select_group(nc, sel[b], sh, g).then_inc(sel_done, 1)

                def mask(it, b, t):
                    g = it * NB + b
                    if t == 0:
                        dve.wait_ge(looked, g + 3)
                        dve.wait_ge(win_done, g + 3)
                    col = (b % 2) * 512 + t * W
                    ins = nc.vector.scalar_tensor_tensor(
                        out=own[b % 2][:, t, :].rearrange("p (h c) -> p h c", c=OC),
                        in0=sh["iota"][:, 0:NT].unsqueeze(2).to_broadcast([P, NT, OC]),
                        scalar=hi[:, bass.ds(g * GT + t, 1)],
                        in1=psg[:, col:col + W].rearrange("p (h c) -> p h c", c=OC),
                        op0=ALU.is_equal, op1=ALU.mult)
                    if t == GT - 1:
                        ins.then_inc(own_done, 1)

                def add(it, b, bases, t):
                    g = it * NB + b
                    if t == 0:
                        dve.wait_ge(win_done, g + NB + 1)
                    dve.wait_ge(added, GT * g + t + 2 * GT)
                    a = acc[:, bass.ds(bases[t], P)]
                    col = ((b % 2) * GT + t) * P
                    nc.vector.tensor_tensor(a, a, psa[0:W, col:col + P], ALU.add).then_inc(added, 1)

                def step(it, b, first):
                    m, a = (None if first and b < k else back(it, b, k) for k in (1, 3))
                    select(it, b)
                    bases = bases_of.step(it, b, first)
                    for t in range(GT):
                        if m:
                            mask(*m, t)
                        if a:
                            add(*a, bases, t)

                def tail(it):
                    for t in range(GT):
                        mask(it, NB - 1, t)
                    for b in range(1, NB):
                        bases = bases_of.group(it * NB + b)
                        for t in range(GT):
                            add(it, b, bases, t)

                skewed(dve, step, tail)
                with dve.Fori(0, CHUNKS // 2) as i:
                    for q in range(2):
                        c = i * 2 + q
                        dve.wait_ge(sum_done, c + 1)
                        a = acc4[:, bass.ds(c * CN, CN)]
                        nc.vector.tensor_tensor(a, a, pss[0:OC, q * 512:q * 512 + CN], ALU.add).then_inc(sum_read, 1)
                dve.wait_ge(sum_done, CHUNKS)
                a = acc4[:, (CHUNKS - 1) * CN:NP]
                nc.vector.tensor_tensor(a, a, pss[0:OC, 0:CN], ALU.add).then_inc(sum_read, 1)

            @block.tensor
            def _(pe):
                for h in range(NT):
                    last = nc.tensor.transpose(pss[:, h * OC:(h + 1) * OC], acc4[:, h * P:(h + 1) * P],
                                               sh["ident"][0:OC, 0:OC])
                last.then_inc(tab_mm, 1)
                pe.wait_ge(setup, 2)

                def transpose(it, b):
                    g = it * NB + b
                    pe.wait_ge(hot_done, g + 1)
                    pe.wait_ge(st_done, g + 1)
                    for t in range(GT):
                        col = ((b % 2) * GT + t) * P
                        last = nc.tensor.transpose(pst[:, col:col + P], hot[b % 2][:, t, :], sh["ident"][:, :])
                    last.then_inc(st_ps, 1)

                def look_up(it, b):
                    g = it * NB + b
                    pe.wait_ge(st_done, g + 3)
                    pe.wait_ge(own_done, g + 1)
                    for t in range(GT):
                        col = (b % 2) * 512 + t * W
                        last = nc.tensor.matmul(psg[:, col:col + W], hot_t[b % 2][:, t, :], tab[:, :], start=True, stop=True)
                    last.then_inc(looked, 1)

                def windows(it, b):
                    g = it * NB + b
                    pe.wait_ge(own_done, g + 3)
                    pe.wait_ge(sel_done, g + 1)
                    pe.wait_ge(added, GT * (g + 1))
                    for t in range(GT):
                        col = ((b % 2) * GT + t) * P
                        last = nc.tensor.matmul(psa[0:W, col:col + P], own[b % 2][:, t, :], sel[b][:, t, :],
                                                start=True, stop=True)
                    last.then_inc(win_done, 1)

                def step(it, b, first):
                    if not first or b >= 1:
                        look_up(*back(it, b, 1))
                    transpose(it, b)
                    if not first or b >= 2:
                        windows(*back(it, b, 2))

                def tail(it):
                    look_up(it, NB - 1)
                    windows(it, NB - 2)
                    windows(it, NB - 1)

                skewed(pe, step, tail)
                pe.wait_ge(added, GT * GROUPS + 2 * GT)
                for c in range(CHUNKS):
                    pe.wait_ge(sum_read, c + 1)
                    nc.tensor.matmul(pss[0:OC, (c % 2) * 512:(c % 2) * 512 + CN], pick[:, :], acc[:, c * CN:(c + 1) * CN],
                                     start=True, stop=True).then_inc(sum_done, 1)


def nodes_out(nc, dram, sh, dinv, acc4):
    with Phase(nc, "n5") as ph:
        wd = ph.sb("wd", [OC, D])
        par = ph.sb("par", [OC, 3])
        bd = ph.sb("bd", [P, D])
        stats = ph.sb("stats", [OC, -(-N // FMAX), 6])
        mv, shift = ph.sb("mv", [OC, 2]), ph.sb("shift", [OC, 1])
        z = pair_of(ph, "z", [OC, CN])
        X, O = (pair_of(ph, n, [P, CT, D]) for n in ("X", "O"))
        ps = psum_pair(ph, "ps")
        S = ph.sem
        w_in, link, mv_done, std_done, shift_done, z_done = (S(s) for s in (
            "w_in", "link", "mv_done", "std_done", "shift_done", "z_done"))
        x_in = [S(f"x_in{p}") for p in range(2)]
        stored = [S(f"stored{p}") for p in range(2)]
        biased = S("biased")
        mm_done = S("mm_done", 2)
        o_done = S("o_done", 2)

        ph.begin()
        with nc.Block() as block:

            @block.sync
            def _(sp):
                sp.dma_start(wd[:, :], dram["gcn_wd"][:, :]).then_inc(w_in, 16)
                sp.dma_start(bd[:, :], on_all(dram["gcn_bd"], D)).then_inc(w_in, 16)
                for j, name in enumerate(("gcn_b2", "gcn_g2", "gcn_be2")):
                    sp.dma_start(par[:, j:j + 1], dram[name].rearrange("(p a) -> p a", a=1)).then_inc(w_in, 16)

                def step(at):
                    c = at(0)
                    hold(sp, ph, o_done, c.n + 1)
                    sp.dma_start(X[c.p][:, :, :], node_rows(dram["x3"], c.n)).then_inc(x_in[c.p], 16)

                staggered(sp, step, 0)

            @block.gpsimd
            def _(pool):
                staggered(pool, lambda at: store_out(nc, pool, ph, O, dram["out"], at(0), o_done, stored), 0)
                all_stored(pool, stored)

            @block.scalar
            def _(act):
                act.wait_ge(mv_done, 1)
                nc.scalar.activation(mv[:, 1:2], mv[:, 1:2], ACT.Sqrt, bias=sh["eps"][0:OC, 0:1]).then_inc(std_done, 1)
                act.wait_ge(shift_done, 1)

                def step(at):
                    c = at(0)
                    act.wait_ge(mm_done, c.n + 1)
                    nc.scalar.activation(z[c.p][:, :], acc4[:, bass.ds(c.n * CN, CN)], ACT.Identity,
                                         bias=shift[:, 0:1], scale=mv[:, 1:2]).then_inc(z_done, 1)

                staggered(act, step, 0)

            @block.vector
            def _(dve):
                ch = Chain(dve, link)
                dve.wait_ge(w_in, 80)
                batch_norm(nc, dve, ch, acc4, dinv, par[:, 0:1], par[:, 1:2], par[:, 2:3], stats, mv, shift[:, :],
                           mv_done, std_done, OC).then_inc(shift_done, 1)

                def step(at):
                    if at(0):
                        c = at(0)
                        dve.wait_ge(x_in[c.p], c.k * 16 + 16)
                        nc.vector.tensor_tensor(X[c.p][:, :, :], X[c.p][:, :, :],
                                                bd[:, :].unsqueeze(1).to_broadcast([P, CT, D]), ALU.add).then_inc(biased, 1)
                    if at(1):
                        c = at(1)
                        dve.wait_ge(biased, c.n + 1)
                        dve.wait_ge(mm_done, c.n + 3)
                        wait_stored(dve, ph, stored, c)
                        xf, of = (a[c.p][:, :, :].rearrange("p t n -> p (t n)") for a in (X, O))
                        for lo, hi in BANKS:
                            last = nc.vector.tensor_tensor(of[:, lo:hi], xf[:, lo:hi], ps[c.p][:, lo:hi], ALU.add)
                        last.then_inc(o_done, 1)

                staggered(dve, step, 1)

            @block.tensor
            def _(pe):
                pe.wait_ge(w_in, 80)

                def step(at):
                    c = at(0)
                    pe.wait_ge(z_done, c.n + 1)
                    pe.wait_ge(o_done, c.n + 1)
                    for t in range(CT):
                        last = nc.tensor.matmul(ps[c.p][:, t * D:(t + 1) * D], z[c.p][:, t * P:(t + 1) * P], wd[:, :],
                                                start=True, stop=True)
                    last.then_inc(mm_done, 1)

                staggered(pe, step, 0)


def bass_gnn_stack(nc, dram):
    with ExitStack() as ctx:
        def keep(name, shape, dtype=F32):
            return ctx.enter_context(nc.sbuf_tensor(name, shape, dtype))

        sh = {"ident": keep("ident", [P, P]), "iota": keep("iota", [P, P]), "ones": keep("ones", [P, P]),
              "eps": keep("eps", [P, 1]), "src_sb": keep("src_sb", [P, TILES], I32),
              "dst_sb": keep("dst_sb", [P, TILES], I32), "rel": keep("rel", [P, TILES])}
        constants(nc, dram, sh)
        embed0(nc, dram, sh)
        with nc.sbuf_tensor("acc0", [P, KH, NW], F32) as acc:
            edges_schnet(nc, dram, sh, acc)
            nodes_schnet(nc, dram, sh, acc)
        with nc.sbuf_tensor("a_src", [P, TILES * HEADS], F32) as a_src, \
                nc.sbuf_tensor("seg_max", [P, TILES * HEADS], F32) as seg_max:
            edges_max(nc, dram, sh, a_src, seg_max)
            with nc.sbuf_tensor("acc1", [P, KH, NW], F32) as acc, nc.sbuf_tensor("acc_d", [2 * HEADS, NW], F32) as acc_d:
                edges_gat(nc, dram, sh, a_src, seg_max, acc, acc_d)
                nodes_gat(nc, dram, sh, acc, acc_d)
        with nc.sbuf_tensor("deg", [P, NW], F32) as deg, nc.sbuf_tensor("acc3", [H3, NW], F32) as acc3:
            with nc.sbuf_tensor("acc2", [P, KH, NW], F32) as acc:
                edges_rows(nc, dram, sh, "l2", dram["tab2"], D, acc, deg)
                nodes_mean(nc, dram, sh, acc, deg, acc3)
            edges_rows(nc, dram, sh, "l3", dram["tab3"], H3, acc3)
            with nc.sbuf_tensor("acc4", [OC, NW], F32) as acc4:
                nodes_gcn(nc, dram, sh, deg, acc3, acc4)
                edges_pairs(nc, sh, acc4)
                nodes_out(nc, dram, sh, deg, acc4)


def layout(i):
    import numpy as np

    def padded(a, rows, value=0):
        out = np.full((rows, *a.shape[1:]), value, a.dtype)
        out[:a.shape[0]] = a
        return out

    def cols(a):
        return np.ascontiguousarray(a.reshape(TILES, P).T)

    a = {k: np.asarray(v) for k, v in i.items()}
    src = padded(a["src"], TILES * P)
    dst = padded(a["dst"], TILES * P, PAD_DST)
    flat = np.concatenate([np.full(1, -1, dst.dtype), dst, np.full(1, -1, dst.dtype)])
    edge = padded(a["edge_attr_64"], TILES * P).reshape(GROUPS // 2, 2, GT * P, NG).transpose(0, 1, 3, 2)
    d = {
        "x": padded(a["x"], NP), "src_cols": cols(src), "dst_cols": cols(dst), "prev_cols": cols(flat[:-2]), "next_cols": cols(flat[2:]),
        "ew_cols": cols(padded(a["edge_weight"], TILES * P)),
        "edge_t": edge.reshape(GROUPS // 2, P, GT * P),
        "fw1_t": a["L0_gnn_fw1"].T, "fb1": a["L0_gnn_fb1"].reshape(KH, P).T, "fw2_t": a["L0_gnn_fw2"].T, "fb2": a["L0_gnn_fb2"],
        "w1_t": a["L0_gnn_w1"].T, "w2_t": a["L0_gnn_w2"].T, "b2": a["L0_gnn_b2"].reshape(KH, P).T,
        "w3_t": a["L0_gnn_w3"].T, "b3": a["L0_gnn_b3"],
        "gat_w": a["L1_gnn_W0"], "gat_w_t": a["L1_gnn_W0"].T, "att_src": a["L1_gnn_att_src0"].reshape(D),
        "att_dst": a["L1_gnn_att_dst0"].reshape(D), "gat_b": a["L1_gnn_b0"],
        "mean_w": a["L2_gnn_W"], "mean_b": a["L2_gnn_b"],
        "gcn_w1": a["L3_gnn_W1"], "gcn_b1": a["L3_gnn_b1"], "gcn_g1": a["L3_gnn_g1"], "gcn_be1": a["L3_gnn_be1"],
        "gcn_w2": a["L3_gnn_W2"], "gcn_b2": a["L3_gnn_b2"], "gcn_g2": a["L3_gnn_g2"], "gcn_be2": a["L3_gnn_be2"],
        "gcn_wd": a["L3_gnn_Wd"], "gcn_bd": a["L3_gnn_bd"],
    }
    return {k: np.ascontiguousarray(v) for k, v in d.items()}


def kernel(**inputs):
    import concourse.bacc as bacc
    from concourse.bass_utils import run_bass_kernel_spmd

    nc = bacc.Bacc("TRN2", target_bir_lowering=False, num_devices=1)
    arrays = layout(inputs)
    dram = {}
    for name, (shape, dtype) in INPUTS.items():
        dram[name] = nc.dram_tensor(f"in_{name}", shape, dtype, kind="ExternalInput").ap()
    for name, shape in SCRATCH.items():
        dram[name] = nc.dram_tensor(f"tmp_{name}", shape, F32).ap()
    dram["out"] = nc.dram_tensor("out", [NP, D], F32, kind="ExternalOutput").ap()
    bass_gnn_stack(nc, dram)
    r = run_bass_kernel_spmd(nc, [{f"in_{k}": v for k, v in arrays.items()}], core_ids=[0])
    return r.results[0]["out"][:N]
```
